# Optimizing a Trainium2 kernel written in Bass

```python
import numpy as np
import jax
import jax.numpy as jnp

def _softmax(x, axis=-1):
    return jax.nn.softmax(x, axis=axis)

def _gelu(x):
    return jax.nn.gelu(x, approximate=True)

def _silu(x):
    return jax.nn.silu(x)

def _sigmoid(x):
    return jax.nn.sigmoid(x)

def _layernorm(x, axis=-1, eps=1e-05):
    m = jnp.mean(x, axis=axis, keepdims=True)
    v = jnp.var(x, axis=axis, keepdims=True)
    return (x - m) / jnp.sqrt(v + eps)

def _scatter_add(tgt, idx, src, axis=0):
    return tgt.at[idx].add(src)

def _segment_sum(src, seg, n):
    return jax.ops.segment_sum(src, seg, n)
kernel_name = 'mk_adaln_attn_ffn_d1_seqx_r8_0bcb0f'

def setup_inputs(seed: int=0):
    np.random.seed(seed)
    _w = jnp.asarray

    def _rec_inputs():
        import jax
        import jax.numpy as jnp
        _rk = jax.random.key(seed)
        x = -0.000125 + 0.9999 * jax.random.normal(jax.random.fold_in(_rk, 1), (32, 32, 512), jnp.float32)
        _lenS = 32 - jax.random.randint(jax.random.fold_in(_rk, 7), (32,), 0, max(1, 32 // 4) + 1, jnp.int32)
        _lenS2 = 32 - jax.random.randint(jax.random.fold_in(_rk, 8), (32,), 0, max(1, 32 // 4) + 1, jnp.int32)
        cond_128 = 0.0061147 + 1.02565 * jax.random.normal(jax.random.fold_in(_rk, 11), (32, 128), jnp.float32)
        fside_S_0 = -0.022604 + 0.987366 * jax.random.normal(jax.random.fold_in(_rk, 12), (32,), jnp.float32)
        return (x, cond_128, fside_S_0)
    x, cond_128, fside_S_0 = _rec_inputs()

    def _L0_cond_setup():
        import jax, jax.numpy as jnp
        import numpy as np
        from jax import lax
        N, C_IN, L = (32, 32, 512)
        C_OUT, K, GROUPS = (32, 9, 4)
        C_DIM, PAD, STRIDE = (128, 4, 1)
        key = jax.random.key(seed)
        k1, k2, k3, k4, k5 = jax.random.split(key, 5)
        x = jax.random.normal(k1, (N, C_IN, L), dtype=jnp.float32)
        c = jax.random.normal(k2, (N, C_DIM), dtype=jnp.float32)
        weight = jax.random.normal(k3, (C_OUT, C_IN // GROUPS, K), dtype=jnp.float32)
        c_weight = jax.random.normal(k4, (C_OUT, C_DIM), dtype=jnp.float32)
        bias = jax.random.normal(k5, (C_OUT,), dtype=jnp.float32)
        return {'x': x, 'c': c, 'weight': weight, 'c_weight': c_weight, 'bias': bias}
    _L0_cond_all = _L0_cond_setup()
    _L0_cond_in = {k: v for k, v in _L0_cond_all.items() if k in ('weight', 'c_weight')}
    del _L0_cond_all

    def _L0_attn_setup():
        import jax, jax.numpy as jnp
        import numpy as np
        import math
        B, S, DM = (1, 256, 512)
        H, HKV, HD = (32, 8, 128)
        EPS = 1e-06
        NEG_INF = -1e+30

        def _alibi_slopes(n_heads: int) -> np.ndarray:
            start = 2 ** (-2 ** (-(math.log2(n_heads) - 3)))
            return np.array([start * start ** i for i in range(n_heads)], dtype=np.float32)

        def _rmsnorm(t, w):
            tf = t.astype(jnp.float32)
            inv = jax.lax.rsqrt(jnp.mean(tf * tf, axis=-1, keepdims=True) + EPS)
            return (tf * inv * w).astype(t.dtype)
        key = jax.random.key(seed)
        ks = jax.random.split(key, 5)
        std = 0.02
        return {'x': jax.random.normal(ks[0], (B, S, DM), dtype=jnp.float32), 'Wq': jax.random.normal(ks[1], (H * HD, DM), dtype=jnp.float32) * std, 'Wk': jax.random.normal(ks[2], (HKV * HD, DM), dtype=jnp.float32) * std, 'Wv': jax.random.normal(ks[3], (HKV * HD, DM), dtype=jnp.float32) * std, 'Wo': jax.random.normal(ks[4], (H * HD, DM), dtype=jnp.float32).T * (std / math.sqrt(2 * 32)), 'q_norm_w': jnp.ones((HD,), dtype=jnp.float32), 'k_norm_w': jnp.ones((HD,), dtype=jnp.float32)}
    _L0_attn_all = _L0_attn_setup()
    _L0_attn_in = {k: v for k, v in _L0_attn_all.items() if k in ('Wq', 'Wk', 'Wv', 'Wo', 'q_norm_w', 'k_norm_w')}
    del _L0_attn_all

    def _L0_cond2_setup():
        import jax, jax.numpy as jnp
        import numpy as np
        K = 8
        T = 1.0
        D_EMBD = 128
        IN_C = 32
        OUT_C = 32
        BS = 32
        H = 512
        HID = 128
        key = jax.random.key(seed)
        ks = jax.random.split(key, 10)
        s = lambda fan_in: 1.0 / np.sqrt(fan_in)
        return {'x': jax.random.normal(ks[0], (BS, IN_C, H), dtype=jnp.float32), 'embedding': jax.random.normal(ks[1], (BS, D_EMBD), dtype=jnp.float32), 'W0': jax.random.normal(ks[2], (D_EMBD, HID), dtype=jnp.float32) * s(D_EMBD), 'b0': jnp.zeros((HID,), dtype=jnp.float32), 'W1': jax.random.normal(ks[3], (HID, HID), dtype=jnp.float32) * s(HID), 'b1': jnp.zeros((HID,), dtype=jnp.float32), 'W2': jax.random.normal(ks[4], (HID, K), dtype=jnp.float32) * s(HID), 'b2': jnp.zeros((K,), dtype=jnp.float32), 'weight': jax.random.normal(ks[5], (K, OUT_C, IN_C, 1), dtype=jnp.float32) * s(IN_C), 'bias_k': jax.random.normal(ks[6], (K, OUT_C), dtype=jnp.float32) * 0.1}
    _L0_cond2_all = _L0_cond2_setup()
    _L0_cond2_in = {k: v for k, v in _L0_cond2_all.items() if k in ('W0', 'b0', 'W1', 'b1', 'W2', 'b2', 'weight', 'bias_k')}
    del _L0_cond2_all

    def _L0_ffn_setup():
        import jax, jax.numpy as jnp
        import numpy as np
        GROUP_SIZE = 128

        def dequantize(imatrix, scales, zeros, group_size, out_dtype):
            rs = jnp.repeat(scales, group_size, axis=0)
            rz = jnp.repeat(zeros, group_size, axis=0)
            return ((imatrix.astype(rs.dtype) - rz.astype(rs.dtype)) * rs).astype(out_dtype)
        key = jax.random.key(seed)
        ks = jax.random.split(key, 10)
        H, I, G = (512, 1792, GROUP_SIZE)
        B, S = (4, 256)
        x = jax.random.normal(ks[0], (B, S, H), dtype=jnp.float32)
        gate_w = jax.random.randint(ks[1], (H, I), 0, 16, dtype=jnp.int32)
        gate_z = jax.random.randint(ks[2], (H // G, I), 0, 16, dtype=jnp.int32)
        gate_s = jax.random.uniform(ks[3], (H // G, I), dtype=jnp.float32) * 0.01
        up_w = jax.random.randint(ks[4], (H, I), 0, 16, dtype=jnp.int32)
        up_z = jax.random.randint(ks[5], (H // G, I), 0, 16, dtype=jnp.int32)
        up_s = jax.random.uniform(ks[6], (H // G, I), dtype=jnp.float32) * 0.01
        down_w = jax.random.randint(ks[7], (I, H), 0, 16, dtype=jnp.int32)
        down_z = jax.random.randint(ks[8], (I // G, H), 0, 16, dtype=jnp.int32)
        down_s = jax.random.uniform(ks[9], (I // G, H), dtype=jnp.float32) * 0.01
        return {'x': x, 'gate_w': gate_w, 'gate_z': gate_z, 'gate_s': gate_s, 'up_w': up_w, 'up_z': up_z, 'up_s': up_s, 'down_w': down_w, 'down_z': down_z, 'down_s': down_s}
    _L0_ffn_all = _L0_ffn_setup()
    _L0_ffn_in = {k: v for k, v in _L0_ffn_all.items() if k in ('gate_w', 'gate_z', 'gate_s', 'up_w', 'up_z', 'up_s', 'down_w', 'down_z', 'down_s')}
    del _L0_ffn_all
    return {'x': x, 'cond_128': cond_128, 'fside_S_0': fside_S_0, 'L0_cond_weight': _L0_cond_in['weight'], 'L0_cond_c_weight': _L0_cond_in['c_weight'], 'L0_attn_Wq': _L0_attn_in['Wq'], 'L0_attn_Wk': _L0_attn_in['Wk'], 'L0_attn_Wv': _L0_attn_in['Wv'], 'L0_attn_Wo': _L0_attn_in['Wo'], 'L0_attn_q_norm_w': _L0_attn_in['q_norm_w'], 'L0_attn_k_norm_w': _L0_attn_in['k_norm_w'], 'L0_cond2_W0': _L0_cond2_in['W0'], 'L0_cond2_b0': _L0_cond2_in['b0'], 'L0_cond2_W1': _L0_cond2_in['W1'], 'L0_cond2_b1': _L0_cond2_in['b1'], 'L0_cond2_W2': _L0_cond2_in['W2'], 'L0_cond2_b2': _L0_cond2_in['b2'], 'L0_cond2_weight': _L0_cond2_in['weight'], 'L0_cond2_bias_k': _L0_cond2_in['bias_k'], 'L0_ffn_gate_w': _L0_ffn_in['gate_w'], 'L0_ffn_gate_z': _L0_ffn_in['gate_z'], 'L0_ffn_gate_s': _L0_ffn_in['gate_s'], 'L0_ffn_up_w': _L0_ffn_in['up_w'], 'L0_ffn_up_z': _L0_ffn_in['up_z'], 'L0_ffn_up_s': _L0_ffn_in['up_s'], 'L0_ffn_down_w': _L0_ffn_in['down_w'], 'L0_ffn_down_z': _L0_ffn_in['down_z'], 'L0_ffn_down_s': _L0_ffn_in['down_s']}

def reference(x, cond_128, fside_S_0, L0_cond_weight, L0_cond_c_weight, L0_attn_Wq, L0_attn_Wk, L0_attn_Wv, L0_attn_Wo, L0_attn_q_norm_w, L0_attn_k_norm_w, L0_cond2_W0, L0_cond2_b0, L0_cond2_W1, L0_cond2_b1, L0_cond2_W2, L0_cond2_b2, L0_cond2_weight, L0_cond2_bias_k, L0_ffn_gate_w, L0_ffn_gate_z, L0_ffn_gate_s, L0_ffn_up_w, L0_ffn_up_z, L0_ffn_up_s, L0_ffn_down_w, L0_ffn_down_z, L0_ffn_down_s):
    import jax
    import jax.numpy as jnp

    def _L0_cond_ref(x, c, weight, c_weight, bias):
        import jax, jax.numpy as jnp
        import numpy as np
        from jax import lax
        N, C_IN, L = (32, 32, 512)
        C_OUT, K, GROUPS = (32, 9, 4)
        C_DIM, PAD, STRIDE = (128, 4, 1)
        out = lax.conv_general_dilated(x, weight, window_strides=(STRIDE,), padding=[(PAD, PAD)], dimension_numbers=('NCH', 'OIH', 'NCH'), feature_group_count=GROUPS)
        ctx = jnp.einsum('nd,od->no', c, c_weight)
        out = out + ctx[:, :, None] + bias[None, :, None]
        return out

    def _L0_attn_ref(x, Wq, Wk, Wv, Wo, q_norm_w, k_norm_w):
        import jax, jax.numpy as jnp
        import numpy as np
        import math
        B, S, DM = (1, 256, 512)
        H, HKV, HD = (32, 8, 128)
        EPS = 1e-06
        NEG_INF = -1e+30

        def _alibi_slopes(n_heads: int) -> np.ndarray:
            start = 2 ** (-2 ** (-(math.log2(n_heads) - 3)))
            return np.array([start * start ** i for i in range(n_heads)], dtype=np.float32)

        def _rmsnorm(t, w):
            tf = t.astype(jnp.float32)
            inv = jax.lax.rsqrt(jnp.mean(tf * tf, axis=-1, keepdims=True) + EPS)
            return (tf * inv * w).astype(t.dtype)
        b, s, _ = x.shape
        G = H // HKV
        q = (x @ Wq.T).reshape(b, s, H, HD).transpose(0, 2, 1, 3)
        k = (x @ Wk.T).reshape(b, s, HKV, HD).transpose(0, 2, 1, 3)
        v = (x @ Wv.T).reshape(b, s, HKV, HD).transpose(0, 2, 1, 3)
        q = _rmsnorm(q, q_norm_w)
        k = _rmsnorm(k, k_norm_w)
        qg = q.reshape(b, HKV, G, s, HD)
        scores = jnp.einsum('bkgqd,bksd->bkgqs', qg, k) / math.sqrt(HD)
        slopes = jnp.asarray(_alibi_slopes(H)).reshape(HKV, G)
        pos = jnp.arange(s, dtype=jnp.float32)
        rel = pos[None, :] - pos[:, None]
        bias = jnp.where(rel > 0, NEG_INF, slopes[:, :, None, None] * rel)
        attn = jax.nn.softmax(scores + bias[None], axis=-1)
        out = jnp.einsum('bkgqs,bksd->bkgqd', attn, v)
        out = out.reshape(b, H, s, HD).transpose(0, 2, 1, 3).reshape(b, s, H * HD)
        return out @ Wo.T

    def _L0_cond2_ref(x, embedding, W0, b0, W1, b1, W2, b2, weight, bias_k):
        import jax, jax.numpy as jnp
        import numpy as np
        K = 8
        T = 1.0
        D_EMBD = 128
        IN_C = 32
        OUT_C = 32
        BS = 32
        H = 512
        HID = 128
        h = jax.nn.gelu(embedding @ W0 + b0, approximate=False)
        h = jax.nn.gelu(h @ W1 + b1, approximate=False)
        att = jax.nn.softmax((h @ W2 + b2) / T, axis=-1)
        agg_w = jnp.einsum('bk,koi->boi', att, weight[..., 0])
        agg_b = att @ bias_k
        out = jnp.einsum('boi,bih->boh', agg_w, x) + agg_b[:, :, None]
        return out

    def _L0_ffn_ref(x, gate_w, gate_z, gate_s, up_w, up_z, up_s, down_w, down_z, down_s):
        import jax, jax.numpy as jnp
        import numpy as np
        GROUP_SIZE = 128

        def dequantize(imatrix, scales, zeros, group_size, out_dtype):
            rs = jnp.repeat(scales, group_size, axis=0)
            rz = jnp.repeat(zeros, group_size, axis=0)
            return ((imatrix.astype(rs.dtype) - rz.astype(rs.dtype)) * rs).astype(out_dtype)
        dt = x.dtype
        gate_proj = dequantize(gate_w, gate_s, gate_z, GROUP_SIZE, dt)
        up_proj = dequantize(up_w, up_s, up_z, GROUP_SIZE, dt)
        down_proj = dequantize(down_w, down_s, down_z, GROUP_SIZE, dt)
        gate = jax.nn.silu(jnp.dot(x, gate_proj))
        up = jnp.dot(x, up_proj)
        return jnp.dot(gate * up, down_proj)
    x = x + _L0_attn_ref(_L0_cond_ref(x, cond_128, L0_cond_weight, L0_cond_c_weight, fside_S_0), L0_attn_Wq, L0_attn_Wk, L0_attn_Wv, L0_attn_Wo, L0_attn_q_norm_w, L0_attn_k_norm_w)
    x = x + _L0_ffn_ref(_L0_cond2_ref(x, cond_128, L0_cond2_W0, L0_cond2_b0, L0_cond2_W1, L0_cond2_b1, L0_cond2_W2, L0_cond2_b2, L0_cond2_weight, L0_cond2_bias_k), L0_ffn_gate_w, L0_ffn_gate_z, L0_ffn_gate_s, L0_ffn_up_w, L0_ffn_up_z, L0_ffn_up_s, L0_ffn_down_w, L0_ffn_down_z, L0_ffn_down_s)
    return x

_drawn_inputs = setup_inputs


def setup_inputs(seed=0):
    import zlib

    import numpy as np

    out = dict(_drawn_inputs(seed))
    spreads = {'L0_attn_q_norm_w': (1.0, 0.2),
     'L0_attn_k_norm_w': (1.0, 0.2),
     'L0_cond2_b0': (0.0, 0.8),
     'L0_cond2_b1': (0.0, 0.679),
     'L0_cond2_b2': (0.0, 0.287)}
    factors = {}
    for name, (base, spread) in spreads.items():
        noise = np.random.default_rng([zlib.crc32(name.encode()), seed]).standard_normal(out[name].shape)
        drawn = base * np.exp(spread * noise) if base else spread * noise
        out[name] = jnp.asarray(drawn.astype(out[name].dtype))
    for name, factor in factors.items():
        out[name] = (out[name] * factor).astype(out[name].dtype)
    return out
```

```python
from contextlib import ExitStack

import numpy as np

import concourse.bass as bass
from concourse import mybir

P = 128
B, S, DM = 32, 32, 512
H, HKV, HD = 32, 8, 128
G = H // HKV
KC = DM // P
BQ = P // S
NQ = B // BQ
HQ = NQ // 2
HB = B // 2
HT = HB * S
TAPS = 9
PAD = TAPS // 2
CG = 8
NGRP = P // CG
XW = DM + 2 * PAD
EXPERTS = 8
INNER = 1792
IC = INNER // P
UNITS = 2 * HKV
EPS = 1e-6
MASKED = -1e30

F32 = mybir.dt.float32
F32R = mybir.dt.float32r
F16 = mybir.dt.float16
I32 = mybir.dt.int32
ALU = mybir.AluOpType
ACT = mybir.ActivationFunctionType
AX_X = mybir.AxisListType.X

C_ID, C_BIAS, C_BLK, C_QUAD = 0, P, P + HKV * S, P + HKV * S + NGRP
C_ALL = C_QUAD + BQ
V_B0, V_B1, V_QW, V_KW, V_FS, V_BK = 0, 1, 2, 3, 4, 5
V_ALL = V_BK + EXPERTS


def constants():
    t = np.zeros((P, C_ALL), np.float32)
    t[:, C_ID:C_ID + P] = np.eye(P, dtype=np.float32)
    start = 2 ** (-2 ** (-(np.log2(H) - 3)))
    slopes = np.array([start * start ** i for i in range(H)], np.float32).reshape(HKV, G)
    pos = np.arange(S, dtype=np.float32)
    rel = pos[None, :] - pos[:, None]
    bias = np.where(rel > 0, np.float32(MASKED), slopes[:, :, None, None] * rel)
    t[:, C_BIAS:C_BLK] = bias.transpose(1, 2, 0, 3).reshape(P, HKV * S)
    p = np.arange(P)
    t[:, C_BLK:C_QUAD] = p[:, None] // CG == np.arange(NGRP)
    t[:, C_QUAD:C_ALL] = p[:, None] // S == np.arange(BQ)
    return t


def build(nc, x_in, cond_in, cw_in, conv_in, wq_in, wkv_in, wo_in, w0_in, w1_in, w2_in, b2_in, mix_in, vec_in,
          gu_w_in, gu_z_in, gu_s_in, dn_w_in, dn_z_in, dn_s_in, const_in, out):
    ctx = ExitStack()
    with ctx:
        def sb(name, shape, dt=F32, where=ctx):
            return where.enter_context(nc.sbuf_tensor(name, shape, dt))

        def sem(name):
            return ctx.enter_context(nc.semaphore(name))

        bank = [ctx.enter_context(nc.psum_tensor(f"bank{i}", [P, DM], F32)) for i in range(8)]
        PA, PB, PC = bank[0:2], bank[2:4], bank[4:8]

        x = sb("x", [P, NQ, DM])
        const = sb("const", [P, C_ALL])
        vec = sb("vec", [P, V_ALL])
        ones = sb("ones", [P, 1])
        aggb = sb("aggb", [P, NQ])
        mixhi = sb("mixhi", [P, NQ, BQ, S], F32R)
        mixlo = sb("mixlo", [P, NQ, BQ, S], F32R)
        ident = const[:, C_ID:C_ID + P]
        blkmask = const[:, C_BLK:C_QUAD]
        quadmask = const[:, C_QUAD:C_ALL]

        att = ExitStack()
        cThi = sb("cThi", [P, NQ, KC, P], F32R, att)
        cTlo = sb("cTlo", [P, NQ, KC, P], F32R, att)
        whwork = ExitStack()
        condT = sb("condT", [P, B], F32, whwork)
        cwT = sb("cwT", [P, S], F32, whwork)
        ctxr = sb("ctxr", [P, B, S], F32, whwork)
        ctxcol = sb("ctxcol", [P, NQ], F32, whwork)
        w0 = sb("w0", [P, P], F32, whwork)
        w1 = sb("w1", [P, P], F32, whwork)
        w2 = sb("w2", [P, EXPERTS], F32, whwork)
        b2 = sb("b2", [P, EXPERTS], F32, whwork)
        h1 = sb("h1", [P, B], F32, whwork)
        h2 = sb("h2", [P, B], F32, whwork)
        h2r = sb("h2r", [P, B, S], F32, whwork)
        lg = sb("lg", [P, NQ, EXPERTS], F32, whwork)
        le = sb("le", [P, NQ, EXPERTS], F32, whwork)
        lst = sb("lst", [P, 2, NQ], F32, whwork)
        mixw = sb("mixw", [P, S, EXPERTS], F32, whwork)
        mixp = sb("mixp", [P, NQ, S, EXPERTS], F32, whwork)
        mixa = sb("mixa", [P, NQ, S], F32, whwork)
        mixf = sb("mixf", [P, NQ, BQ, S], F32, whwork)
        mixb = sb("mixb", [P, NQ, EXPERTS], F32, whwork)
        cwr = sb("cwr", [P, TAPS, CG], F32, whwork)
        cwf = sb("cwf", [P, TAPS, NGRP, CG], F32, whwork)
        cwhi = sb("cwhi", [P, TAPS, P], F32R, whwork)
        cwlo = sb("cwlo", [P, TAPS, P], F32R, whwork)
        xhi = sb("xhi", [P, 2, XW], F32R, whwork)
        xlo = sb("xlo", [P, 2, XW], F32R, whwork)
        cnat = sb("cnat", [P, 2, DM], F32, whwork)
        whwork.close()

        wqr = sb("wqr", [P, KC, DM], F32, att)
        wkvr = sb("wkvr", [P, KC, 2 * HD], F32, att)
        wor = sb("wor", [P, G, DM], F32, att)
        wqhi = sb("wqhi", [P, KC, DM], F32R, att)
        wqlo = sb("wqlo", [P, KC, DM], F32R, att)
        wkvhi = sb("wkvhi", [P, KC, 2 * HD], F32R, att)
        wkvlo = sb("wkvlo", [P, KC, 2 * HD], F32R, att)
        wohi = sb("wohi", [P, G, DM], F32R, att)
        wolo = sb("wolo", [P, G, DM], F32R, att)
        qraw = sb("qraw", [P, HQ, G, HD], F32, att)
        qsq = sb("qsq", [P, 2, G, HD], F32, att)
        qn = sb("qn", [P, HQ, G, HD], F32, att)
        qss = sb("qss", [P, HQ, G], F32, att)
        qms = sb("qms", [P, HQ, G], F32, att)
        kms = sb("kms", [P, HQ], F32, att)
        qinv = sb("qinv", [P, HQ, G], F32, att)
        kraw = sb("kraw", [P, HQ, HD], F32, att)
        ksq = sb("ksq", [P, HQ, HD], F32, att)
        kn = sb("kn", [P, HQ, HD], F32, att)
        kss = sb("kss", [P, HQ], F32, att)
        kinv = sb("kinv", [P, HQ], F32, att)
        neghalf = sb("neghalf", [P, HQ, G], F32, att)
        qhi = sb("qhi", [P, HB, G, S], F16, att)
        qlo = sb("qlo", [P, HB, G, S], F16, att)
        khi = sb("khi", [P, HB, S], F16, att)
        klo = sb("klo", [P, HB, S], F16, att)
        vhi = sb("vhi", [P, HQ, HD], F32R, att)
        vlo = sb("vlo", [P, HQ, HD], F32R, att)
        sc = sb("sc", [P, HB, S], F32, att)
        ex = sb("ex", [P, HB, S], F32, att)
        pr = sb("pr", [P, HB, S], F32, att)
        smax = sb("smax", [P, HB], F32, att)
        ssum = sb("ssum", [P, HB], F32, att)
        srec = sb("srec", [P, HB], F32, att)
        pThi = sb("pThi", [P, HQ, G, BQ, S], F32R, att)
        pTlo = sb("pTlo", [P, HQ, G, BQ, S], F32R, att)
        oThi = sb("oThi", [P, HQ, G, P], F32R, att)
        oTlo = sb("oTlo", [P, HQ, G, P], F32R, att)
        wcol = sb("wcol", [P, 4], F32, att)
        wmax = sb("wmax", [P, 2], F32, att)
        wn = sb("wn", [P, 1], F32, att)
        scale = sb("scale", [P, 1], F32, att)
        att.close()

        ffn = ExitStack()
        fThi = sb("fThi", [P, KC, NQ * P], F32R, ffn)
        fTlo = sb("fTlo", [P, KC, NQ * P], F32R, ffn)
        mixwork = ExitStack()
        x2hi = sb("x2hi", [P, 2, DM], F32R, mixwork)
        x2lo = sb("x2lo", [P, 2, DM], F32R, mixwork)
        fnat = sb("fnat", [P, 2, DM], F32, mixwork)
        mixwork.close()
        hThi = sb("hThi", [P, IC, NQ * P], F32R, ffn)
        hTlo = sb("hTlo", [P, IC, NQ * P], F32R, ffn)
        silu = sb("silu", [P, HT], F32, ffn)
        hf = sb("hf", [P, HT], F32, ffn)
        guw = sb("guw", [P, 2, KC, P], I32, ffn)
        guz = sb("guz", [P, 2, KC, P], I32, ffn)
        gus = sb("gus", [P, 2, KC, P], F32, ffn)
        guf = sb("guf", [P, 2, KC, P], F32, ffn)
        guhi = sb("guhi", [P, 2, 2, KC, P], F32R, ffn)
        gulo = sb("gulo", [P, 2, 2, KC, P], F32R, ffn)
        ffn.close()

        l_x0 = sem("l_x0")
        l_x1 = sem("l_x1")
        l_const = sem("l_const")
        l_vec = sem("l_vec")
        l_cond = sem("l_cond")
        l_conv = sem("l_conv")
        l_mlp = sem("l_mlp")
        l_mix = sem("l_mix")
        l_wq = sem("l_wq")
        l_wkv = sem("l_wkv")
        l_wo = sem("l_wo")
        l_guw = sem("l_guw")
        l_dnw = sem("l_dnw")
        l_out = sem("l_out")
        g_pad = sem("g_pad")
        g_ctx = sem("g_ctx")
        g_wabs = sem("g_wabs")
        g_wmax = sem("g_wmax")
        g_zero = sem("g_zero")
        d_ones = sem("d_ones")
        d_ctxr = sem("d_ctxr")
        d_ctxcol = sem("d_ctxcol")
        d_wcol = sem("d_wcol")
        d_wscale = sem("d_wscale")
        d_cwf = sem("d_cwf")
        d_cwlo = sem("d_cwlo")
        d_xlo = sem("d_xlo")
        d_cTlo = sem("d_cTlo")
        d_h2r = sem("d_h2r")
        d_lg = sem("d_lg")
        d_lsum = sem("d_lsum")
        d_le = sem("d_le")
        d_mix = sem("d_mix")
        d_self = sem("d_self")
        a_cwhi = sem("a_cwhi")
        a_xhi = sem("a_xhi")
        a_cnat = sem("a_cnat")
        a_cThi = sem("a_cThi")
        a_h1 = sem("a_h1")
        a_h2 = sem("a_h2")
        a_lexp = sem("a_lexp")
        a_mixhi = sem("a_mixhi")
        t_ctx = sem("t_ctx")
        t_h1 = sem("t_h1")
        t_h2 = sem("t_h2")
        t_lg = sem("t_lg")
        t_conv = sem("t_conv")
        t_cT = sem("t_cT")
        a_wq = sem("a_wq")
        a_wkv = sem("a_wkv")
        a_wo = sem("a_wo")
        p_wq = sem("p_wq")
        p_wkv = sem("p_wkv")
        p_wo = sem("p_wo")
        t_q = sem("t_q")
        t_kv = sem("t_kv")
        t_kT = sem("t_kT")
        t_qT = sem("t_qT")
        t_s = sem("t_s")
        t_pT = sem("t_pT")
        t_pv = sem("t_pv")
        t_y = sem("t_y")
        a_qraw = sem("a_qraw")
        a_qsq = sem("a_qsq")
        d_qss = sem("d_qss")
        d_qms = sem("d_qms")
        d_kms = sem("d_kms")
        p_qpow = sem("p_qpow")
        p_qn = sem("p_qn")
        a_kraw = sem("a_kraw")
        a_ksq = sem("a_ksq")
        d_kss = sem("d_kss")
        p_kpow = sem("p_kpow")
        p_kn = sem("p_kn")
        a_vhi = sem("a_vhi")
        d_vlo = sem("d_vlo")
        a_khi = sem("a_khi")
        d_klo = sem("d_klo")
        a_qhi = sem("a_qhi")
        d_qlo = sem("d_qlo")
        d_sc = sem("d_sc")
        d_smax = sem("d_smax")
        p_sub = sem("p_sub")
        a_exp = sem("a_exp")
        d_srec = sem("d_srec")
        p_pr = sem("p_pr")
        a_pThi = sem("a_pThi")
        d_pTlo = sem("d_pTlo")
        a_oThi = sem("a_oThi")
        d_oTlo = sem("d_oTlo")
        d_y = sem("d_y")
        a_x2hi = sem("a_x2hi")
        d_x2lo = sem("d_x2lo")
        t_f = sem("t_f")
        a_fnat = sem("a_fnat")
        t_fT = sem("t_fT")
        a_fThi = sem("a_fThi")
        d_fTlo = sem("d_fTlo")
        d_gsub = sem("d_gsub")
        p_gmul = sem("p_gmul")
        a_guhi = sem("a_guhi")
        d_gulo = sem("d_gulo")
        t_g = sem("t_g")
        t_u = sem("t_u")
        a_silu = sem("a_silu")
        d_h = sem("d_h")
        a_hhi = sem("a_hhi")
        p_hlo = sem("p_hlo")
        d_dsub = sem("d_dsub")
        p_dmul = sem("p_dmul")
        a_dhi = sem("a_dhi")
        d_dlo = sem("d_dlo")
        t_dn = sem("t_dn")
        t_acc = sem("t_acc")
        d_res = sem("d_res")

        def chain(eng, sm, start=0):
            n = [start]

            def link(ins):
                n[0] += 1
                ins.then_inc(sm, 1)
                eng.wait_ge(sm, n[0])
            return link

        def quads(u_half):
            return range(HQ * u_half, HQ * u_half + HQ)

        block = ctx.enter_context(nc.Block())

        @block.sync
        def _(sp):
            sp.dma_start(const[:, :], const_in).then_inc(l_const, 16)
            sp.dma_start(condT[:, :], cond_in).then_inc(l_cond, 16)
            sp.dma_start(cwT[:, :], cw_in).then_inc(l_cond, 16)
            for b in range(BQ):
                sp.dma_start(cwr[S * b:S * b + S, :, :], conv_in).then_inc(l_conv, 16)
            sp.dma_start(vec[:, :], vec_in).then_inc(l_vec, 16)
            sp.dma_start(x[:, 0:2, :], x_in[:, 0:2, :]).then_inc(l_x0, 16)
            sp.dma_start(x[:, 2:NQ, :], x_in[:, 2:NQ, :]).then_inc(l_x1, 16)
            for dst, src in ((w0, w0_in), (w1, w1_in), (w2, w2_in)):
                sp.dma_start(dst[:, :], src).then_inc(l_mlp, 16)
            sp.dma_start(b2[:, :], b2_in.broadcast_to([P, EXPERTS])).then_inc(l_mlp, 16)
            for b in range(BQ):
                sp.dma_start(mixw[S * b:S * b + S, :, :], mix_in).then_inc(l_mix, 16)

            def load_heads(kv, first):
                if not first:
                    sp.wait_ge(p_wq, KC * kv)
                sp.dma_start(wqr[:, :, :], wq_in[kv]).then_inc(l_wq, 16)
                if not first:
                    sp.wait_ge(p_wkv, 2 * kv)
                sp.dma_start(wkvr[:, :, :], wkv_in[kv]).then_inc(l_wkv, 16)
                if not first:
                    sp.wait_ge(p_wo, G * kv)
                sp.dma_start(wor[:, :, :], wo_in[kv]).then_inc(l_wo, 16)

            sp.wait_ge(t_cT, NQ)
            sp.wait_ge(d_mix, 1)
            sp.wait_ge(a_mixhi, 1)
            load_heads(0, True)
            with sp.Fori(1, HKV) as kv:
                load_heads(kv, False)

            sp.wait_ge(d_y, HQ * UNITS)

            def load_gu(i, first):
                if not first:
                    sp.wait_ge(p_gmul, i)
                sp.dma_start(guw[:, :, :, :], gu_w_in[i]).then_inc(l_guw, 16)
                sp.dma_start(guz[:, :, :, :].rearrange("p a b c -> p (a b c)"),
                             gu_z_in[i].broadcast_to([P, 2 * KC * P])).then_inc(l_guw, 16)
                sp.dma_start(gus[:, :, :, :].rearrange("p a b c -> p (a b c)"),
                             gu_s_in[i].broadcast_to([P, 2 * KC * P])).then_inc(l_guw, 16)

            load_gu(0, True)
            with sp.Fori(1, IC) as i:
                load_gu(i, False)

            def load_dn(i, first):
                if first:
                    sp.wait_ge(p_gmul, IC)
                else:
                    sp.wait_ge(p_dmul, i)
                sp.dma_start(guw[:, 0, :, :].rearrange("p b c -> p (b c)"), dn_w_in[i]).then_inc(l_dnw, 16)
                sp.dma_start(guz[:, 0, :, :].rearrange("p b c -> p (b c)"),
                             dn_z_in[i].broadcast_to([P, DM])).then_inc(l_dnw, 16)
                sp.dma_start(gus[:, 0, :, :].rearrange("p b c -> p (b c)"),
                             dn_s_in[i].broadcast_to([P, DM])).then_inc(l_dnw, 16)

            load_dn(0, True)
            with sp.Fori(1, IC) as i:
                load_dn(i, False)
            for t in range(NQ):
                sp.wait_ge(d_res, t + 1)
                sp.dma_start(out[:, t, :], x[:, t, :]).then_inc(l_out, 16)
            sp.wait_ge(l_out, 16 * NQ)

        @block.tensor
        def _(pe):
            mm = nc.tensor.matmul

            def split_product(o, parts, start, stop):
                n = len(parts)
                for k, (ahi, alo, bhi, blo) in enumerate(parts):
                    mm(o, ahi, bhi, start=start and k == 0, stop=False)
                    mm(o, ahi, blo, start=False, stop=False)
                    last = mm(o, alo, bhi, start=False, stop=stop and k == n - 1)
                return last

            pe.wait_ge(d_ctxr, 1)
            pe.wait_ge(d_ones, 1)
            for q in range(NQ):
                last = mm(PC[0][:, q:q + 1], ctxr[:, BQ * q:BQ * q + BQ, :], ones[:, :], start=True, stop=True)
            last.then_inc(t_ctx, 1)
            pe.wait_ge(l_mlp, 64)
            mm(PC[1][:, 0:B], w0[:, :], condT[:, :], start=True, stop=True).then_inc(t_h1, 1)
            pe.wait_ge(a_h1, 1)
            mm(PC[1][:, 0:B], w1[:, :], h1[:, :], start=True, stop=True).then_inc(t_h2, 1)
            pe.wait_ge(d_h2r, 1)
            for q in range(NQ):
                last = mm(PC[2][:, EXPERTS * q:EXPERTS * q + EXPERTS], h2r[:, BQ * q:BQ * q + BQ, :], w2[:, :],
                          start=True, stop=True)
            last.then_inc(t_lg, 1)

            def conv_transpose(q):
                pe.wait_ge(a_cnat, q + 1)
                if q >= 2:
                    pe.wait_ge(d_cTlo, q - 1)
                for c in range(KC):
                    last = nc.tensor.transpose(PB[q % 2][:, P * c:P * c + P], cnat[:, q % 2, P * c:P * c + P], ident)
                last.then_inc(t_cT, 1)

            pe.wait_ge(d_cwlo, 1)
            for q in range(NQ):
                pe.wait_ge(d_xlo, q + 1)
                if q >= 2:
                    pe.wait_ge(a_cnat, q - 1)
                split_product(PA[q % 2][:, :],
                              [(cwhi[:, k, :], cwlo[:, k, :], xhi[:, q % 2, k:k + DM], xlo[:, q % 2, k:k + DM])
                               for k in range(TAPS)], True, True).then_inc(t_conv, 1)
                if q:
                    conv_transpose(q - 1)
            conv_transpose(NQ - 1)

            def project_q(u, half, kv):
                if half == 0:
                    pe.wait_ge(p_wq, KC * kv + KC)
                for t in range(HQ):
                    tq = HQ * half + t
                    if t < 2:
                        if not (isinstance(u, int) and u == 0):
                            pe.wait_ge(d_vlo, 2 * u)
                            pe.wait_ge(a_vhi, 2 * u)
                            pe.wait_ge(a_kraw, 2 * u)
                    else:
                        pe.wait_ge(a_qraw, HQ * u + t - 1)
                    split_product(PA[t % 2][:, :],
                                  [(cThi[:, tq, c, :], cTlo[:, tq, c, :], wqhi[:, c, :], wqlo[:, c, :])
                                   for c in range(KC)], True, True).then_inc(t_q, 1)

            def project_kv(u, half, kv):
                if half == 0:
                    pe.wait_ge(p_wkv, 2 * kv + 2)
                for j in range(2):
                    pe.wait_ge(a_qraw, HQ * u + 3 + j)
                    for t in (2 * j, 2 * j + 1):
                        tq = HQ * half + t
                        last = split_product(PA[j][:, 2 * HD * (t % 2):2 * HD * (t % 2) + 2 * HD],
                                             [(cThi[:, tq, c, :], cTlo[:, tq, c, :], wkvhi[:, c, :], wkvlo[:, c, :])
                                              for c in range(KC)], True, True)
                    last.then_inc(t_kv, 1)

            def scores(u, half):
                first = isinstance(u, int) and u == 0
                pe.wait_ge(p_kn, u + 1)
                if not first:
                    pe.wait_ge(d_pTlo, u)
                for t in range(HQ):
                    last = nc.tensor.transpose(PB[0][:, P * t:P * t + P], kn[:, t, :], ident)
                last.then_inc(t_kT, 1)
                for t in range(HQ):
                    pe.wait_ge(p_qn, HQ * u + t + 1)
                    if t == 0:
                        if not first:
                            pe.wait_ge(d_sc, u)
                    elif t == 1:
                        pe.wait_ge(d_klo, u + 1)
                    else:
                        pe.wait_ge(d_qlo, HQ * u + t - 1)
                    for g in range(G):
                        last = nc.tensor.transpose(PB[(t + 1) % 2][:, P * g:P * g + P], qn[:, t, g, :], ident)
                    last.then_inc(t_qT, 1)
                pe.wait_ge(d_klo, u + 1)
                pe.wait_ge(d_qlo, HQ * u + HQ)
                for b in range(HB):
                    o = PB[1][:, S * b:S * b + S]
                    mm(o, qhi[:, b, :, :], khi[:, b, :], start=True, stop=False)
                    mm(o, qhi[:, b, :, :], klo[:, b, :], start=False, stop=False)
                    last = mm(o, qlo[:, b, :, :], khi[:, b, :], start=False, stop=True)
                last.then_inc(t_s, 1)

            def apply_probs(u, half):
                first = isinstance(u, int) and u == 0
                pe.wait_ge(p_pr, u + 1)
                for t in range(HQ):
                    last = nc.tensor.transpose(PB[0][:, P * t:P * t + P], pr[:, BQ * t:BQ * t + BQ, :], ident)
                last.then_inc(t_pT, 1)
                pe.wait_ge(d_pTlo, u + 1)
                pe.wait_ge(d_vlo, 2 * u + 2)
                for t in range(HQ):
                    if not first:
                        pe.wait_ge(d_y, HQ * u - HQ + t + 1)
                    split_product(PC[t][:, :], [(vhi[:, t, :], vlo[:, t, :], pThi[:, t, :, :, :], pTlo[:, t, :, :, :])],
                                  True, True).then_inc(t_pv, 1)

            def project_out(u, half, kv):
                if half == 0:
                    pe.wait_ge(p_wo, G * kv + G)
                for t in range(HQ):
                    pe.wait_ge(d_oTlo, HQ * u + t + 1)
                    split_product(PC[t][:, :], [(oThi[:, t, g, :], oTlo[:, t, g, :], wohi[:, g, :], wolo[:, g, :])
                                                for g in range(G)], True, True).then_inc(t_y, 1)

            pe.wait_ge(d_cTlo, NQ)
            project_q(0, 0, 0)
            project_kv(0, 0, 0)
            scores(0, 0)

            def step(u, half, kv):
                prev_kv = kv if half else kv - 1
                project_q(u, half, kv)
                apply_probs(u - 1, 1 - half)
                project_kv(u, half, kv)
                project_out(u - 1, 1 - half, prev_kv)
                scores(u, half)

            step(1, 1, 0)
            with pe.Fori(1, HKV) as kv:
                step(2 * kv, 0, kv)
                step(2 * kv + 1, 1, kv)
            apply_probs(UNITS - 1, 1)
            project_out(UNITS - 1, 1, HKV - 1)

            def mix_transpose(q):
                pe.wait_ge(a_fnat, q + 1)
                if q >= 2:
                    pe.wait_ge(d_fTlo, q - 1)
                for c in range(KC):
                    last = nc.tensor.transpose(PB[q % 2][:, P * c:P * c + P], fnat[:, q % 2, P * c:P * c + P], ident)
                last.then_inc(t_fT, 1)

            for q in range(NQ):
                pe.wait_ge(d_x2lo, q + 1)
                if q >= 2:
                    pe.wait_ge(a_fnat, q - 1)
                split_product(PA[q % 2][:, :], [(mixhi[:, q, :, :], mixlo[:, q, :, :], x2hi[:, q % 2, :],
                                                 x2lo[:, q % 2, :])], True, True).then_inc(t_f, 1)
                if q:
                    mix_transpose(q - 1)
            mix_transpose(NQ - 1)

            def gate_up(i, slot, first):
                pe.wait_ge(d_gulo, i + 1)
                for half in range(2):
                    if first and half == 0:
                        pe.wait_ge(d_fTlo, NQ)
                    if not first:
                        pe.wait_ge(d_h, 2 * i + half - 1)
                    for j, t_done in ((0, t_g), (1, t_u)):
                        split_product(PA[half][:, :] if j == 0 else PC[half][:, :],
                                      [(guhi[:, slot, j, c, :], gulo[:, slot, j, c, :],
                                        fThi[:, c, HT * half:HT * half + HT], fTlo[:, c, HT * half:HT * half + HT])
                                       for c in range(KC)], True, True).then_inc(t_done, 1)

            gate_up(0, 0, True)
            gate_up(1, 1, False)
            with pe.Fori(2, IC, 2) as i:
                gate_up(i, 0, False)
                gate_up(i + 1, 1, False)

            pe.wait_ge(d_h, 2 * IC)
            pe.wait_ge(p_hlo, 2 * IC)
            tail = IC - 2
            for i in range(tail):
                pe.wait_ge(d_dlo, i + 1)
                for q in range(NQ):
                    last = split_product(bank[q][:, :],
                                         [(hThi[:, i, P * q:P * q + P], hTlo[:, i, P * q:P * q + P],
                                           guhi[:, i % 2, 0, :, :], gulo[:, i % 2, 0, :, :])], i == 0, False)
                last.then_inc(t_dn, 1)
            pe.wait_ge(d_dlo, IC)
            for q in range(NQ):
                split_product(bank[q][:, :],
                              [(hThi[:, i, P * q:P * q + P], hTlo[:, i, P * q:P * q + P],
                                guhi[:, i % 2, 0, :, :], gulo[:, i % 2, 0, :, :]) for i in range(tail, IC)],
                              False, True).then_inc(t_acc, 1)

        @block.scalar
        def _(act):
            A = nc.scalar.activation
            act.wait_ge(l_vec, 16)
            act.wait_ge(d_cwf, 1)
            A(cwhi[:, :, :], cwf[:, :, :, :].rearrange("p k a o -> p k (a o)"), ACT.Copy).then_inc(a_cwhi, 1)

            def conv_input(q):
                act.wait_ge(l_x0 if q < 2 else l_x1, 16)
                if q >= 2:
                    act.wait_ge(t_conv, q - 1)
                A(xhi[:, q % 2, PAD:PAD + DM], x[:, q, :], ACT.Copy).then_inc(a_xhi, 1)

            def conv_high(q):
                act.wait_ge(t_cT, q + 1)
                A(cThi[:, q, :, :], PB[q % 2][:, :].rearrange("p (c t) -> p c t", c=KC), ACT.Copy).then_inc(a_cThi, 1)

            conv_input(0)
            conv_input(1)
            act.wait_ge(t_h1, 1)
            A(h1[:, :], PC[1][:, 0:B], ACT.Gelu, bias=vec[:, V_B0:V_B0 + 1]).then_inc(a_h1, 1)
            act.wait_ge(t_h2, 1)
            A(h2[:, :], PC[1][:, 0:B], ACT.Gelu, bias=vec[:, V_B1:V_B1 + 1]).then_inc(a_h2, 1)
            act.wait_ge(d_lg, 1)
            A(le[:, :, :], lg[:, :, :], ACT.Exp).then_inc(a_lexp, 1)
            act.wait_ge(d_ctxcol, 1)
            for q in range(NQ):
                act.wait_ge(t_conv, q + 1)
                if q >= 2:
                    act.wait_ge(t_cT, q - 1)
                A(cnat[:, q % 2, :], PA[q % 2][:, :], ACT.Identity, bias=ctxcol[:, q:q + 1]).then_inc(a_cnat, 1)
                if q + 2 < NQ:
                    conv_input(q + 2)
                if q:
                    conv_high(q - 1)
            conv_high(NQ - 1)
            act.wait_ge(d_mix, 1)
            A(mixhi[:, :, :, :], mixf[:, :, :, :], ACT.Copy).then_inc(a_mixhi, 1)

            def split_wq(kv, first):
                act.wait_ge(l_wq, 16 * kv + 16)
                for c in range(KC):
                    A(wqhi[:, c, :], wqr[:, c, :], ACT.Copy).then_inc(a_wq, 1)

            def split_wkv(kv, first):
                act.wait_ge(l_wkv, 16 * kv + 16)
                for c in range(0, KC, 2):
                    A(wkvhi[:, c:c + 2, :], wkvr[:, c:c + 2, :], ACT.Copy).then_inc(a_wkv, 1)

            def split_wo(kv, first):
                act.wait_ge(l_wo, 16 * kv + 16)
                for g in range(G):
                    A(wohi[:, g, :], wor[:, g, :], ACT.Copy).then_inc(a_wo, 1)

            def queries(u):
                first = isinstance(u, int) and u == 0
                for t in range(HQ):
                    act.wait_ge(t_q, HQ * u + t + 1)
                    if t == 0 and not first:
                        act.wait_ge(p_qn, HQ * u)
                    A(qraw[:, t, :, :], PA[t % 2][:, :].rearrange("p (g d) -> p g d", g=G),
                      ACT.Copy).then_inc(a_qraw, 1)
                    act.wait_ge(a_qraw, HQ * u + t + 1)
                    if not (first and t < 2):
                        act.wait_ge(d_qss, HQ * u + t - 1)
                    A(qsq[:, t % 2, :, :], qraw[:, t, :, :], ACT.Square).then_inc(a_qsq, 1)

            def keys_values(u):
                first = isinstance(u, int) and u == 0
                for j in range(2):
                    kv2 = PA[j][:, :].rearrange("p (t w) -> p t w", t=2)
                    act.wait_ge(t_kv, 2 * u + j + 1)
                    if j == 0 and not first:
                        act.wait_ge(p_kn, u)
                    A(kraw[:, 2 * j:2 * j + 2, :], kv2[:, :, 0:HD], ACT.Copy).then_inc(a_kraw, 1)
                    A(vhi[:, 2 * j:2 * j + 2, :], kv2[:, :, HD:2 * HD], ACT.Copy).then_inc(a_vhi, 1)
                    act.wait_ge(a_kraw, 2 * u + j + 1)
                    if j == 0 and not first:
                        act.wait_ge(d_kss, 2 * u)
                    A(ksq[:, 2 * j:2 * j + 2, :], kraw[:, 2 * j:2 * j + 2, :], ACT.Square).then_inc(a_ksq, 1)

            def score_operands(u):
                act.wait_ge(t_kT, u + 1)
                A(khi[:, :, :], PB[0][:, :].rearrange("p (b k) -> p b k", k=S), ACT.Copy,
                  scale=wn[:, 0:1]).then_inc(a_khi, 1)
                for t in range(HQ):
                    act.wait_ge(t_qT, HQ * u + t + 1)
                    A(qhi[:, BQ * t:BQ * t + BQ, :, :].rearrange("p b g s -> p g b s"),
                      PB[(t + 1) % 2][:, :].rearrange("p (g b s) -> p g b s", g=G, b=BQ),
                      ACT.Copy).then_inc(a_qhi, 1)
                act.wait_ge(p_sub, u + 1)
                if not (isinstance(u, int) and u == 0):
                    act.wait_ge(p_pr, u)
                A(ex[:, :, :], sc[:, :, :], ACT.Exp).then_inc(a_exp, 1)

            def probs_high(u):
                act.wait_ge(t_pT, u + 1)
                for b in range(BQ):
                    A(pThi[S * b:S * b + S, :, :, b, :],
                      PB[0][S * b:S * b + S, :].rearrange("p (t g s) -> p t g s", t=HQ, g=G),
                      ACT.Copy).then_inc(a_pThi, 1)

            def outputs_high(u):
                for t in range(HQ):
                    act.wait_ge(t_pv, HQ * u + t + 1)
                    A(oThi[:, t, :, :], PC[t][:, :].rearrange("p (g n) -> p g n", g=G), ACT.Copy).then_inc(a_oThi, 1)

            act.wait_ge(d_wscale, 1)
            split_wq(0, True)
            split_wkv(0, True)
            queries(0)
            keys_values(0)
            split_wo(0, True)
            score_operands(0)

            def step(u, half, kv, last):
                queries(u)
                if half and not last:
                    act.wait_ge(t_q, HQ * u + HQ)
                    split_wq(kv + 1, False)
                probs_high(u - 1)
                outputs_high(u - 1)
                keys_values(u)
                if half and not last:
                    act.wait_ge(t_kv, 2 * u + 2)
                    split_wkv(kv + 1, False)
                if not half:
                    act.wait_ge(t_y, HQ * u)
                    split_wo(kv, False)
                score_operands(u)

            step(1, 1, 0, False)
            with act.Fori(1, HKV - 1) as kv:
                step(2 * kv, 0, kv, False)
                step(2 * kv + 1, 1, kv, False)
            step(UNITS - 2, 0, HKV - 1, True)
            step(UNITS - 1, 1, HKV - 1, True)
            probs_high(UNITS - 1)
            outputs_high(UNITS - 1)

            act.wait_ge(d_y, HQ * UNITS)

            def mix_high(q):
                act.wait_ge(t_fT, q + 1)
                A(fThi[:, :, P * q:P * q + P], PB[q % 2][:, :].rearrange("p (c t) -> p c t", c=KC),
                  ACT.Copy).then_inc(a_fThi, 1)

            def mix_input(q):
                if q >= 2:
                    act.wait_ge(t_f, q - 1)
                A(x2hi[:, q % 2, :], x[:, q, :], ACT.Copy).then_inc(a_x2hi, 1)

            mix_input(0)
            mix_input(1)
            for q in range(NQ):
                act.wait_ge(t_f, q + 1)
                if q >= 2:
                    act.wait_ge(t_fT, q - 1)
                A(fnat[:, q % 2, :], PA[q % 2][:, :], ACT.Identity, bias=aggb[:, q:q + 1]).then_inc(a_fnat, 1)
                if q + 2 < NQ:
                    mix_input(q + 2)
                if q:
                    mix_high(q - 1)
            mix_high(NQ - 1)

            def weights_high(i, slot, first):
                act.wait_ge(p_gmul, i + 1)
                if not first:
                    act.wait_ge(t_u, 2 * i - 2)
                A(guhi[:, slot, :, :, :], guf[:, :, :, :], ACT.Copy).then_inc(a_guhi, 1)

            def hidden_high(i, first):
                for half in range(2):
                    act.wait_ge(t_g, 2 * i + half + 1)
                    if not (first and half == 0):
                        act.wait_ge(d_h, 2 * i + half)
                    A(silu[:, :], PA[half][:, :], ACT.Silu).then_inc(a_silu, 1)
                    act.wait_ge(d_h, 2 * i + half + 1)
                    A(hThi[:, i, HT * half:HT * half + HT], hf[:, :], ACT.Copy).then_inc(a_hhi, 1)

            weights_high(0, 0, True)
            weights_high(1, 1, True)
            hidden_high(0, True)
            with act.Fori(1, IC - 1, 2) as i:
                weights_high(i + 1, 0, False)
                hidden_high(i, False)
                weights_high(i + 2, 1, False)
                hidden_high(i + 1, False)
            hidden_high(IC - 1, False)

            def down_high(i, slot, first):
                act.wait_ge(p_dmul, i + 1)
                if first:
                    act.wait_ge(t_u, 2 * IC)
                else:
                    act.wait_ge(t_dn, i - 1)
                A(guhi[:, slot, 0, :, :], guf[:, 0, :, :], ACT.Copy).then_inc(a_dhi, 1)

            down_high(0, 0, True)
            down_high(1, 1, True)
            with act.Fori(2, IC, 2) as i:
                down_high(i, 0, False)
                down_high(i + 1, 1, False)

        @block.vector
        def _(dve):
            V = nc.vector
            link = chain(dve, d_self)
            V.memset(ones[:, :], 1.0).then_inc(d_ones, 1)
            dve.wait_ge(l_const, 16)
            dve.wait_ge(l_conv, 64)
            V.tensor_tensor(cwf[:, :, :, :], cwr[:, :, None, :].broadcast_to([P, TAPS, NGRP, CG]),
                            blkmask[:, None, :, None].broadcast_to([P, TAPS, NGRP, CG]), ALU.mult).then_inc(d_cwf, 1)
            dve.wait_ge(l_cond, 32)
            V.tensor_tensor(ctxr[:, :, :], condT[:, :, None].broadcast_to([P, B, S]),
                            cwT[:, None, :].broadcast_to([P, B, S]), ALU.mult).then_inc(d_ctxr, 1)
            dve.wait_ge(a_cwhi, 1)
            V.tensor_tensor(cwlo[:, :, :], cwf[:, :, :, :].rearrange("p k a o -> p k (a o)"), cwhi[:, :, :].bitcast(F32),
                            ALU.subtract).then_inc(d_cwlo, 1)

            def conv_low(q):
                dve.wait_ge(a_xhi, q + 1)
                if q < 1:
                    dve.wait_ge(g_pad, 4)
                V.tensor_tensor(xlo[:, q % 2, PAD:PAD + DM], x[:, q, :], xhi[:, q % 2, PAD:PAD + DM].bitcast(F32),
                                ALU.subtract).then_inc(d_xlo, 1)

            conv_low(0)
            conv_low(1)
            dve.wait_ge(l_vec, 16)
            dve.wait_ge(t_ctx, 1)
            V.tensor_scalar(ctxcol[:, :], PC[0][:, 0:NQ], vec[:, V_FS:V_FS + 1], None, ALU.add).then_inc(d_ctxcol, 1)
            dve.wait_ge(a_h2, 1)
            V.tensor_copy(h2r[:, :, :], h2[:, :, None].broadcast_to([P, B, S])).then_inc(d_h2r, 1)
            dve.wait_ge(t_lg, 1)
            e8 = [P, NQ, EXPERTS]
            link(V.tensor_tensor(lg[:, :, :], PC[2][:, 0:NQ * EXPERTS].rearrange("p (q e) -> p q e", q=NQ),
                                 b2[:, None, :].broadcast_to(e8), ALU.add))
            link(V.tensor_reduce(lst[:, 0, :], lg[:, :, :], AX_X, ALU.max))
            V.tensor_tensor(lg[:, :, :], lg[:, :, :], lst[:, 0, :, None].broadcast_to(e8),
                            ALU.subtract).then_inc(d_lg, 1)
            for q in range(NQ):
                if q + 2 < NQ:
                    conv_low(q + 2)
                if q == 0:
                    dve.wait_ge(a_lexp, 1)
                    link(V.tensor_reduce(lst[:, 1, :], le[:, :, :], AX_X, ALU.add))
                    link(V.reciprocal(lst[:, 0, :], lst[:, 1, :]))
                    link(V.tensor_tensor(le[:, :, :], le[:, :, :], lst[:, 0, :, None].broadcast_to(e8), ALU.mult))
                if q == 1:
                    dve.wait_ge(l_mix, 64)
                    link(V.tensor_tensor(mixp[:, :, :, :], mixw[:, None, :, :].broadcast_to([P, NQ, S, EXPERTS]),
                                         le[:, :, None, :].broadcast_to([P, NQ, S, EXPERTS]), ALU.mult))
                if q == 2:
                    link(V.tensor_reduce(mixa[:, :, :], mixp[:, :, :, :], AX_X, ALU.add))
                    link(V.tensor_tensor(mixb[:, :, :], le[:, :, :],
                                         vec[:, None, V_BK:V_BK + EXPERTS].broadcast_to(e8), ALU.mult))
                if q == 3:
                    link(V.tensor_reduce(aggb[:, :], mixb[:, :, :], AX_X, ALU.add))
                    V.tensor_tensor(mixf[:, :, :, :], mixa[:, :, None, :].broadcast_to([P, NQ, BQ, S]),
                                    quadmask[:, None, :, None].broadcast_to([P, NQ, BQ, S]),
                                    ALU.mult).then_inc(d_mix, 1)
                dve.wait_ge(a_cThi, q + 1)
                V.tensor_tensor(cTlo[:, q, :, :], PB[q % 2][:, :].rearrange("p (c t) -> p c t", c=KC),
                                cThi[:, q, :, :].bitcast(F32), ALU.subtract).then_inc(d_cTlo, 1)
            dve.wait_ge(a_mixhi, 1)
            link(V.tensor_tensor(mixlo[:, :, :, :], mixf[:, :, :, :], mixhi[:, :, :, :].bitcast(F32), ALU.subtract))
            dve.wait_ge(t_cT, NQ)
            V.memset(neghalf[:, :, :], -0.5).then_inc(d_wcol, 1)
            link(V.tensor_tensor(wcol[:, 0:1], vec[:, V_QW:V_QW + 1], vec[:, V_KW:V_KW + 1], ALU.mult))
            link(V.tensor_scalar(wcol[:, 1:2], wcol[:, 0:1], -1.0, None, ALU.mult))
            V.tensor_tensor(wcol[:, 2:3], wcol[:, 0:1], wcol[:, 1:2], ALU.max).then_inc(d_wcol, 1)
            dve.wait_ge(g_wmax, 1)
            link(V.tensor_scalar(wmax[:, 1:2], wmax[:, 0:1], 1e-30, None, ALU.max))
            link(V.reciprocal(wcol[:, 3:4], wmax[:, 1:2]))
            link(V.tensor_scalar(scale[:, :], wmax[:, 1:2], float(HD) ** -0.5, None, ALU.mult))
            V.tensor_tensor(wn[:, :], wcol[:, 0:1], wcol[:, 3:4], ALU.mult).then_inc(d_wscale, 1)

            def queries(u):
                for t in range(HQ):
                    dve.wait_ge(a_qsq, HQ * u + t + 1)
                    V.tensor_reduce(qss[:, t, :], qsq[:, t % 2, :, :], AX_X, ALU.add).then_inc(d_qss, 1)
                if not (isinstance(u, int) and u == 0):
                    dve.wait_ge(p_qpow, u)
                dve.wait_ge(d_qss, HQ * u + HQ)
                V.tensor_scalar(qms[:, :, :], qss[:, :, :], 1.0 / HD, EPS, ALU.mult, ALU.add).then_inc(d_qms, 1)

            def keys_values(u):
                for j in range(2):
                    dve.wait_ge(a_ksq, 2 * u + j + 1)
                    dve.wait_ge(a_vhi, 2 * u + j + 1)
                    kv2 = PA[j][:, :].rearrange("p (t w) -> p t w", t=2)
                    V.tensor_tensor(vlo[:, 2 * j:2 * j + 2, :], kv2[:, :, HD:2 * HD],
                                    vhi[:, 2 * j:2 * j + 2, :].bitcast(F32), ALU.subtract).then_inc(d_vlo, 1)
                    V.tensor_reduce(kss[:, 2 * j:2 * j + 2], ksq[:, 2 * j:2 * j + 2, :], AX_X,
                                    ALU.add).then_inc(d_kss, 1)
                if not (isinstance(u, int) and u == 0):
                    dve.wait_ge(p_kpow, u)
                dve.wait_ge(d_kss, 2 * u + 2)
                V.tensor_scalar(kms[:, :], kss[:, :], 1.0 / HD, EPS, ALU.mult, ALU.add).then_inc(d_kms, 1)

            def score_operands(u, kv):
                first = isinstance(u, int) and u == 0
                dve.wait_ge(a_khi, u + 1)
                V.scalar_tensor_tensor(klo[:, :, :], PB[0][:, :].rearrange("p (b k) -> p b k", k=S), wn[:, 0:1],
                                       khi[:, :, :], ALU.mult, ALU.subtract).then_inc(d_klo, 1)
                for t in range(HQ):
                    dve.wait_ge(a_qhi, HQ * u + t + 1)
                    V.tensor_tensor(qlo[:, BQ * t:BQ * t + BQ, :, :].rearrange("p b g s -> p g b s"),
                                    PB[(t + 1) % 2][:, :].rearrange("p (g b s) -> p g b s", g=G, b=BQ),
                                    qhi[:, BQ * t:BQ * t + BQ, :, :].rearrange("p b g s -> p g b s"),
                                    ALU.subtract).then_inc(d_qlo, 1)
                dve.wait_ge(t_s, u + 1)
                if not first:
                    dve.wait_ge(a_exp, u)
                bias = const[:, bass.ds(kv * S + C_BIAS, S)]
                V.scalar_tensor_tensor(sc[:, :, :], PB[1][:, :].rearrange("p (b k) -> p b k", k=S), scale[:, 0:1],
                                       bias[:, None, :].broadcast_to([P, HB, S]), ALU.mult,
                                       ALU.add).then_inc(d_sc, 1)
                dve.wait_ge(d_sc, u + 1)
                V.tensor_reduce(smax[:, :], sc[:, :, :], AX_X, ALU.max).then_inc(d_smax, 1)
                dve.wait_ge(a_exp, u + 1)
                V.tensor_reduce(ssum[:, :], ex[:, :, :], AX_X, ALU.add).then_inc(d_srec, 1)
                dve.wait_ge(d_srec, 2 * u + 1)
                if not first:
                    dve.wait_ge(p_pr, u)
                V.reciprocal(srec[:, :], ssum[:, :]).then_inc(d_srec, 1)

            def probs_low(u):
                for b in range(BQ):
                    dve.wait_ge(a_pThi, BQ * u + b + 1)
                    ins = V.tensor_tensor(pTlo[S * b:S * b + S, :, :, b, :],
                                          PB[0][S * b:S * b + S, :].rearrange("p (t g s) -> p t g s", t=HQ, g=G),
                                          pThi[S * b:S * b + S, :, :, b, :].bitcast(F32), ALU.subtract)
                ins.then_inc(d_pTlo, 1)

            def outputs_low(u):
                for t in range(HQ):
                    dve.wait_ge(a_oThi, HQ * u + t + 1)
                    V.tensor_tensor(oTlo[:, t, :, :], PC[t][:, :].rearrange("p (g n) -> p g n", g=G),
                                    oThi[:, t, :, :].bitcast(F32), ALU.subtract).then_inc(d_oTlo, 1)

            def add_outputs(u, half):
                for t in range(HQ):
                    dve.wait_ge(t_y, HQ * u + t + 1)
                    if not (isinstance(u, int) and u < 2):
                        dve.wait_ge(d_y, HQ * u - 2 * HQ + t + 1)
                    q = HQ * half + t
                    V.tensor_tensor(x[:, q, :], PC[t][:, :], x[:, q, :], ALU.add).then_inc(d_y, 1)

            dve.wait_ge(g_zero, 2)
            queries(0)
            keys_values(0)
            score_operands(0, 0)

            def step(u, half, kv):
                queries(u)
                probs_low(u - 1)
                outputs_low(u - 1)
                keys_values(u)
                add_outputs(u - 1, 1 - half)
                score_operands(u, kv)

            step(1, 1, 0)
            step(2, 0, 1)
            step(3, 1, 1)
            with dve.Fori(2, HKV) as kv:
                step(2 * kv, 0, kv)
                step(2 * kv + 1, 1, kv)
            probs_low(UNITS - 1)
            outputs_low(UNITS - 1)
            add_outputs(UNITS - 1, 1)

            def mix_input(q):
                dve.wait_ge(a_x2hi, q + 1)
                V.tensor_tensor(x2lo[:, q % 2, :], x[:, q, :], x2hi[:, q % 2, :].bitcast(F32),
                                ALU.subtract).then_inc(d_x2lo, 1)

            dve.wait_ge(d_y, HQ * UNITS)
            mix_input(0)
            mix_input(1)
            for q in range(NQ):
                if q + 2 < NQ:
                    mix_input(q + 2)
                dve.wait_ge(a_fThi, q + 1)
                V.tensor_tensor(fTlo[:, :, P * q:P * q + P], PB[q % 2][:, :].rearrange("p (c t) -> p c t", c=KC),
                                fThi[:, :, P * q:P * q + P].bitcast(F32), ALU.subtract).then_inc(d_fTlo, 1)

            def weights_low(i, slot):
                dve.wait_ge(l_guw, 48 * i + 48)
                if not (isinstance(i, int) and i == 0):
                    dve.wait_ge(d_gulo, i)
                V.tensor_tensor(guf[:, :, :, :], guw[:, :, :, :], guz[:, :, :, :], ALU.subtract).then_inc(d_gsub, 1)
                dve.wait_ge(a_guhi, i + 1)
                V.tensor_tensor(gulo[:, slot, :, :, :], guf[:, :, :, :], guhi[:, slot, :, :, :].bitcast(F32),
                                ALU.subtract).then_inc(d_gulo, 1)

            def hidden(i, first):
                for half in range(2):
                    dve.wait_ge(t_u, 2 * i + half + 1)
                    dve.wait_ge(a_silu, 2 * i + half + 1)
                    if not (first and half == 0):
                        dve.wait_ge(p_hlo, 2 * i + half)
                    V.tensor_tensor(hf[:, :], silu[:, :], PC[half][:, :], ALU.mult).then_inc(d_h, 1)

            weights_low(0, 0)
            weights_low(1, 1)
            hidden(0, True)
            with dve.Fori(1, IC - 1, 2) as i:
                weights_low(i + 1, 0)
                hidden(i, False)
                weights_low(i + 2, 1)
                hidden(i + 1, False)
            hidden(IC - 1, False)

            def down_low(i, slot, first):
                dve.wait_ge(l_dnw, 48 * i + 48)
                dve.wait_ge(d_gulo, IC)
                if not first:
                    dve.wait_ge(d_dlo, i)
                V.tensor_tensor(guf[:, 0, :, :], guw[:, 0, :, :], guz[:, 0, :, :], ALU.subtract).then_inc(d_dsub, 1)
                dve.wait_ge(a_dhi, i + 1)
                V.tensor_tensor(gulo[:, slot, 0, :, :], guf[:, 0, :, :], guhi[:, slot, 0, :, :].bitcast(F32),
                                ALU.subtract).then_inc(d_dlo, 1)

            down_low(0, 0, True)
            down_low(1, 1, False)
            with dve.Fori(2, IC, 2) as i:
                down_low(i, 0, False)
                down_low(i + 1, 1, False)
            for q in range(NQ):
                dve.wait_ge(t_acc, q + 1)
                V.tensor_tensor(x[:, q, :], bank[q][:, :], x[:, q, :], ALU.add).then_inc(d_res, 1)

        @block.gpsimd
        def _(pool):
            Q = nc.gpsimd
            for t in (xhi, xlo):
                Q.memset(t[:, :, 0:PAD].bitcast(F32), 0.0).then_inc(g_pad, 1)
                Q.memset(t[:, :, PAD + DM:XW].bitcast(F32), 0.0).then_inc(g_pad, 1)
            pool.wait_ge(t_cT, NQ)
            pool.wait_ge(d_mix, 1)
            pool.wait_ge(a_mixhi, 1)
            pool.wait_ge(d_wcol, 2)
            Q.partition_all_reduce(wmax[:, 0:1], wcol[:, 2:3], P, bass.bass_isa.ReduceOp.max).then_inc(g_wmax, 1)
            Q.memset(pThi[:, :, :, :, :].bitcast(F32), 0.0).then_inc(g_zero, 1)
            Q.memset(pTlo[:, :, :, :, :].bitcast(F32), 0.0).then_inc(g_zero, 1)

            def split_wq(kv):
                for c in range(KC):
                    pool.wait_ge(a_wq, KC * kv + c + 1)
                    Q.tensor_tensor(wqlo[:, c, :], wqr[:, c, :], wqhi[:, c, :].bitcast(F32),
                                    ALU.subtract).then_inc(p_wq, 1)

            def split_wkv(kv):
                for c in range(0, KC, 2):
                    pool.wait_ge(a_wkv, 2 * kv + c // 2 + 1)
                    Q.tensor_tensor(wkvlo[:, c:c + 2, :], wkvr[:, c:c + 2, :], wkvhi[:, c:c + 2, :].bitcast(F32),
                                    ALU.subtract).then_inc(p_wkv, 1)

            def split_wo(kv):
                for g in range(G):
                    pool.wait_ge(a_wo, G * kv + g + 1)
                    Q.tensor_tensor(wolo[:, g, :], wor[:, g, :], wohi[:, g, :].bitcast(F32),
                                    ALU.subtract).then_inc(p_wo, 1)

            def queries(u):
                pool.wait_ge(d_qms, u + 1)
                Q.tensor_tensor(qinv[:, :, :], qms[:, :, :], neghalf[:, :, :], ALU.pow).then_inc(p_qpow, 1)
                pool.wait_ge(p_qpow, u + 1)
                for t in range(HQ):
                    if not (isinstance(u, int) and u == 0):
                        pool.wait_ge(t_qT, HQ * u - HQ + t + 1)
                    Q.tensor_tensor(qn[:, t, :, :], qraw[:, t, :, :],
                                    qinv[:, t, :, None].broadcast_to([P, G, HD]), ALU.mult).then_inc(p_qn, 1)

            def keys_values(u):
                pool.wait_ge(d_kms, u + 1)
                Q.tensor_tensor(kinv[:, :], kms[:, :], neghalf[:, :, 0], ALU.pow).then_inc(p_kpow, 1)
                pool.wait_ge(p_kpow, u + 1)
                if not (isinstance(u, int) and u == 0):
                    pool.wait_ge(t_kT, u)
                Q.tensor_tensor(kn[:, :, :], kraw[:, :, :], kinv[:, :, None].broadcast_to([P, HQ, HD]),
                                ALU.mult).then_inc(p_kn, 1)

            def softmax(u):
                pool.wait_ge(d_smax, u + 1)
                Q.tensor_tensor(sc[:, :, :], sc[:, :, :], smax[:, :, None].broadcast_to([P, HB, S]),
                                ALU.subtract).then_inc(p_sub, 1)
                pool.wait_ge(d_srec, 2 * u + 2)
                if not (isinstance(u, int) and u == 0):
                    pool.wait_ge(t_pT, u)
                Q.tensor_tensor(pr[:, :, :], ex[:, :, :], srec[:, :, None].broadcast_to([P, HB, S]),
                                ALU.mult).then_inc(p_pr, 1)

            pool.wait_ge(g_zero, 2)
            split_wq(0)
            split_wkv(0)
            queries(0)
            keys_values(0)
            split_wo(0)
            softmax(0)

            def step(u, half, kv, last):
                queries(u)
                if half and not last:
                    split_wq(kv + 1)
                keys_values(u)
                if half and not last:
                    split_wkv(kv + 1)
                if not half:
                    split_wo(kv)
                softmax(u)

            step(1, 1, 0, False)
            with pool.Fori(1, HKV - 1) as kv:
                step(2 * kv, 0, kv, False)
                step(2 * kv + 1, 1, kv, False)
            step(UNITS - 2, 0, HKV - 1, True)
            step(UNITS - 1, 1, HKV - 1, True)

            pool.wait_ge(d_y, HQ * UNITS)

            def scale_gu(i):
                pool.wait_ge(d_gsub, i + 1)
                Q.tensor_tensor(guf[:, :, :, :], guf[:, :, :, :], gus[:, :, :, :], ALU.mult).then_inc(p_gmul, 1)

            def hidden_low(i):
                for half in range(2):
                    pool.wait_ge(a_hhi, 2 * i + half + 1)
                    Q.tensor_tensor(hTlo[:, i, HT * half:HT * half + HT], hf[:, :],
                                    hThi[:, i, HT * half:HT * half + HT].bitcast(F32),
                                    ALU.subtract).then_inc(p_hlo, 1)

            scale_gu(0)
            scale_gu(1)
            hidden_low(0)
            with pool.Fori(1, IC - 1) as i:
                scale_gu(i + 1)
                hidden_low(i)
            hidden_low(IC - 1)

            with pool.Fori(0, IC) as i:
                pool.wait_ge(d_dsub, i + 1)
                Q.tensor_tensor(guf[:, 0, :, :], guf[:, 0, :, :], gus[:, 0, :, :], ALU.mult).then_inc(p_dmul, 1)


def kernel(**inputs):
    import concourse.bacc as _bacc
    from concourse import mybir as _mybir
    from concourse.bass_utils import run_bass_kernel_spmd as _run

    a = {k: np.asarray(v) for k, v in inputs.items()}

    def tile_gu(w):
        return w.reshape(KC, P, IC, P).transpose(2, 1, 0, 3)

    def row_gu(w):
        return w.reshape(KC, IC, P).transpose(1, 0, 2)

    wk = a["L0_attn_Wk"].reshape(HKV, HD, KC, P).transpose(0, 3, 2, 1)
    wv = a["L0_attn_Wv"].reshape(HKV, HD, KC, P).transpose(0, 3, 2, 1)
    vec = np.concatenate([
        np.stack([a["L0_cond2_b0"], a["L0_cond2_b1"], a["L0_attn_q_norm_w"], a["L0_attn_k_norm_w"],
                  np.tile(a["fside_S_0"], BQ)], axis=1),
        np.tile(a["L0_cond2_bias_k"].T, (BQ, 1))], axis=1)
    arrays = {
        "x": a["x"].reshape(NQ, P, DM).transpose(1, 0, 2),
        "cond": a["cond_128"].T,
        "cw": a["L0_cond_c_weight"].T,
        "conv": a["L0_cond_weight"].reshape(S // CG, CG, CG, TAPS).transpose(0, 2, 3, 1).reshape(S, TAPS, CG),
        "wq": a["L0_attn_Wq"].reshape(HKV, G * HD, KC, P).transpose(0, 3, 2, 1),
        "wkv": np.concatenate([wk, wv], axis=3),
        "wo": a["L0_attn_Wo"].T.reshape(HKV, G, HD, DM).transpose(0, 2, 1, 3) if a["L0_attn_Wo"].shape[0] == DM else None,
        "w0": a["L0_cond2_W0"], "w1": a["L0_cond2_W1"], "w2": a["L0_cond2_W2"],
        "b2": a["L0_cond2_b2"].reshape(1, EXPERTS),
        "mix": a["L0_cond2_weight"][..., 0].transpose(2, 1, 0),
        "vec": vec,
        "gu_w": np.stack([tile_gu(a["L0_ffn_gate_w"]), tile_gu(a["L0_ffn_up_w"])], axis=2),
        "gu_z": np.stack([row_gu(a["L0_ffn_gate_z"]), row_gu(a["L0_ffn_up_z"])], axis=1).reshape(IC, 1, 2 * KC * P),
        "gu_s": np.stack([row_gu(a["L0_ffn_gate_s"]), row_gu(a["L0_ffn_up_s"])], axis=1).reshape(IC, 1, 2 * KC * P),
        "dn_w": a["L0_ffn_down_w"].reshape(IC, P, DM),
        "dn_z": a["L0_ffn_down_z"].reshape(IC, 1, DM),
        "dn_s": a["L0_ffn_down_s"].reshape(IC, 1, DM),
        "consts": constants(),
    }
    nc = _bacc.Bacc("TRN2", target_bir_lowering=False, num_devices=1)
    feed, args = {}, []
    for name, v in arrays.items():
        v = np.ascontiguousarray(v)
        feed[f"in_{name}"] = v
        args.append(nc.dram_tensor(f"in_{name}", v.shape, _mybir.dt.from_np(v.dtype), kind="ExternalInput").ap())
    o = nc.dram_tensor("result", (P, NQ, DM), _mybir.dt.float32, kind="ExternalOutput").ap()
    build(nc, *args, o)
    r = _run(nc, [feed], core_ids=[0])
    return np.asarray(r.results[0]["result"]).transpose(1, 0, 2).reshape(B, S, DM)
```

```python
from contextlib import ExitStack

import numpy as np

import concourse.bass as bass
from concourse import mybir

P = 128
B, S, DM = 32, 32, 512
H, HKV, HD = 32, 8, 128
G = H // HKV
KC = DM // P
BQ = P // S
NQ = B // BQ
HQ = NQ // 2
HB = B // 2
HT = HB * S
TAPS = 9
PAD = TAPS // 2
CG = 8
NGRP = P // CG
XW = DM + 2 * PAD
EXPERTS = 8
INNER = 1792
IC = INNER // P
UNITS = 2 * HKV
EPS = 1e-6
MASKED = -1e30

F32 = mybir.dt.float32
F32R = mybir.dt.float32r
F16 = mybir.dt.float16
I32 = mybir.dt.int32
ALU = mybir.AluOpType
ACT = mybir.ActivationFunctionType
AX_X = mybir.AxisListType.X

C_ID, C_BIAS, C_BLK, C_QUAD = 0, P, P + HKV * S, P + HKV * S + NGRP
C_ALL = C_QUAD + BQ
V_B0, V_B1, V_QW, V_KW, V_FS, V_BK = 0, 1, 2, 3, 4, 5
V_ALL = V_BK + EXPERTS


def constants():
    t = np.zeros((P, C_ALL), np.float32)
    t[:, C_ID:C_ID + P] = np.eye(P, dtype=np.float32)
    start = 2 ** (-2 ** (-(np.log2(H) - 3)))
    slopes = np.array([start * start ** i for i in range(H)], np.float32).reshape(HKV, G)
    pos = np.arange(S, dtype=np.float32)
    rel = pos[None, :] - pos[:, None]
    bias = np.where(rel > 0, np.float32(MASKED), slopes[:, :, None, None] * rel)
    t[:, C_BIAS:C_BLK] = bias.transpose(1, 2, 0, 3).reshape(P, HKV * S)
    p = np.arange(P)
    t[:, C_BLK:C_QUAD] = p[:, None] // CG == np.arange(NGRP)
    t[:, C_QUAD:C_ALL] = p[:, None] // S == np.arange(BQ)
    return t


def build(nc, x_in, cond_in, cw_in, conv_in, wq_in, wkv_in, wo_in, w0_in, w1_in, w2_in, b2_in, mix_in, vec_in,
          gu_w_in, gu_z_in, gu_s_in, dn_w_in, dn_z_in, dn_s_in, const_in, out):
    ctx = ExitStack()
    with ctx:
        def sb(name, shape, dt=F32, where=ctx):
            return where.enter_context(nc.sbuf_tensor(name, shape, dt))

        def sem(name):
            return ctx.enter_context(nc.semaphore(name))

        bank = [ctx.enter_context(nc.psum_tensor(f"bank{i}", [P, DM], F32)) for i in range(8)]
        PA, PB, PC = bank[0:2], bank[2:4], bank[4:8]

        x = sb("x", [P, NQ, DM])
        const = sb("const", [P, C_ALL])
        vec = sb("vec", [P, V_ALL])
        ones = sb("ones", [P, 1])
        aggb = sb("aggb", [P, NQ])
        mixhi = sb("mixhi", [P, NQ, BQ, S], F32R)
        mixlo = sb("mixlo", [P, NQ, BQ, S], F32R)
        ident = const[:, C_ID:C_ID + P]
        blkmask = const[:, C_BLK:C_QUAD]
        quadmask = const[:, C_QUAD:C_ALL]

        neghalf = sb("neghalf", [P, HQ, G])
        wcol = sb("wcol", [P, 4])
        wmax = sb("wmax", [P, 2])
        wn = sb("wn", [P, 1])
        scale = sb("scale", [P, 1])

        proj = ExitStack()
        wqr = sb("wqr", [P, KC, DM], F32, proj)
        wkvr = sb("wkvr", [P, KC, 2 * HD], F32, proj)
        wqhi = sb("wqhi", [P, KC, DM], F32R, proj)
        wqlo = sb("wqlo", [P, KC, DM], F32R, proj)
        wkvhi = sb("wkvhi", [P, KC, 2 * HD], F32R, proj)
        wkvlo = sb("wkvlo", [P, KC, 2 * HD], F32R, proj)
        att = ExitStack()
        cThi = sb("cThi", [P, NQ, KC, P], F32R, att)
        cTlo = sb("cTlo", [P, NQ, KC, P], F32R, att)
        qraw = sb("qraw", [P, HQ, G, HD], F32, att)
        qsq = sb("qsq", [P, 2, G, HD], F32, att)
        qn = sb("qn", [P, HQ, G, HD], F32, att)
        wor = sb("wor", [P, G, DM], F32, att)
        wohi = sb("wohi", [P, G, DM], F32R, att)
        wolo = sb("wolo", [P, G, DM], F32R, att)
        early = ExitStack()
        condT = sb("condT", [P, B], F32, early)
        cwT = sb("cwT", [P, S], F32, early)
        ctxr = sb("ctxr", [P, B, S], F32, early)
        ctxcol = sb("ctxcol", [P, NQ], F32, early)
        w0 = sb("w0", [P, P], F32, early)
        w1 = sb("w1", [P, P], F32, early)
        w2 = sb("w2", [P, EXPERTS], F32, early)
        b2 = sb("b2", [P, EXPERTS], F32, early)
        h1 = sb("h1", [P, B], F32, early)
        h2 = sb("h2", [P, B], F32, early)
        h2r = sb("h2r", [P, B, S], F32, early)
        lg = sb("lg", [P, NQ, EXPERTS], F32, early)
        le = sb("le", [P, NQ, EXPERTS], F32, early)
        lst = sb("lst", [P, 2, NQ], F32, early)
        mixw = sb("mixw", [P, S, EXPERTS], F32, early)
        mixp = sb("mixp", [P, NQ, S, EXPERTS], F32, early)
        mixa = sb("mixa", [P, NQ, S], F32, early)
        mixf = sb("mixf", [P, NQ, BQ, S], F32, early)
        mixb = sb("mixb", [P, NQ, EXPERTS], F32, early)
        cwr = sb("cwr", [P, TAPS, CG], F32, early)
        cwf = sb("cwf", [P, TAPS, NGRP, CG], F32, early)
        cwhi = sb("cwhi", [P, TAPS, P], F32R, early)
        cwlo = sb("cwlo", [P, TAPS, P], F32R, early)
        xhi = sb("xhi", [P, 2, XW], F32R, early)
        xlo = sb("xlo", [P, 2, XW], F32R, early)
        cnat = sb("cnat", [P, 2, DM], F32, early)
        early.close()
        qss = sb("qss", [P, HQ, G], F32, att)
        qms = sb("qms", [P, HQ, G], F32, att)
        kms = sb("kms", [P, HQ], F32, att)
        qinv = sb("qinv", [P, HQ, G], F32, att)
        kraw = sb("kraw", [P, HQ, HD], F32, att)
        ksq = sb("ksq", [P, HQ, HD], F32, att)
        kn = sb("kn", [P, HQ, HD], F32, att)
        kss = sb("kss", [P, HQ], F32, att)
        kinv = sb("kinv", [P, HQ], F32, att)
        qhi = sb("qhi", [P, HB, G, S], F16, att)
        qlo = sb("qlo", [P, HB, G, S], F16, att)
        khi = sb("khi", [P, HB, S], F16, att)
        klo = sb("klo", [P, HB, S], F16, att)
        vhi = sb("vhi", [P, 2, HQ, HD], F32R, att)
        vlo = sb("vlo", [P, 2, HQ, HD], F32R, att)
        sc = sb("sc", [P, HB, S], F32, att)
        ex = sb("ex", [P, HB, S], F32, att)
        pr = sb("pr", [P, HB, S], F32, att)
        smax = sb("smax", [P, HB], F32, att)
        ssum = sb("ssum", [P, HB], F32, att)
        srec = sb("srec", [P, HB], F32, att)
        pThi = sb("pThi", [P, HQ, G, BQ, S], F32R, att)
        pTlo = sb("pTlo", [P, HQ, G, BQ, S], F32R, att)
        oThi = sb("oThi", [P, HQ, G, P], F32R, att)
        oTlo = sb("oTlo", [P, HQ, G, P], F32R, att)
        att.close()
        proj.close()

        ffn = ExitStack()
        guw = sb("guw", [P, 2, KC, P], I32, ffn)
        guz = sb("guz", [P, 2, KC, P], I32, ffn)
        gus = sb("gus", [P, 2, KC, P], F32, ffn)
        guf = sb("guf", [P, 2, KC, P], F32, ffn)
        guhi = sb("guhi", [P, 2, 2, KC, P], F32R, ffn)
        gulo = sb("gulo", [P, 2, 2, KC, P], F32R, ffn)
        silu = sb("silu", [P, HT], F32, ffn)
        hf = sb("hf", [P, HT], F32, ffn)
        fThi = sb("fThi", [P, KC, NQ * P], F32R, ffn)
        fTlo = sb("fTlo", [P, KC, NQ * P], F32R, ffn)
        mixwork = ExitStack()
        x2hi = sb("x2hi", [P, 2, DM], F32R, mixwork)
        x2lo = sb("x2lo", [P, 2, DM], F32R, mixwork)
        fnat = sb("fnat", [P, 2, DM], F32, mixwork)
        mixwork.close()
        hThi = sb("hThi", [P, IC, NQ * P], F32R, ffn)
        hTlo = sb("hTlo", [P, IC, NQ * P], F32R, ffn)
        ffn.close()

        l_x0 = sem("l_x0")
        l_x1 = sem("l_x1")
        l_const = sem("l_const")
        l_vec = sem("l_vec")
        l_cond = sem("l_cond")
        l_conv = sem("l_conv")
        l_mlp = sem("l_mlp")
        l_mix = sem("l_mix")
        l_wq = sem("l_wq")
        l_wkv = sem("l_wkv")
        l_wo = sem("l_wo")
        l_guw = sem("l_guw")
        l_dn0 = sem("l_dn0")
        l_dn1 = sem("l_dn1")
        d_mixlo = sem("d_mixlo")
        l_out = sem("l_out")
        g_pad = sem("g_pad")
        g_ctx = sem("g_ctx")
        g_wabs = sem("g_wabs")
        g_wmax = sem("g_wmax")
        g_zero = sem("g_zero")
        d_ones = sem("d_ones")
        d_ctxr = sem("d_ctxr")
        d_ctxcol = sem("d_ctxcol")
        d_wcol = sem("d_wcol")
        d_wscale = sem("d_wscale")
        d_cwf = sem("d_cwf")
        d_cwlo = sem("d_cwlo")
        d_xlo = sem("d_xlo")
        d_cTlo = sem("d_cTlo")
        d_h2r = sem("d_h2r")
        d_lg = sem("d_lg")
        d_lsum = sem("d_lsum")
        d_le = sem("d_le")
        d_mix = sem("d_mix")
        d_self = sem("d_self")
        a_cwhi = sem("a_cwhi")
        a_xhi = sem("a_xhi")
        a_cnat = sem("a_cnat")
        a_cThi = sem("a_cThi")
        a_h1 = sem("a_h1")
        a_h2 = sem("a_h2")
        a_lexp = sem("a_lexp")
        a_mixhi = sem("a_mixhi")
        t_ctx = sem("t_ctx")
        t_h1 = sem("t_h1")
        t_h2 = sem("t_h2")
        t_lg = sem("t_lg")
        t_conv = sem("t_conv")
        t_cT = sem("t_cT")
        a_wq = sem("a_wq")
        a_wkv = sem("a_wkv")
        a_wo = sem("a_wo")
        p_wq = sem("p_wq")
        p_wkv = sem("p_wkv")
        p_wo = sem("p_wo")
        t_q = sem("t_q")
        t_kv = sem("t_kv")
        t_kT = sem("t_kT")
        t_qT = sem("t_qT")
        t_s = sem("t_s")
        t_pT = sem("t_pT")
        t_pv = sem("t_pv")
        t_y = sem("t_y")
        a_qraw = sem("a_qraw")
        a_qsq = sem("a_qsq")
        d_qss = sem("d_qss")
        d_qms = sem("d_qms")
        d_kms = sem("d_kms")
        p_qpow = sem("p_qpow")
        p_qn = sem("p_qn")
        a_kraw = sem("a_kraw")
        a_ksq = sem("a_ksq")
        d_kss = sem("d_kss")
        p_kpow = sem("p_kpow")
        p_kn = sem("p_kn")
        a_vhi = sem("a_vhi")
        d_vlo = sem("d_vlo")
        a_khi = sem("a_khi")
        d_klo = sem("d_klo")
        a_qhi = sem("a_qhi")
        d_qlo = sem("d_qlo")
        d_sc = sem("d_sc")
        d_smax = sem("d_smax")
        p_sub = sem("p_sub")
        a_exp = sem("a_exp")
        d_srec = sem("d_srec")
        p_pr = sem("p_pr")
        a_pThi = sem("a_pThi")
        d_pTlo = sem("d_pTlo")
        a_oThi = sem("a_oThi")
        d_oTlo = sem("d_oTlo")
        d_y = sem("d_y")
        p_x2hi = sem("p_x2hi")
        d_x2lo = sem("d_x2lo")
        t_f = sem("t_f")
        a_fnat = sem("a_fnat")
        t_fT = sem("t_fT")
        a_fThi = sem("a_fThi")
        d_fTlo = sem("d_fTlo")
        d_gsub = sem("d_gsub")
        p_gmul = sem("p_gmul")
        a_guhi = sem("a_guhi")
        d_gulo = sem("d_gulo")
        t_g = sem("t_g")
        t_u = sem("t_u")
        a_silu = sem("a_silu")
        d_h = sem("d_h")
        a_hhi = sem("a_hhi")
        p_hlo = sem("p_hlo")
        d_dsub = sem("d_dsub")
        p_dmul = sem("p_dmul")
        a_dhi = sem("a_dhi")
        d_dlo = sem("d_dlo")
        t_dn = sem("t_dn")
        t_acc = sem("t_acc")
        d_res = sem("d_res")

        def chain(eng, sm, start=0):
            n = [start]

            def link(ins):
                n[0] += 1
                ins.then_inc(sm, 1)
                eng.wait_ge(sm, n[0])
            return link

        def quads(u_half):
            return range(HQ * u_half, HQ * u_half + HQ)

        block = ctx.enter_context(nc.Block())

        @block.sync
        def _(sp):
            sp.dma_start(const[:, :], const_in).then_inc(l_const, 16)
            sp.dma_start(condT[:, :], cond_in).then_inc(l_cond, 16)
            sp.dma_start(cwT[:, :], cw_in).then_inc(l_cond, 16)
            for b in range(BQ):
                sp.dma_start(cwr[S * b:S * b + S, :, :], conv_in).then_inc(l_conv, 16)
            sp.dma_start(vec[:, :], vec_in).then_inc(l_vec, 16)
            sp.dma_start(x[:, 0:2, :], x_in[:, 0:2, :]).then_inc(l_x0, 16)
            sp.dma_start(x[:, 2:NQ, :], x_in[:, 2:NQ, :]).then_inc(l_x1, 16)
            for dst, src in ((w0, w0_in), (w1, w1_in), (w2, w2_in)):
                sp.dma_start(dst[:, :], src).then_inc(l_mlp, 16)
            sp.dma_start(b2[:, :], b2_in.broadcast_to([P, EXPERTS])).then_inc(l_mlp, 16)
            for b in range(BQ):
                sp.dma_start(mixw[S * b:S * b + S, :, :], mix_in).then_inc(l_mix, 16)

            def load_heads(kv, first):
                if not first:
                    sp.wait_ge(p_wq, KC * kv)
                sp.dma_start(wqr[:, :, :], wq_in[kv]).then_inc(l_wq, 16)
                if not first:
                    sp.wait_ge(p_wkv, 2 * kv)
                sp.dma_start(wkvr[:, :, :], wkv_in[kv]).then_inc(l_wkv, 16)
                if not first:
                    sp.wait_ge(p_wo, G * kv)
                sp.dma_start(wor[:, :, :], wo_in[kv]).then_inc(l_wo, 16)

            load_heads(0, True)
            with sp.Fori(1, HKV) as kv:
                load_heads(kv, False)

            sp.wait_ge(p_wq, KC * HKV)
            sp.wait_ge(p_wkv, 2 * HKV)
            sp.wait_ge(t_kv, 2 * UNITS)

            def load_gu(i, first):
                if not first:
                    sp.wait_ge(p_gmul, i)
                sp.dma_start(guw[:, :, :, :], gu_w_in[i]).then_inc(l_guw, 16)
                sp.dma_start(guz[:, :, :, :].rearrange("p a b c -> p (a b c)"),
                             gu_z_in[i].broadcast_to([P, 2 * KC * P])).then_inc(l_guw, 16)
                sp.dma_start(gus[:, :, :, :].rearrange("p a b c -> p (a b c)"),
                             gu_s_in[i].broadcast_to([P, 2 * KC * P])).then_inc(l_guw, 16)

            load_gu(0, True)
            with sp.Fori(1, IC) as i:
                load_gu(i, False)

            def load_dn(i, slot, loaded, first):
                if first:
                    sp.wait_ge(p_gmul, IC)
                else:
                    sp.wait_ge(p_dmul, i - 1)
                sp.dma_start(guw[:, slot, :, :].rearrange("p b c -> p (b c)"), dn_w_in[i]).then_inc(loaded, 16)
                sp.dma_start(guz[:, slot, :, :].rearrange("p b c -> p (b c)"),
                             dn_z_in[i].broadcast_to([P, DM])).then_inc(loaded, 16)
                sp.dma_start(gus[:, slot, :, :].rearrange("p b c -> p (b c)"),
                             dn_s_in[i].broadcast_to([P, DM])).then_inc(loaded, 16)

            load_dn(0, 0, l_dn0, True)
            load_dn(1, 1, l_dn1, True)
            with sp.Fori(1, IC // 2) as pair:
                load_dn(2 * pair, 0, l_dn0, False)
                load_dn(2 * pair + 1, 1, l_dn1, False)
            for t in range(NQ):
                sp.wait_ge(d_res, t + 1)
                sp.dma_start(out[:, t, :], x[:, t, :]).then_inc(l_out, 16)
            sp.wait_ge(l_out, 16 * NQ)

        @block.tensor
        def _(pe):
            mm = nc.tensor.matmul

            def split_product(o, parts, start, stop):
                n = len(parts)
                for k, (ahi, alo, bhi, blo) in enumerate(parts):
                    mm(o, ahi, bhi, start=start and k == 0, stop=False)
                    mm(o, ahi, blo, start=False, stop=False)
                    last = mm(o, alo, bhi, start=False, stop=stop and k == n - 1)
                return last

            def context():
                pe.wait_ge(d_ctxr, 1)
                pe.wait_ge(d_ones, 1)
                for q in range(NQ):
                    last = mm(PC[0][:, q:q + 1], ctxr[:, BQ * q:BQ * q + BQ, :], ones[:, :], start=True, stop=True)
                last.then_inc(t_ctx, 1)

            def gate_layer1():
                pe.wait_ge(l_mlp, 64)
                mm(PC[1][:, 0:B], w0[:, :], condT[:, :], start=True, stop=True).then_inc(t_h1, 1)

            def gate_layer2():
                pe.wait_ge(a_h1, 1)
                mm(PC[1][:, 0:B], w1[:, :], h1[:, :], start=True, stop=True).then_inc(t_h2, 1)

            def gate_logits():
                pe.wait_ge(d_h2r, 1)
                for q in range(NQ):
                    last = mm(PC[2][:, EXPERTS * q:EXPERTS * q + EXPERTS], h2r[:, BQ * q:BQ * q + BQ, :], w2[:, :],
                              start=True, stop=True)
                last.then_inc(t_lg, 1)

            def conv_transpose(q):
                pe.wait_ge(a_cnat, q + 1)
                if q >= 2:
                    pe.wait_ge(d_cTlo, q - 1)
                for c in range(KC):
                    last = nc.tensor.transpose(PB[q % 2][:, P * c:P * c + P], cnat[:, q % 2, P * c:P * c + P], ident)
                last.then_inc(t_cT, 1)

            pe.wait_ge(d_cwlo, 1)
            for q in range(NQ):
                pe.wait_ge(d_xlo, q + 1)
                if q >= 2:
                    pe.wait_ge(a_cnat, q - 1)
                split_product(PA[q % 2][:, :],
                              [(cwhi[:, k, :], cwlo[:, k, :], xhi[:, q % 2, k:k + DM], xlo[:, q % 2, k:k + DM])
                               for k in range(TAPS)], True, True).then_inc(t_conv, 1)
                if q:
                    conv_transpose(q - 1)
                if q == 0:
                    context()
                elif q == 1:
                    gate_layer1()
                elif q == 2:
                    gate_layer2()
                elif q == 4:
                    gate_logits()
            conv_transpose(NQ - 1)

            def project_q(u, half, kv, t):
                if half == 0 and t == 0:
                    pe.wait_ge(p_wq, KC * kv + KC)
                if t >= 2:
                    pe.wait_ge(a_qraw, HQ * u + t - 1)
                elif not (isinstance(u, int) and u == 0):
                    pe.wait_ge(d_vlo, 2 * u)
                    pe.wait_ge(a_kraw, 2 * u)
                tq = HQ * half + t
                split_product(PA[t % 2][:, :],
                              [(cThi[:, tq, c, :], cTlo[:, tq, c, :], wqhi[:, c, :], wqlo[:, c, :])
                               for c in range(KC)], True, True).then_inc(t_q, 1)

            def project_kv(u, half, kv):
                if half == 0:
                    pe.wait_ge(p_wkv, 2 * kv + 2)
                for j in range(2):
                    pe.wait_ge(a_qraw, HQ * u + 3 + j)
                    for t in (2 * j, 2 * j + 1):
                        tq = HQ * half + t
                        last = split_product(PA[j][:, 2 * HD * (t % 2):2 * HD * (t % 2) + 2 * HD],
                                             [(cThi[:, tq, c, :], cTlo[:, tq, c, :], wkvhi[:, c, :], wkvlo[:, c, :])
                                              for c in range(KC)], True, True)
                    last.then_inc(t_kv, 1)

            def transpose_k(u):
                pe.wait_ge(p_kn, u + 1)
                if not (isinstance(u, int) and u == 0):
                    pe.wait_ge(d_pTlo, u)
                for t in range(HQ):
                    last = nc.tensor.transpose(PB[0][:, P * t:P * t + P], kn[:, t, :], ident)
                last.then_inc(t_kT, 1)

            def transpose_q(u, t):
                pe.wait_ge(p_qn, HQ * u + t + 1)
                if t == 0:
                    if not (isinstance(u, int) and u == 0):
                        pe.wait_ge(d_sc, u)
                elif t == 1:
                    pe.wait_ge(d_klo, u + 1)
                else:
                    pe.wait_ge(d_qlo, HQ * u + t - 1)
                for g in range(G):
                    last = nc.tensor.transpose(PB[(t + 1) % 2][:, P * g:P * g + P], qn[:, t, g, :], ident)
                last.then_inc(t_qT, 1)

            def scores(u):
                pe.wait_ge(d_klo, u + 1)
                pe.wait_ge(d_qlo, HQ * u + HQ)
                for b in range(HB):
                    o = PB[1][:, S * b:S * b + S]
                    mm(o, qhi[:, b, :, :], khi[:, b, :], start=True, stop=False)
                    mm(o, qhi[:, b, :, :], klo[:, b, :], start=False, stop=False)
                    last = mm(o, qlo[:, b, :, :], khi[:, b, :], start=False, stop=True)
                last.then_inc(t_s, 1)

            def transpose_probs(u):
                pe.wait_ge(p_pr, u + 1)
                pe.wait_ge(d_qlo, HQ * u + HQ)
                for t in range(HQ):
                    last = nc.tensor.transpose(PB[0][:, P * t:P * t + P], pr[:, BQ * t:BQ * t + BQ, :], ident)
                last.then_inc(t_pT, 1)

            def apply_probs(u, half):
                pe.wait_ge(d_pTlo, u + 1)
                pe.wait_ge(d_vlo, 2 * u + 2)
                for t in range(HQ):
                    if not (isinstance(u, int) and u == 0):
                        pe.wait_ge(d_y, HQ * u - HQ + t + 1)
                    split_product(PC[t][:, :], [(vhi[:, half, t, :], vlo[:, half, t, :], pThi[:, t, :, :, :],
                                                 pTlo[:, t, :, :, :])], True, True).then_inc(t_pv, 1)

            def project_out(u, half, kv, t):
                if half == 0 and t == 0:
                    pe.wait_ge(p_wo, G * kv + G)
                pe.wait_ge(d_oTlo, HQ * u + t + 1)
                split_product(PC[t][:, :], [(oThi[:, t, g, :], oTlo[:, t, g, :], wohi[:, g, :], wolo[:, g, :])
                                            for g in range(G)], True, True).then_inc(t_y, 1)

            def step(u, half, kv):
                project_q(u, half, kv, 0)
                scores(u - 1)
                for t in range(1, HQ):
                    project_q(u, half, kv, t)
                transpose_probs(u - 1)
                project_kv(u, half, kv)
                apply_probs(u - 1, 1 - half)
                for t in range(HQ):
                    project_out(u - 1, 1 - half, kv if half else kv - 1, t)
                    if t == 0:
                        transpose_k(u)
                    transpose_q(u, t)

            pe.wait_ge(d_cTlo, NQ)
            for t in range(HQ):
                project_q(0, 0, 0, t)
            project_kv(0, 0, 0)
            transpose_k(0)
            for t in range(HQ):
                transpose_q(0, t)
            step(1, 1, 0)
            with pe.Fori(1, HKV) as kv:
                step(2 * kv, 0, kv)
                step(2 * kv + 1, 1, kv)

            def mix(q):
                pe.wait_ge(d_x2lo, q + 1)
                if q < 2:
                    pe.wait_ge(d_vlo, 2 * UNITS)
                else:
                    pe.wait_ge(a_fnat, q - 1)
                split_product(PA[q % 2][:, :], [(mixhi[:, q, :, :], mixlo[:, q, :, :], x2hi[:, q % 2, :],
                                                 x2lo[:, q % 2, :])], True, True).then_inc(t_f, 1)

            def mix_transpose(q):
                pe.wait_ge(a_fnat, q + 1)
                pe.wait_ge(d_y, HQ * (UNITS - 1) if q < HQ else HQ * (UNITS - 1) + q - HQ + 1)
                for c in range(KC):
                    last = nc.tensor.transpose(PC[q % HQ][:, P * c:P * c + P], fnat[:, q % 2, P * c:P * c + P], ident)
                last.then_inc(t_fT, 1)

            scores(UNITS - 1)
            mix(0)
            mix(1)
            mix_transpose(0)
            mix(2)
            mix_transpose(1)
            mix(3)
            mix_transpose(2)
            transpose_probs(UNITS - 1)
            mix_transpose(3)
            pe.wait_ge(d_fTlo, HQ)
            apply_probs(UNITS - 1, 1)
            for t in range(HQ):
                project_out(UNITS - 1, 1, HKV - 1, t)
            for q in range(HQ, NQ):
                mix(q)
                if q > HQ:
                    mix_transpose(q - 1)
            mix_transpose(NQ - 1)

            def gate_up(i, slot, first):
                pe.wait_ge(d_gulo, i + 1)
                for half in range(2):
                    if first and half == 0:
                        pe.wait_ge(d_fTlo, NQ)
                    if not first:
                        pe.wait_ge(d_h, 2 * i + half - 1)
                    for j, t_done in ((0, t_g), (1, t_u)):
                        split_product(PA[half][:, :] if j == 0 else PC[half][:, :],
                                      [(guhi[:, slot, j, c, :], gulo[:, slot, j, c, :],
                                        fThi[:, c, HT * half:HT * half + HT], fTlo[:, c, HT * half:HT * half + HT])
                                       for c in range(KC)], True, True).then_inc(t_done, 1)

            gate_up(0, 0, True)
            gate_up(1, 1, False)
            with pe.Fori(2, IC, 2) as i:
                gate_up(i, 0, False)
                gate_up(i + 1, 1, False)

            free_first = (2, 3, 6, 7, 0, 4, 1, 5)
            tail = IC - 2
            for i in range(tail):
                pe.wait_ge(d_dlo, i + 1)
                for n, q in enumerate(free_first):
                    if i == 0 and n >= 4:
                        pe.wait_ge(d_h, 2 * IC - 1 + (n >= 6))
                    last = split_product(bank[q][:, :],
                                         [(hThi[:, i, P * q:P * q + P], hTlo[:, i, P * q:P * q + P],
                                           guhi[:, i % 2, 0, :, :], gulo[:, i % 2, 0, :, :])], i == 0, False)
                last.then_inc(t_dn, 1)
            pe.wait_ge(d_dlo, IC)
            pe.wait_ge(p_hlo, 2 * IC)
            for q in range(NQ):
                split_product(bank[q][:, :],
                              [(hThi[:, i, P * q:P * q + P], hTlo[:, i, P * q:P * q + P],
                                guhi[:, i % 2, 0, :, :], gulo[:, i % 2, 0, :, :]) for i in range(tail, IC)],
                              False, True).then_inc(t_acc, 1)

        @block.scalar
        def _(act):
            A = nc.scalar.activation
            act.wait_ge(l_vec, 16)
            act.wait_ge(d_cwf, 1)
            A(cwhi[:, :, :], cwf[:, :, :, :].rearrange("p k a o -> p k (a o)"), ACT.Copy).then_inc(a_cwhi, 1)

            def conv_input(q):
                act.wait_ge(l_x0 if q < 2 else l_x1, 16)
                if q >= 2:
                    act.wait_ge(t_conv, q - 1)
                A(xhi[:, q % 2, PAD:PAD + DM], x[:, q, :], ACT.Copy).then_inc(a_xhi, 1)

            def conv_high(q):
                act.wait_ge(t_cT, q + 1)
                A(cThi[:, q, :, :], PB[q % 2][:, :].rearrange("p (c t) -> p c t", c=KC), ACT.Copy).then_inc(a_cThi, 1)

            conv_input(0)
            conv_input(1)
            act.wait_ge(d_ctxcol, 1)
            for q in range(NQ):
                act.wait_ge(t_conv, q + 1)
                if q >= 2:
                    act.wait_ge(t_cT, q - 1)
                A(cnat[:, q % 2, :], PA[q % 2][:, :], ACT.Identity, bias=ctxcol[:, q:q + 1]).then_inc(a_cnat, 1)
                if q + 2 < NQ:
                    conv_input(q + 2)
                if q:
                    conv_high(q - 1)
                if q == 1:
                    act.wait_ge(t_h1, 1)
                    A(h1[:, :], PC[1][:, 0:B], ACT.Gelu, bias=vec[:, V_B0:V_B0 + 1]).then_inc(a_h1, 1)
                elif q == 2:
                    act.wait_ge(t_h2, 1)
                    A(h2[:, :], PC[1][:, 0:B], ACT.Gelu, bias=vec[:, V_B1:V_B1 + 1]).then_inc(a_h2, 1)
                elif q == 3:
                    act.wait_ge(l_wq, 16)
                    for c in range(KC):
                        A(wqhi[:, c, :], wqr[:, c, :], ACT.Copy).then_inc(a_wq, 1)
                elif q == 4:
                    act.wait_ge(l_wkv, 16)
                    for c in range(0, KC, 2):
                        A(wkvhi[:, c:c + 2, :], wkvr[:, c:c + 2, :], ACT.Copy).then_inc(a_wkv, 1)
                elif q == 5:
                    act.wait_ge(d_lg, 1)
                    A(le[:, :, :], lg[:, :, :], ACT.Exp).then_inc(a_lexp, 1)
            conv_high(NQ - 1)
            act.wait_ge(d_mix, 1)
            A(mixhi[:, :, :, :], mixf[:, :, :, :], ACT.Copy).then_inc(a_mixhi, 1)

            def split_wq(kv):
                act.wait_ge(t_q, 8 * kv)
                act.wait_ge(l_wq, 16 * kv + 16)
                for c in range(KC):
                    A(wqhi[:, c, :], wqr[:, c, :], ACT.Copy).then_inc(a_wq, 1)

            def split_wkv(kv):
                act.wait_ge(t_kv, 4 * kv)
                act.wait_ge(l_wkv, 16 * kv + 16)
                for c in range(0, KC, 2):
                    A(wkvhi[:, c:c + 2, :], wkvr[:, c:c + 2, :], ACT.Copy).then_inc(a_wkv, 1)

            def split_wo(kv):
                if not (isinstance(kv, int) and kv == 0):
                    act.wait_ge(t_y, 2 * HQ * kv)
                act.wait_ge(l_wo, 16 * kv + 16)
                for g in range(G):
                    A(wohi[:, g, :], wor[:, g, :], ACT.Copy).then_inc(a_wo, 1)

            def queries(u, t):
                first = isinstance(u, int) and u == 0
                act.wait_ge(t_q, HQ * u + t + 1)
                if not first:
                    act.wait_ge(p_qn, HQ * u - HQ + t + 1)
                A(qraw[:, t, :, :], PA[t % 2][:, :].rearrange("p (g d) -> p g d", g=G),
                  ACT.Copy).then_inc(a_qraw, 1)
                act.wait_ge(a_qraw, HQ * u + t + 1)
                if not (first and t < 2):
                    act.wait_ge(d_qss, HQ * u + t - 1)
                A(qsq[:, t % 2, :, :], qraw[:, t, :, :], ACT.Square).then_inc(a_qsq, 1)

            def keys_values(u, half):
                first = isinstance(u, int) and u == 0
                for j in range(2):
                    kv2 = PA[j][:, :].rearrange("p (t w) -> p t w", t=2)
                    act.wait_ge(t_kv, 2 * u + j + 1)
                    if j == 0 and not first:
                        act.wait_ge(p_kn, u)
                    A(kraw[:, 2 * j:2 * j + 2, :], kv2[:, :, 0:HD], ACT.Copy).then_inc(a_kraw, 1)
                    A(vhi[:, half, 2 * j:2 * j + 2, :], kv2[:, :, HD:2 * HD], ACT.Copy).then_inc(a_vhi, 1)
                    act.wait_ge(a_kraw, 2 * u + j + 1)
                    if j == 0 and not first:
                        act.wait_ge(d_kss, 2 * u)
                    A(ksq[:, 2 * j:2 * j + 2, :], kraw[:, 2 * j:2 * j + 2, :], ACT.Square).then_inc(a_ksq, 1)

            def score_operands(u):
                act.wait_ge(t_kT, u + 1)
                A(khi[:, :, :], PB[0][:, :].rearrange("p (b k) -> p b k", k=S), ACT.Copy,
                  scale=wn[:, 0:1]).then_inc(a_khi, 1)
                for t in range(HQ):
                    act.wait_ge(t_qT, HQ * u + t + 1)
                    A(qhi[:, BQ * t:BQ * t + BQ, :, :].rearrange("p b g s -> p g b s"),
                      PB[(t + 1) % 2][:, :].rearrange("p (g b s) -> p g b s", g=G, b=BQ),
                      ACT.Copy).then_inc(a_qhi, 1)

            def exponentials(u):
                act.wait_ge(p_sub, u + 1)
                if not (isinstance(u, int) and u == 0):
                    act.wait_ge(p_pr, u)
                A(ex[:, :, :], sc[:, :, :], ACT.Exp).then_inc(a_exp, 1)

            def probs_high(u):
                act.wait_ge(t_pT, u + 1)
                for b in range(BQ):
                    A(pThi[S * b:S * b + S, :, :, b, :],
                      PB[0][S * b:S * b + S, :].rearrange("p (t g s) -> p t g s", t=HQ, g=G),
                      ACT.Copy).then_inc(a_pThi, 1)

            def outputs_high(u):
                for t in range(HQ):
                    act.wait_ge(t_pv, HQ * u + t + 1)
                    A(oThi[:, t, :, :], PC[t][:, :].rearrange("p (g n) -> p g n", g=G), ACT.Copy).then_inc(a_oThi, 1)

            def step(u, half, kv, last):
                queries(u, 0)
                exponentials(u - 1)
                queries(u, 1)
                if half:
                    split_wo(kv)
                queries(u, 2)
                queries(u, 3)
                probs_high(u - 1)
                if half and not last:
                    split_wq(kv + 1)
                keys_values(u, half)
                if half and not last:
                    split_wkv(kv + 1)
                outputs_high(u - 1)
                score_operands(u)

            act.wait_ge(t_cT, NQ)
            act.wait_ge(d_mixlo, 1)
            act.wait_ge(d_wscale, 1)
            for t in range(HQ):
                queries(0, t)
            keys_values(0, 0)
            score_operands(0)
            step(1, 1, 0, False)
            with act.Fori(1, HKV - 1) as kv:
                step(2 * kv, 0, kv, False)
                step(2 * kv + 1, 1, kv, False)
            step(UNITS - 2, 0, HKV - 1, True)
            step(UNITS - 1, 1, HKV - 1, True)

            def mix_out(q):
                act.wait_ge(t_f, q + 1)
                if q >= 2:
                    act.wait_ge(t_fT, q - 1)
                A(fnat[:, q % 2, :], PA[q % 2][:, :], ACT.Identity, bias=aggb[:, q:q + 1]).then_inc(a_fnat, 1)

            def mix_high(q):
                act.wait_ge(t_fT, q + 1)
                A(fThi[:, :, P * q:P * q + P], PC[q % HQ][:, :].rearrange("p (c t) -> p c t", c=KC),
                  ACT.Copy).then_inc(a_fThi, 1)

            def weights_high(i, slot, first):
                act.wait_ge(p_gmul, i + 1)
                if not first:
                    act.wait_ge(t_u, 2 * i - 2)
                A(guhi[:, slot, :, :, :], guf[:, :, :, :], ACT.Copy).then_inc(a_guhi, 1)

            def hidden_high(i, first):
                for half in range(2):
                    act.wait_ge(t_g, 2 * i + half + 1)
                    if not (first and half == 0):
                        act.wait_ge(d_h, 2 * i + half)
                    A(silu[:, :], PA[half][:, :], ACT.Silu).then_inc(a_silu, 1)
                    act.wait_ge(d_h, 2 * i + half + 1)
                    A(hThi[:, i, HT * half:HT * half + HT], hf[:, :], ACT.Copy).then_inc(a_hhi, 1)

            exponentials(UNITS - 1)
            for q in range(HQ):
                mix_out(q)
                if q:
                    mix_high(q - 1)
            probs_high(UNITS - 1)
            mix_high(HQ - 1)
            weights_high(0, 0, True)
            weights_high(1, 1, True)
            outputs_high(UNITS - 1)
            for q in range(HQ, NQ):
                mix_out(q)
                if q > HQ:
                    mix_high(q - 1)
            mix_high(NQ - 1)
            hidden_high(0, True)
            with act.Fori(1, IC - 1, 2) as i:
                weights_high(i + 1, 0, False)
                hidden_high(i, False)
                weights_high(i + 2, 1, False)
                hidden_high(i + 1, False)

            def down_high(i, slot, first):
                act.wait_ge(p_dmul, i + 1)
                if first:
                    act.wait_ge(t_u, 2 * IC - 2 + 2 * slot)
                else:
                    act.wait_ge(t_dn, i - 1)
                A(guhi[:, slot, 0, :, :], guf[:, slot, :, :], ACT.Copy).then_inc(a_dhi, 1)

            down_high(0, 0, True)
            hidden_high(IC - 1, False)
            down_high(1, 1, True)
            with act.Fori(2, IC, 2) as i:
                down_high(i, 0, False)
                down_high(i + 1, 1, False)

        @block.vector
        def _(dve):
            V = nc.vector
            link = chain(dve, d_self)
            V.memset(ones[:, :], 1.0).then_inc(d_ones, 1)
            dve.wait_ge(l_const, 16)
            dve.wait_ge(l_conv, 64)
            V.tensor_tensor(cwf[:, :, :, :], cwr[:, :, None, :].broadcast_to([P, TAPS, NGRP, CG]),
                            blkmask[:, None, :, None].broadcast_to([P, TAPS, NGRP, CG]), ALU.mult).then_inc(d_cwf, 1)
            dve.wait_ge(l_cond, 32)
            V.tensor_tensor(ctxr[:, :, :], condT[:, :, None].broadcast_to([P, B, S]),
                            cwT[:, None, :].broadcast_to([P, B, S]), ALU.mult).then_inc(d_ctxr, 1)
            dve.wait_ge(a_cwhi, 1)
            V.tensor_tensor(cwlo[:, :, :], cwf[:, :, :, :].rearrange("p k a o -> p k (a o)"), cwhi[:, :, :].bitcast(F32),
                            ALU.subtract).then_inc(d_cwlo, 1)

            def conv_low(q):
                dve.wait_ge(a_xhi, q + 1)
                if q < 1:
                    dve.wait_ge(g_pad, 4)
                V.tensor_tensor(xlo[:, q % 2, PAD:PAD + DM], x[:, q, :], xhi[:, q % 2, PAD:PAD + DM].bitcast(F32),
                                ALU.subtract).then_inc(d_xlo, 1)

            conv_low(0)
            dve.wait_ge(l_vec, 16)
            dve.wait_ge(t_ctx, 1)
            V.tensor_scalar(ctxcol[:, :], PC[0][:, 0:NQ], vec[:, V_FS:V_FS + 1], None, ALU.add).then_inc(d_ctxcol, 1)
            conv_low(1)
            V.memset(neghalf[:, :, :], -0.5).then_inc(d_wcol, 1)
            link(V.tensor_tensor(wcol[:, 0:1], vec[:, V_QW:V_QW + 1], vec[:, V_KW:V_KW + 1], ALU.mult))
            link(V.tensor_scalar(wcol[:, 1:2], wcol[:, 0:1], -1.0, None, ALU.mult))
            V.tensor_tensor(wcol[:, 2:3], wcol[:, 0:1], wcol[:, 1:2], ALU.max).then_inc(d_wcol, 1)
            e8 = [P, NQ, EXPERTS]
            for q in range(NQ):
                if q + 2 < NQ:
                    conv_low(q + 2)
                if q == 1:
                    dve.wait_ge(g_wmax, 1)
                    link(V.tensor_scalar(wmax[:, 1:2], wmax[:, 0:1], 1e-30, None, ALU.max))
                    link(V.reciprocal(wcol[:, 3:4], wmax[:, 1:2]))
                    link(V.tensor_scalar(scale[:, :], wmax[:, 1:2], float(HD) ** -0.5, None, ALU.mult))
                    V.tensor_tensor(wn[:, :], wcol[:, 0:1], wcol[:, 3:4], ALU.mult).then_inc(d_wscale, 1)
                if q == 5:
                    dve.wait_ge(a_lexp, 1)
                    link(V.tensor_reduce(lst[:, 1, :], le[:, :, :], AX_X, ALU.add))
                    link(V.reciprocal(lst[:, 0, :], lst[:, 1, :]))
                    link(V.tensor_tensor(le[:, :, :], le[:, :, :], lst[:, 0, :, None].broadcast_to(e8), ALU.mult))
                    dve.wait_ge(l_mix, 64)
                    link(V.tensor_tensor(mixp[:, :, :, :], mixw[:, None, :, :].broadcast_to([P, NQ, S, EXPERTS]),
                                         le[:, :, None, :].broadcast_to([P, NQ, S, EXPERTS]), ALU.mult))
                if q == 6:
                    link(V.tensor_reduce(mixa[:, :, :], mixp[:, :, :, :], AX_X, ALU.add))
                    link(V.tensor_tensor(mixb[:, :, :], le[:, :, :],
                                         vec[:, None, V_BK:V_BK + EXPERTS].broadcast_to(e8), ALU.mult))
                    link(V.tensor_reduce(aggb[:, :], mixb[:, :, :], AX_X, ALU.add))
                    V.tensor_tensor(mixf[:, :, :, :], mixa[:, :, None, :].broadcast_to([P, NQ, BQ, S]),
                                    quadmask[:, None, :, None].broadcast_to([P, NQ, BQ, S]),
                                    ALU.mult).then_inc(d_mix, 1)
                dve.wait_ge(a_cThi, q + 1)
                V.tensor_tensor(cTlo[:, q, :, :], PB[q % 2][:, :].rearrange("p (c t) -> p c t", c=KC),
                                cThi[:, q, :, :].bitcast(F32), ALU.subtract).then_inc(d_cTlo, 1)
                if q == 2:
                    dve.wait_ge(a_h2, 1)
                    V.tensor_copy(h2r[:, :, :], h2[:, :, None].broadcast_to([P, B, S])).then_inc(d_h2r, 1)
                if q == 4:
                    dve.wait_ge(t_lg, 1)
                    link(V.tensor_tensor(lg[:, :, :], PC[2][:, 0:NQ * EXPERTS].rearrange("p (q e) -> p q e", q=NQ),
                                         b2[:, None, :].broadcast_to(e8), ALU.add))
                    link(V.tensor_reduce(lst[:, 0, :], lg[:, :, :], AX_X, ALU.max))
                    V.tensor_tensor(lg[:, :, :], lg[:, :, :], lst[:, 0, :, None].broadcast_to(e8),
                                    ALU.subtract).then_inc(d_lg, 1)
            dve.wait_ge(a_mixhi, 1)
            V.tensor_tensor(mixlo[:, :, :, :], mixf[:, :, :, :], mixhi[:, :, :, :].bitcast(F32),
                            ALU.subtract).then_inc(d_mixlo, 1)

            def queries(u, t):
                dve.wait_ge(a_qsq, HQ * u + t + 1)
                V.tensor_reduce(qss[:, t, :], qsq[:, t % 2, :, :], AX_X, ALU.add).then_inc(d_qss, 1)
                if t == HQ - 1:
                    if not (isinstance(u, int) and u == 0):
                        dve.wait_ge(p_qpow, u)
                    dve.wait_ge(d_qss, HQ * u + HQ)
                    V.tensor_scalar(qms[:, :, :], qss[:, :, :], 1.0 / HD, EPS, ALU.mult, ALU.add).then_inc(d_qms, 1)

            def keys_values(u, half):
                for j in range(2):
                    dve.wait_ge(a_vhi, 2 * u + j + 1)
                    kv2 = PA[j][:, :].rearrange("p (t w) -> p t w", t=2)
                    V.tensor_tensor(vlo[:, half, 2 * j:2 * j + 2, :], kv2[:, :, HD:2 * HD],
                                    vhi[:, half, 2 * j:2 * j + 2, :].bitcast(F32), ALU.subtract).then_inc(d_vlo, 1)
                    dve.wait_ge(a_ksq, 2 * u + j + 1)
                    V.tensor_reduce(kss[:, 2 * j:2 * j + 2], ksq[:, 2 * j:2 * j + 2, :], AX_X,
                                    ALU.add).then_inc(d_kss, 1)
                if not (isinstance(u, int) and u == 0):
                    dve.wait_ge(p_kpow, u)
                dve.wait_ge(d_kss, 2 * u + 2)
                V.tensor_scalar(kms[:, :], kss[:, :], 1.0 / HD, EPS, ALU.mult, ALU.add).then_inc(d_kms, 1)

            def keys_low(u):
                dve.wait_ge(a_khi, u + 1)
                V.scalar_tensor_tensor(klo[:, :, :], PB[0][:, :].rearrange("p (b k) -> p b k", k=S), wn[:, 0:1],
                                       khi[:, :, :], ALU.mult, ALU.subtract).then_inc(d_klo, 1)

            def queries_low(u, t):
                dve.wait_ge(a_qhi, HQ * u + t + 1)
                V.tensor_tensor(qlo[:, BQ * t:BQ * t + BQ, :, :].rearrange("p b g s -> p g b s"),
                                PB[(t + 1) % 2][:, :].rearrange("p (g b s) -> p g b s", g=G, b=BQ),
                                qhi[:, BQ * t:BQ * t + BQ, :, :].rearrange("p b g s -> p g b s"),
                                ALU.subtract).then_inc(d_qlo, 1)

            def softmax(u, kv):
                first = isinstance(u, int) and u == 0
                dve.wait_ge(t_s, u + 1)
                if not first:
                    dve.wait_ge(a_exp, u)
                bias = const[:, bass.ds(kv * S + C_BIAS, S)]
                V.scalar_tensor_tensor(sc[:, :, :], PB[1][:, :].rearrange("p (b k) -> p b k", k=S), scale[:, 0:1],
                                       bias[:, None, :].broadcast_to([P, HB, S]), ALU.mult,
                                       ALU.add).then_inc(d_sc, 1)
                dve.wait_ge(d_sc, u + 1)
                V.tensor_reduce(smax[:, :], sc[:, :, :], AX_X, ALU.max).then_inc(d_smax, 1)
                dve.wait_ge(a_exp, u + 1)
                V.tensor_reduce(ssum[:, :], ex[:, :, :], AX_X, ALU.add).then_inc(d_srec, 1)
                dve.wait_ge(d_srec, 2 * u + 1)
                if not first:
                    dve.wait_ge(p_pr, u)
                V.reciprocal(srec[:, :], ssum[:, :]).then_inc(d_srec, 1)

            def probs_low(u):
                for b in range(BQ):
                    dve.wait_ge(a_pThi, BQ * u + b + 1)
                    ins = V.tensor_tensor(pTlo[S * b:S * b + S, :, :, b, :],
                                          PB[0][S * b:S * b + S, :].rearrange("p (t g s) -> p t g s", t=HQ, g=G),
                                          pThi[S * b:S * b + S, :, :, b, :].bitcast(F32), ALU.subtract)
                ins.then_inc(d_pTlo, 1)

            def outputs_low(u):
                for t in range(HQ):
                    dve.wait_ge(a_oThi, HQ * u + t + 1)
                    V.tensor_tensor(oTlo[:, t, :, :], PC[t][:, :].rearrange("p (g n) -> p g n", g=G),
                                    oThi[:, t, :, :].bitcast(F32), ALU.subtract).then_inc(d_oTlo, 1)

            def add_outputs(u, half, t):
                dve.wait_ge(t_y, HQ * u + t + 1)
                if not (isinstance(u, int) and u < 2):
                    dve.wait_ge(d_y, HQ * u - 2 * HQ + t + 1)
                q = HQ * half + t
                V.tensor_tensor(x[:, q, :], PC[t][:, :], x[:, q, :], ALU.add).then_inc(d_y, 1)

            def step(u, half, kv):
                queries(u, 0)
                softmax(u - 1, kv if half else kv - 1)
                for t in range(1, HQ):
                    queries(u, t)
                probs_low(u - 1)
                keys_values(u, half)
                outputs_low(u - 1)
                for t in range(HQ):
                    add_outputs(u - 1, 1 - half, t)
                    if t == 0:
                        keys_low(u)
                    queries_low(u, t)

            dve.wait_ge(g_zero, 2)
            for t in range(HQ):
                queries(0, t)
            keys_values(0, 0)
            keys_low(0)
            for t in range(HQ):
                queries_low(0, t)
            step(1, 1, 0)
            step(2, 0, 1)
            step(3, 1, 1)
            with dve.Fori(2, HKV) as kv:
                step(2 * kv, 0, kv)
                step(2 * kv + 1, 1, kv)

            def mix_input(q):
                dve.wait_ge(p_x2hi, q + 1)
                V.tensor_tensor(x2lo[:, q % 2, :], x[:, q, :], x2hi[:, q % 2, :].bitcast(F32),
                                ALU.subtract).then_inc(d_x2lo, 1)

            def mix_low(q):
                dve.wait_ge(a_fThi, q + 1)
                V.tensor_tensor(fTlo[:, :, P * q:P * q + P], PC[q % HQ][:, :].rearrange("p (c t) -> p c t", c=KC),
                                fThi[:, :, P * q:P * q + P].bitcast(F32), ALU.subtract).then_inc(d_fTlo, 1)

            def weights_low(i, slot):
                dve.wait_ge(l_guw, 48 * i + 48)
                if not (isinstance(i, int) and i == 0):
                    dve.wait_ge(d_gulo, i)
                V.tensor_tensor(guf[:, :, :, :], guw[:, :, :, :], guz[:, :, :, :], ALU.subtract).then_inc(d_gsub, 1)
                dve.wait_ge(a_guhi, i + 1)
                V.tensor_tensor(gulo[:, slot, :, :, :], guf[:, :, :, :], guhi[:, slot, :, :, :].bitcast(F32),
                                ALU.subtract).then_inc(d_gulo, 1)

            def hidden(i, first):
                for half in range(2):
                    dve.wait_ge(t_u, 2 * i + half + 1)
                    dve.wait_ge(a_silu, 2 * i + half + 1)
                    if not (first and half == 0):
                        dve.wait_ge(p_hlo, 2 * i + half)
                    V.tensor_tensor(hf[:, :], silu[:, :], PC[half][:, :], ALU.mult).then_inc(d_h, 1)

            softmax(UNITS - 1, HKV - 1)
            mix_input(0)
            mix_input(1)
            mix_input(2)
            mix_low(0)
            mix_input(3)
            mix_low(1)
            mix_low(2)
            probs_low(UNITS - 1)
            mix_low(3)
            weights_low(0, 0)
            weights_low(1, 1)
            outputs_low(UNITS - 1)
            for t in range(HQ):
                add_outputs(UNITS - 1, 1, t)
            mix_input(4)
            mix_input(5)
            for q in range(HQ, NQ):
                if q + 2 < NQ:
                    mix_input(q + 2)
                mix_low(q)
            hidden(0, True)
            with dve.Fori(1, IC - 1, 2) as i:
                weights_low(i + 1, 0)
                hidden(i, False)
                weights_low(i + 2, 1)
                hidden(i + 1, False)

            def down_low(i, slot, loaded, first):
                dve.wait_ge(loaded, 24 * i - 24 * slot + 48)
                if first:
                    dve.wait_ge(d_gulo, IC)
                else:
                    dve.wait_ge(d_dlo, i - 1)
                V.tensor_tensor(guf[:, slot, :, :], guw[:, slot, :, :], guz[:, slot, :, :],
                                ALU.subtract).then_inc(d_dsub, 1)
                dve.wait_ge(a_dhi, i + 1)
                V.tensor_tensor(gulo[:, slot, 0, :, :], guf[:, slot, :, :], guhi[:, slot, 0, :, :].bitcast(F32),
                                ALU.subtract).then_inc(d_dlo, 1)

            down_low(0, 0, l_dn0, True)
            hidden(IC - 1, False)
            down_low(1, 1, l_dn1, True)
            with dve.Fori(2, IC, 2) as i:
                down_low(i, 0, l_dn0, False)
                down_low(i + 1, 1, l_dn1, False)
            for q in range(NQ):
                dve.wait_ge(t_acc, q + 1)
                V.tensor_tensor(x[:, q, :], bank[q][:, :], x[:, q, :], ALU.add).then_inc(d_res, 1)

        @block.gpsimd
        def _(pool):
            Q = nc.gpsimd
            for t in (xhi, xlo):
                Q.memset(t[:, :, 0:PAD].bitcast(F32), 0.0).then_inc(g_pad, 1)
                Q.memset(t[:, :, PAD + DM:XW].bitcast(F32), 0.0).then_inc(g_pad, 1)
            pool.wait_ge(d_wcol, 2)
            Q.partition_all_reduce(wmax[:, 0:1], wcol[:, 2:3], P, bass.bass_isa.ReduceOp.max).then_inc(g_wmax, 1)

            def split_wq(kv):
                for c in range(KC):
                    pool.wait_ge(a_wq, KC * kv + c + 1)
                    Q.tensor_tensor(wqlo[:, c, :], wqr[:, c, :], wqhi[:, c, :].bitcast(F32),
                                    ALU.subtract).then_inc(p_wq, 1)

            def split_wkv(kv):
                for c in range(0, KC, 2):
                    pool.wait_ge(a_wkv, 2 * kv + c // 2 + 1)
                    Q.tensor_tensor(wkvlo[:, c:c + 2, :], wkvr[:, c:c + 2, :], wkvhi[:, c:c + 2, :].bitcast(F32),
                                    ALU.subtract).then_inc(p_wkv, 1)

            def split_wo(kv):
                for g in range(G):
                    pool.wait_ge(a_wo, G * kv + g + 1)
                    Q.tensor_tensor(wolo[:, g, :], wor[:, g, :], wohi[:, g, :].bitcast(F32),
                                    ALU.subtract).then_inc(p_wo, 1)

            def queries(u):
                pool.wait_ge(d_qms, u + 1)
                Q.tensor_tensor(qinv[:, :, :], qms[:, :, :], neghalf[:, :, :], ALU.pow).then_inc(p_qpow, 1)
                pool.wait_ge(p_qpow, u + 1)
                for t in range(HQ):
                    if not (isinstance(u, int) and u == 0):
                        pool.wait_ge(t_qT, HQ * u - HQ + t + 1)
                    Q.tensor_tensor(qn[:, t, :, :], qraw[:, t, :, :],
                                    qinv[:, t, :, None].broadcast_to([P, G, HD]), ALU.mult).then_inc(p_qn, 1)

            def keys_values(u):
                pool.wait_ge(d_kms, u + 1)
                Q.tensor_tensor(kinv[:, :], kms[:, :], neghalf[:, :, 0], ALU.pow).then_inc(p_kpow, 1)
                pool.wait_ge(p_kpow, u + 1)
                if not (isinstance(u, int) and u == 0):
                    pool.wait_ge(t_kT, u)
                Q.tensor_tensor(kn[:, :, :], kraw[:, :, :], kinv[:, :, None].broadcast_to([P, HQ, HD]),
                                ALU.mult).then_inc(p_kn, 1)

            def softmax(u):
                pool.wait_ge(d_smax, u + 1)
                Q.tensor_tensor(sc[:, :, :], sc[:, :, :], smax[:, :, None].broadcast_to([P, HB, S]),
                                ALU.subtract).then_inc(p_sub, 1)
                pool.wait_ge(d_srec, 2 * u + 2)
                if not (isinstance(u, int) and u == 0):
                    pool.wait_ge(t_pT, u)
                Q.tensor_tensor(pr[:, :, :], ex[:, :, :], srec[:, :, None].broadcast_to([P, HB, S]),
                                ALU.mult).then_inc(p_pr, 1)

            def step(u, half, kv, last):
                softmax(u - 1)
                if half:
                    split_wo(kv)
                queries(u)
                keys_values(u)
                if half and not last:
                    split_wq(kv + 1)
                    split_wkv(kv + 1)

            split_wq(0)
            split_wkv(0)
            pool.wait_ge(t_cT, NQ)
            pool.wait_ge(d_mixlo, 1)
            Q.memset(pThi[:, :, :, :, :].bitcast(F32), 0.0).then_inc(g_zero, 1)
            Q.memset(pTlo[:, :, :, :, :].bitcast(F32), 0.0).then_inc(g_zero, 1)
            pool.wait_ge(g_zero, 2)
            queries(0)
            keys_values(0)
            step(1, 1, 0, False)
            with pool.Fori(1, HKV - 1) as kv:
                step(2 * kv, 0, kv, False)
                step(2 * kv + 1, 1, kv, False)
            step(UNITS - 2, 0, HKV - 1, True)
            step(UNITS - 1, 1, HKV - 1, True)

            def mix_input(q):
                if q < HQ:
                    pool.wait_ge(d_y, HQ * (UNITS - 1))
                    pool.wait_ge(t_qT, HQ * UNITS)
                else:
                    pool.wait_ge(d_y, HQ * (UNITS - 1) + q - HQ + 1)
                if q >= 2:
                    pool.wait_ge(t_f, q - 1)
                Q.tensor_copy(x2hi[:, q % 2, :], x[:, q, :]).then_inc(p_x2hi, 1)

            def scale_gu(i):
                pool.wait_ge(d_gsub, i + 1)
                Q.tensor_tensor(guf[:, :, :, :], guf[:, :, :, :], gus[:, :, :, :], ALU.mult).then_inc(p_gmul, 1)

            def hidden_low(i):
                for half in range(2):
                    pool.wait_ge(a_hhi, 2 * i + half + 1)
                    Q.tensor_tensor(hTlo[:, i, HT * half:HT * half + HT], hf[:, :],
                                    hThi[:, i, HT * half:HT * half + HT].bitcast(F32),
                                    ALU.subtract).then_inc(p_hlo, 1)

            mix_input(0)
            mix_input(1)
            softmax(UNITS - 1)
            mix_input(2)
            mix_input(3)
            scale_gu(0)
            scale_gu(1)
            for q in range(HQ, NQ):
                mix_input(q)
            hidden_low(0)
            with pool.Fori(1, IC - 1) as i:
                scale_gu(i + 1)
                hidden_low(i)

            def scale_dn(i, slot):
                pool.wait_ge(d_dsub, i + 1)
                Q.tensor_tensor(guf[:, slot, :, :], guf[:, slot, :, :], gus[:, slot, :, :],
                                ALU.mult).then_inc(p_dmul, 1)

            scale_dn(0, 0)
            hidden_low(IC - 1)
            scale_dn(1, 1)
            with pool.Fori(2, IC, 2) as i:
                scale_dn(i, 0)
                scale_dn(i + 1, 1)


def kernel(**inputs):
    import concourse.bacc as _bacc
    from concourse import mybir as _mybir
    from concourse.bass_utils import run_bass_kernel_spmd as _run

    a = {k: np.asarray(v) for k, v in inputs.items()}

    def tile_gu(w):
        return w.reshape(KC, P, IC, P).transpose(2, 1, 0, 3)

    def row_gu(w):
        return w.reshape(KC, IC, P).transpose(1, 0, 2)

    wk = a["L0_attn_Wk"].reshape(HKV, HD, KC, P).transpose(0, 3, 2, 1)
    wv = a["L0_attn_Wv"].reshape(HKV, HD, KC, P).transpose(0, 3, 2, 1)
    vec = np.concatenate([
        np.stack([a["L0_cond2_b0"], a["L0_cond2_b1"], a["L0_attn_q_norm_w"], a["L0_attn_k_norm_w"],
                  np.tile(a["fside_S_0"], BQ)], axis=1),
        np.tile(a["L0_cond2_bias_k"].T, (BQ, 1))], axis=1)
    arrays = {
        "x": a["x"].reshape(NQ, P, DM).transpose(1, 0, 2),
        "cond": a["cond_128"].T,
        "cw": a["L0_cond_c_weight"].T,
        "conv": a["L0_cond_weight"].reshape(S // CG, CG, CG, TAPS).transpose(0, 2, 3, 1).reshape(S, TAPS, CG),
        "wq": a["L0_attn_Wq"].reshape(HKV, G * HD, KC, P).transpose(0, 3, 2, 1),
        "wkv": np.concatenate([wk, wv], axis=3),
        "wo": a["L0_attn_Wo"].T.reshape(HKV, G, HD, DM).transpose(0, 2, 1, 3) if a["L0_attn_Wo"].shape[0] == DM else None,
        "w0": a["L0_cond2_W0"], "w1": a["L0_cond2_W1"], "w2": a["L0_cond2_W2"],
        "b2": a["L0_cond2_b2"].reshape(1, EXPERTS),
        "mix": a["L0_cond2_weight"][..., 0].transpose(2, 1, 0),
        "vec": vec,
        "gu_w": np.stack([tile_gu(a["L0_ffn_gate_w"]), tile_gu(a["L0_ffn_up_w"])], axis=2),
        "gu_z": np.stack([row_gu(a["L0_ffn_gate_z"]), row_gu(a["L0_ffn_up_z"])], axis=1).reshape(IC, 1, 2 * KC * P),
        "gu_s": np.stack([row_gu(a["L0_ffn_gate_s"]), row_gu(a["L0_ffn_up_s"])], axis=1).reshape(IC, 1, 2 * KC * P),
        "dn_w": a["L0_ffn_down_w"].reshape(IC, P, DM),
        "dn_z": a["L0_ffn_down_z"].reshape(IC, 1, DM),
        "dn_s": a["L0_ffn_down_s"].reshape(IC, 1, DM),
        "consts": constants(),
    }
    nc = _bacc.Bacc("TRN2", target_bir_lowering=False, num_devices=1)
    feed, args = {}, []
    for name, v in arrays.items():
        v = np.ascontiguousarray(v)
        feed[f"in_{name}"] = v
        args.append(nc.dram_tensor(f"in_{name}", v.shape, _mybir.dt.from_np(v.dtype), kind="ExternalInput").ap())
    o = nc.dram_tensor("result", (P, NQ, DM), _mybir.dt.float32, kind="ExternalOutput").ap()
    build(nc, *args, o)
    r = _run(nc, [feed], core_ids=[0])
    return np.asarray(r.results[0]["result"]).transpose(1, 0, 2).reshape(B, S, DM)
```

```python
from contextlib import ExitStack

import numpy as np

import concourse.bass as bass
from concourse import mybir

P = 128
B, S, DM = 32, 32, 512
H, HKV, HD = 32, 8, 128
G = H // HKV
KC = DM // P
BQ = P // S
NQ = B // BQ
HQ = NQ // 2
HB = B // 2
HT = HB * S
TAPS = 9
CG = 8
NGRP = S // CG
PH = KC
SHIFTS = 3
EXPERTS = 8
INNER = 1792
IC = INNER // P
EXACT = 3
UNITS = 2 * HKV
EPS = 1e-6
MASKED = -1e30

F32 = mybir.dt.float32
F32R = mybir.dt.float32r
F16 = mybir.dt.float16
I32 = mybir.dt.int32
ALU = mybir.AluOpType
ACT = mybir.ActivationFunctionType
AX_X = mybir.AxisListType.X

C_ID, C_BIAS, C_QUAD = 0, P, P + HKV * S
C_ALL = C_QUAD + BQ
V_B0, V_B1, V_QW, V_KW, V_BK = 0, 1, 2, 3, 4
V_ALL = V_BK + EXPERTS


def constants():
    t = np.zeros((P, C_ALL), np.float32)
    t[:, C_ID:C_ID + P] = np.eye(P, dtype=np.float32)
    start = 2 ** (-2 ** (-(np.log2(H) - 3)))
    slopes = np.array([start * start ** i for i in range(H)], np.float32).reshape(HKV, G)
    pos = np.arange(S, dtype=np.float32)
    rel = pos[None, :] - pos[:, None]
    bias = np.where(rel > 0, np.float32(MASKED), slopes[:, :, None, None] * rel)
    t[:, C_BIAS:C_QUAD] = bias.transpose(1, 2, 0, 3).reshape(P, HKV * S)
    p = np.arange(P)
    t[:, C_QUAD:C_ALL] = p[:, None] // S == np.arange(BQ)
    return t


def group_mask():
    p = np.arange(P)
    return (p[:, None] % S // CG == np.arange(NGRP)).astype(np.float32)


def build(nc, x_in, xt_in, mask_in, fs_in, cond_in, cw_in, conv_in, wq_in, wkv_in, wo_in, w0_in, w1_in, w2_in, b2_in, mix_in, vec_in,
          gu_w_in, gu_z_in, gu_s_in, dn_w_in, dn_z_in, dn_s_in, const_in, out):
    ctx = ExitStack()
    with ctx:
        def sb(name, shape, dt=F32, where=ctx):
            return where.enter_context(nc.sbuf_tensor(name, shape, dt))

        def sem(name):
            return ctx.enter_context(nc.semaphore(name))

        bank = [ctx.enter_context(nc.psum_tensor(f"bank{i}", [P, DM], F32)) for i in range(8)]
        PA, PB, PC = bank[0:2], bank[2:4], bank[4:8]

        x = sb("x", [P, NQ, DM])
        const = sb("const", [P, C_ALL])
        vec = sb("vec", [P, V_ALL])
        aggb = sb("aggb", [P, NQ])
        ident = const[:, C_ID:C_ID + P]
        quadmask = const[:, C_QUAD:C_ALL]

        gus = sb("gus", [P, IC, 2, KC])
        neghalf = sb("neghalf", [P, HQ, G])
        wcol = sb("wcol", [P, 4])
        wmax = sb("wmax", [P, 2])
        wn = sb("wn", [P, 1])
        scale = sb("scale", [P, 1])

        mixing = ExitStack()
        mixhi = sb("mixhi", [P, NQ, BQ, S], F32R, mixing)
        mixlo = sb("mixlo", [P, NQ, BQ, S], F32R, mixing)

        proj = ExitStack()
        wqr = sb("wqr", [P, KC, DM], F32, proj)
        wkvr = sb("wkvr", [P, KC, 2 * HD], F32, proj)
        wqhi = sb("wqhi", [P, KC, DM], F32R, proj)
        wqlo = sb("wqlo", [P, KC, DM], F32R, proj)
        wkvhi = sb("wkvhi", [P, KC, 2 * HD], F32R, proj)
        wkvlo = sb("wkvlo", [P, KC, 2 * HD], F32R, proj)
        att = ExitStack()
        cThi = sb("cThi", [P, NQ, KC, P], F32R, att)
        cTlo = sb("cTlo", [P, NQ, KC, P], F32R, att)
        qraw = sb("qraw", [P, HQ, G, HD], F32, att)
        qsq = sb("qsq", [P, 2, G, HD], F32, att)
        qn = sb("qn", [P, HQ, G, HD], F32, att)
        wor = sb("wor", [P, G, DM], F32, att)
        gates = ExitStack()
        lg = sb("lg", [P, NQ, EXPERTS], F32, gates)
        le = sb("le", [P, NQ, EXPERTS], F32, gates)
        lst = sb("lst", [P, 2, NQ], F32, gates)
        mixw = sb("mixw", [P, S, EXPERTS], F32, gates)
        mixp = sb("mixp", [P, NQ, S, EXPERTS], F32, gates)
        mixa = sb("mixa", [P, NQ, S], F32, gates)
        mixb = sb("mixb", [P, NQ, EXPERTS], F32, gates)
        mixf = sb("mixf", [P, NQ, BQ, S], F32, gates)
        gates.close()
        wohi = sb("wohi", [P, G, DM], F32R, att)
        wolo = sb("wolo", [P, G, DM], F32R, att)
        qss = sb("qss", [P, HQ, G], F32, att)
        qms = sb("qms", [P, HQ, G], F32, att)
        kms = sb("kms", [P, HQ], F32, att)
        qinv = sb("qinv", [P, HQ, G], F32, att)
        kraw = sb("kraw", [P, HQ, HD], F32, att)
        ksq = sb("ksq", [P, HQ, HD], F32, att)
        kn = sb("kn", [P, HQ, HD], F32, att)
        kss = sb("kss", [P, HQ], F32, att)
        kinv = sb("kinv", [P, HQ], F32, att)
        qhi = sb("qhi", [P, HB, G, S], F16, att)
        qlo = sb("qlo", [P, HB, G, S], F16, att)
        khi = sb("khi", [P, HB, S], F16, att)
        klo = sb("klo", [P, HB, S], F16, att)
        vhi = sb("vhi", [P, 2, HQ, HD], F32R, att)
        vlo = sb("vlo", [P, 2, HQ, HD], F32R, att)
        early = ExitStack()
        xT = sb("xT", [P, B, P + 2], F32, early)
        cwr = sb("cwr", [P, SHIFTS, PH, CG], F32, early)
        cwf = sb("cwf", [P, SHIFTS, PH, NGRP, CG], F32, early)
        mask = sb("mask", [P, NGRP], F32, early)
        fs = sb("fs", [P, S], F32, early)
        condT = sb("condT", [P, B], F32, early)
        cwT = sb("cwT", [P, S], F32, early)
        ones = sb("ones", [P, P], F32, early)
        ctxr = sb("ctxr", [P, B, S], F32, early)
        ctxb = sb("ctxb", [P, B, S], F32, early)
        cf = sb("cf", [P, 2, PH, BQ, S], F32, early)
        w0 = sb("w0", [P, P], F32, early)
        w1 = sb("w1", [P, P], F32, early)
        w2 = sb("w2", [P, EXPERTS], F32, early)
        b2 = sb("b2", [P, EXPERTS], F32, early)
        h1 = sb("h1", [P, B], F32, early)
        h2 = sb("h2", [P, B], F32, early)
        h2r = sb("h2r", [P, B, S], F32, early)
        early.close()
        sc = sb("sc", [P, HB, S], F32, att)
        ex = sb("ex", [P, HB, S], F32, att)
        pr = sb("pr", [P, HB, S], F32, att)
        smax = sb("smax", [P, HB], F32, att)
        ssum = sb("ssum", [P, HB], F32, att)
        srec = sb("srec", [P, HB], F32, att)
        pThi = sb("pThi", [P, HQ, G, BQ, S], F32R, att)
        pTlo = sb("pTlo", [P, HQ, G, BQ, S], F32R, att)
        oThi = sb("oThi", [P, HQ, G, P], F32R, att)
        oTlo = sb("oTlo", [P, HQ, G, P], F32R, att)
        att.close()
        proj.close()
        mixing.close()

        ffn = ExitStack()
        dnhi = sb("dnhi", [P, 2, DM], F32R, ffn)
        dnlo = sb("dnlo", [P, 2, DM], F32R, ffn)
        guw = sb("guw", [P, 2, KC, P], I32, ffn)
        guz = sb("guz", [P, 2, KC, P], I32, ffn)
        gun = sb("gun", [P, 2, 2, KC, P], F32R, ffn)
        part = sb("part", [P, 2, HT], F32, ffn)
        whole = sb("whole", [P, 2, 2, HT], F32, ffn)
        scl = sb("scl", [P, 2, 2, KC], F32, ffn)
        hf = sb("hf", [P, 2, HT], F32, ffn)
        dns = sb("dns", [P, 2, DM], F32, ffn)
        fThi = sb("fThi", [P, KC, NQ * P], F32R, ffn)
        fTlo = sb("fTlo", [P, KC, NQ * P], F32R, ffn)
        mixwork = ExitStack()
        spare = sb("spare", [P, 3 * HT], F32, mixwork)
        x2hi = sb("x2hi", [P, 2, DM], F32R, mixwork)
        x2lo = sb("x2lo", [P, 2, DM], F32R, mixwork)
        fnat = sb("fnat", [P, 2, DM], F32, mixwork)
        mixwork.close()
        hThi = sb("hThi", [P, IC, NQ * P], F32R, ffn)
        hTlo = sb("hTlo", [P, IC, NQ * P], F32R, ffn)
        ffn.close()

        l_xt0 = sem("l_xt0")
        l_xt1 = sem("l_xt1")
        l_xt2 = sem("l_xt2")
        l_xt3 = sem("l_xt3")
        l_x = sem("l_x")
        l_const = sem("l_const")
        l_vec = sem("l_vec")
        l_cond = sem("l_cond")
        l_conv = sem("l_conv")
        l_mlp = sem("l_mlp")
        l_mix = sem("l_mix")
        l_wq = sem("l_wq")
        l_wkv = sem("l_wkv")
        l_wo = sem("l_wo")
        l_gus = sem("l_gus")
        l_gate = sem("l_gate")
        l_up = sem("l_up")
        l_dn0 = sem("l_dn0")
        l_dn1 = sem("l_dn1")
        d_mixlo = sem("d_mixlo")
        l_out = sem("l_out")
        g_pad = sem("g_pad")
        g_wmax = sem("g_wmax")
        g_zero = sem("g_zero")
        d_ones = sem("d_ones")
        d_ctxr = sem("d_ctxr")
        d_ctxb = sem("d_ctxb")
        d_cf = sem("d_cf")
        d_wcol = sem("d_wcol")
        d_wscale = sem("d_wscale")
        d_cwf = sem("d_cwf")
        d_cTlo = sem("d_cTlo")
        d_h2r = sem("d_h2r")
        d_lg = sem("d_lg")
        d_mix = sem("d_mix")
        d_self = sem("d_self")
        a_cThi = sem("a_cThi")
        a_h1 = sem("a_h1")
        a_h2 = sem("a_h2")
        a_lexp = sem("a_lexp")
        a_mixhi = sem("a_mixhi")
        t_ctx = sem("t_ctx")
        t_h1 = sem("t_h1")
        t_h2 = sem("t_h2")
        t_lg = sem("t_lg")
        t_conv = sem("t_conv")
        a_wq = sem("a_wq")
        a_wkv = sem("a_wkv")
        a_wo = sem("a_wo")
        p_wq = sem("p_wq")
        p_wkv = sem("p_wkv")
        p_wo = sem("p_wo")
        t_q = sem("t_q")
        t_kv = sem("t_kv")
        t_kT = sem("t_kT")
        t_qT = sem("t_qT")
        t_s = sem("t_s")
        t_pT = sem("t_pT")
        t_pv = sem("t_pv")
        t_y = sem("t_y")
        a_qraw = sem("a_qraw")
        a_qsq = sem("a_qsq")
        d_qss = sem("d_qss")
        d_qms = sem("d_qms")
        d_kms = sem("d_kms")
        p_qpow = sem("p_qpow")
        p_qn = sem("p_qn")
        a_kraw = sem("a_kraw")
        a_ksq = sem("a_ksq")
        d_kss = sem("d_kss")
        p_kpow = sem("p_kpow")
        p_kn = sem("p_kn")
        a_vhi = sem("a_vhi")
        d_vlo = sem("d_vlo")
        a_khi = sem("a_khi")
        d_klo = sem("d_klo")
        a_qhi = sem("a_qhi")
        d_qlo = sem("d_qlo")
        d_sc = sem("d_sc")
        d_smax = sem("d_smax")
        p_sub = sem("p_sub")
        a_exp = sem("a_exp")
        d_srec = sem("d_srec")
        p_pr = sem("p_pr")
        a_pThi = sem("a_pThi")
        d_pTlo = sem("d_pTlo")
        a_oThi = sem("a_oThi")
        d_oTlo = sem("d_oTlo")
        d_y = sem("d_y")
        a_x2hi = sem("a_x2hi")
        d_x2lo = sem("d_x2lo")
        t_f = sem("t_f")
        a_fnat = sem("a_fnat")
        t_fT = sem("t_fT")
        a_fThi = sem("a_fThi")
        d_fTlo = sem("d_fTlo")
        d_gun = sem("d_gun")
        t_gu = sem("t_gu")
        d_scl = sem("d_scl")
        a_part = sem("a_part")
        d_part = sem("d_part")
        p_whole = sem("p_whole")
        a_silu = sem("a_silu")
        d_h = sem("d_h")
        a_hhi = sem("a_hhi")
        p_hlo = sem("p_hlo")
        d_dsub = sem("d_dsub")
        p_dmul = sem("p_dmul")
        a_dhi = sem("a_dhi")
        d_dlo = sem("d_dlo")
        t_dn = sem("t_dn")
        t_dint = sem("t_dint")
        d_prod = sem("d_prod")
        d_sum = sem("d_sum")
        p_sum = sem("p_sum")
        t_acc = sem("t_acc")
        d_res = sem("d_res")

        def chain(eng, sm, start=0):
            n = [start]

            def link(ins):
                n[0] += 1
                ins.then_inc(sm, 1)
                eng.wait_ge(sm, n[0])
            return link

        def quads(u_half):
            return range(HQ * u_half, HQ * u_half + HQ)

        start_tiles = ((0, 0), (1, 0), (0, 1), (1, 1))

        def tile_of(i, half):
            return start_tiles.index((i, half)) if isinstance(i, int) and i < 2 else 2 * i + half

        def tile_before(i, half, by=1):
            if isinstance(i, int) and tile_of(i, half) - by < len(start_tiles):
                return start_tiles[tile_of(i, half) - by]
            if by == 2:
                return i - 1, half
            return (i, 0) if half else (i - 1, 1)

        def gate_up_bank(n, k):
            if isinstance(n, int) and n < 2:
                return PB[k % 2] if n else (PA + PC + PA)[k]
            return bank[k]

        def down_ints(slot, place):
            return gun[:, slot, place, :, :].rearrange("p b c -> p (b c)")

        def down_weights(i, slot):
            if isinstance(i, int) and i < 2:
                return guw[:, slot, :, :].rearrange("p b c -> p (b c)").bitcast(F32)
            return hf[:, slot, :]

        def down_scales(slot, place):
            return part[:, slot, :] if place else dns[:, slot, :]

        def down_product(q):
            return whole[:, q // 2, q % 2, :]

        def queries_after(t):
            return ((0,), (1, 2), (3,), ())[t]

        def query_bank(u, t):
            return PC[t - 1] if isinstance(u, int) and u == 0 and t else PB[(t + 1) % 2]

        def tile_slot(i, half):
            n = tile_of(i, half)
            return n % 2 if isinstance(n, int) else half

        def tokens(half):
            return slice(HT * half, HT * half + HT)

        block = ctx.enter_context(nc.Block())

        @block.sync
        def _(sp):
            sp.dma_start(mask[:, :], mask_in).then_inc(l_conv, 16)
            sp.dma_start(cwr[:, :, :, :], conv_in).then_inc(l_conv, 16)

            def load_xt(first, end, loaded):
                sp.dma_start(xT[:, BQ * first:BQ * end, 1:P + 1], xt_in[:, BQ * first:BQ * end, :]).then_inc(loaded, 16)

            load_xt(0, 1, l_xt0)
            sp.dma_start(condT[:, :], cond_in).then_inc(l_cond, 16)
            sp.dma_start(cwT[:, :], cw_in).then_inc(l_cond, 16)
            sp.dma_start(fs[:, :], fs_in.broadcast_to([P, S])).then_inc(l_cond, 16)
            load_xt(1, 2, l_xt1)
            sp.dma_start(vec[:, :], vec_in).then_inc(l_vec, 16)
            load_xt(2, 4, l_xt2)
            for dst, src in ((w0, w0_in), (w1, w1_in), (w2, w2_in)):
                sp.dma_start(dst[:, :], src).then_inc(l_mlp, 16)
            sp.dma_start(b2[:, :], b2_in.broadcast_to([P, EXPERTS])).then_inc(l_mlp, 16)
            load_xt(4, NQ, l_xt3)

            def load_heads(kv, first):
                if not first:
                    sp.wait_ge(p_wq, KC * kv)
                sp.dma_start(wqr[:, :, :], wq_in[kv]).then_inc(l_wq, 16)
                if not first:
                    sp.wait_ge(p_wkv, 2 * kv)
                sp.dma_start(wkvr[:, :, :], wkv_in[kv]).then_inc(l_wkv, 16)
                if not first:
                    sp.wait_ge(p_wo, G * kv)
                sp.dma_start(wor[:, :, :], wo_in[kv]).then_inc(l_wo, 16)

            load_heads(0, True)
            sp.dma_start(const[:, :], const_in).then_inc(l_const, 16)
            for b in range(BQ):
                sp.dma_start(mixw[S * b:S * b + S, :, :], mix_in).then_inc(l_mix, 16)
            sp.dma_start(x[:, :, :], x_in).then_inc(l_x, 16)
            sp.dma_start(gus[:, :, :, :], gu_s_in).then_inc(l_gus, 16)
            with sp.Fori(1, HKV) as kv:
                load_heads(kv, False)

            sp.wait_ge(p_wq, KC * HKV)
            sp.wait_ge(p_wkv, 2 * HKV)
            sp.wait_ge(t_kv, 2 * UNITS)

            def load_gu(i, first):
                for j, loaded in ((0, l_gate), (1, l_up)):
                    if not first:
                        sp.wait_ge(d_gun, 2 * i - 1 + j)
                    sp.dma_start(guw[:, j, :, :], gu_w_in[i][:, j, :, :]).then_inc(loaded, 16)
                    sp.dma_start(guz[:, j, :, :].rearrange("p b c -> p (b c)"),
                                 gu_z_in[i][:, DM * j:DM * j + DM].broadcast_to([P, DM])).then_inc(loaded, 16)

            load_gu(0, True)
            with sp.Fori(1, IC) as i:
                load_gu(i, False)

            def load_dn(i, slot, place, loaded):
                if isinstance(i, int) and i < 2:
                    sp.wait_ge(d_gun, 2 * IC - 1 + slot)
                else:
                    sp.wait_ge(d_dsub, i - 1)
                    if isinstance(i, int) and i < 4:
                        sp.wait_ge(d_dlo, i - 1)
                sp.dma_start(guw[:, slot, :, :].rearrange("p b c -> p (b c)"), dn_w_in[i]).then_inc(loaded, 16)
                sp.dma_start(guz[:, slot, :, :].rearrange("p b c -> p (b c)"),
                             dn_z_in[i].broadcast_to([P, DM])).then_inc(loaded, 16)
                if isinstance(i, int) and i in (2, 3):
                    sp.wait_ge(p_whole, 4 * IC)
                elif not (isinstance(i, int) and i < 2):
                    sp.wait_ge(d_prod, EXACT * i - 3 * EXACT)
                sp.dma_start(down_scales(slot, place), dn_s_in[i].broadcast_to([P, DM])).then_inc(loaded, 16)

            for i in range(6):
                load_dn(i, i % 2, i // 2 % 2, (l_dn0, l_dn1)[i % 2])
            with sp.Fori(0, (IC - 6) // 4) as four:
                load_dn(4 * four + 6, 0, 1, l_dn0)
                load_dn(4 * four + 7, 1, 1, l_dn1)
                load_dn(4 * four + 8, 0, 0, l_dn0)
                load_dn(4 * four + 9, 1, 0, l_dn1)
            for q in range(NQ):
                if q == 0:
                    sp.wait_ge(d_sum, IC)
                elif q < EXACT:
                    sp.wait_ge(p_sum, 2 * IC - 2 + q)
                else:
                    sp.wait_ge(d_res, q - EXACT + 1)
                sp.dma_start(out[:, q, :], x[:, q, :]).then_inc(l_out, 16)
            sp.wait_ge(l_out, 16 * NQ)

        @block.tensor
        def _(pe):
            mm = nc.tensor.matmul

            def split_product(o, parts, start, stop):
                n = len(parts)
                for k, (ahi, alo, bhi, blo) in enumerate(parts):
                    mm(o, ahi, bhi, start=start and k == 0, stop=False)
                    mm(o, ahi, blo, start=False, stop=False)
                    last = mm(o, alo, bhi, start=False, stop=stop and k == n - 1)
                return last

            def context():
                pe.wait_ge(d_ctxr, 1)
                for h in range(2):
                    mm(PC[h][:, :], ones[:, :], ctxr[:, HB * h:HB * h + HB, :], start=True, stop=True).then_inc(t_ctx, 1)

            def gate_layer1():
                pe.wait_ge(l_mlp, 64)
                mm(PC[2][:, 0:B], w0[:, :], condT[:, :], start=True, stop=True).then_inc(t_h1, 1)

            def gate_layer2():
                pe.wait_ge(a_h1, 1)
                mm(PC[2][:, 0:B], w1[:, :], h1[:, :], start=True, stop=True).then_inc(t_h2, 1)

            def gate_logits():
                pe.wait_ge(d_h2r, 1)
                for q in range(NQ):
                    last = mm(PC[3][:, EXPERTS * q:EXPERTS * q + EXPERTS], h2r[:, BQ * q:BQ * q + BQ, :], w2[:, :],
                              start=True, stop=True)
                last.then_inc(t_lg, 1)

            pe.wait_ge(d_ones, 1)
            for _ in range(8):
                mm(PC[3][:, 0:P], ones[:, :], ones[:, :], start=True, stop=True)
            arrived = (l_xt0, l_xt1, l_xt2, l_xt2, l_xt3, l_xt3, l_xt3, l_xt3)
            pe.wait_ge(d_cwf, 1)
            pe.wait_ge(g_pad, 2)
            for q in range(NQ):
                pe.wait_ge(arrived[q], 16)
                if q >= 2:
                    pe.wait_ge(d_cf, q - 1)
                out4 = PA[q % 2][:, :].rearrange("p (c b s) -> p c b s", c=PH, b=BQ)
                for b in range(BQ):
                    for j in range(SHIFTS):
                        last = mm(out4[:, :, b, :], xT[:, BQ * q + b, j:j + P], cwf[:, j, :, :, :],
                                  start=j == 0, stop=j == SHIFTS - 1)
                last.then_inc(t_conv, 1)
                if q == 0:
                    context()
                elif q == 2:
                    gate_layer1()
                elif q == 4:
                    gate_layer2()

            def project_q(u, half, kv, t):
                if half == 0 and t == 0:
                    pe.wait_ge(p_wq, KC * kv + KC)
                if t >= 2:
                    pe.wait_ge(a_qraw, HQ * u + t - 1)
                elif not (isinstance(u, int) and u == 0):
                    pe.wait_ge(d_vlo, 2 * u)
                    pe.wait_ge(a_kraw, 2 * u)
                tq = HQ * half + t
                split_product(PA[t % 2][:, :],
                              [(cThi[:, tq, c, :], cTlo[:, tq, c, :], wqhi[:, c, :], wqlo[:, c, :])
                               for c in range(KC)], True, True).then_inc(t_q, 1)

            def project_kv(u, half, kv, pairs=(0, 1)):
                if half == 0:
                    pe.wait_ge(p_wkv, 2 * kv + 2)
                for j in pairs:
                    pe.wait_ge(a_qraw, HQ * u + 3 + j)
                    for t in (2 * j, 2 * j + 1):
                        tq = HQ * half + t
                        last = split_product(PA[j][:, 2 * HD * (t % 2):2 * HD * (t % 2) + 2 * HD],
                                             [(cThi[:, tq, c, :], cTlo[:, tq, c, :], wkvhi[:, c, :], wkvlo[:, c, :])
                                              for c in range(KC)], True, True)
                    last.then_inc(t_kv, 1)

            def transpose_k(u):
                if isinstance(u, int) and u == 0:
                    pe.wait_ge(l_const, 16)
                pe.wait_ge(p_kn, u + 1)
                if not (isinstance(u, int) and u == 0):
                    pe.wait_ge(d_pTlo, u)
                for t in range(HQ):
                    last = nc.tensor.transpose(PB[0][:, P * t:P * t + P], kn[:, t, :], ident)
                last.then_inc(t_kT, 1)

            def transpose_q(u, t):
                pe.wait_ge(p_qn, HQ * u + t + 1)
                if isinstance(u, int) and u == 0:
                    pe.wait_ge(d_ctxb, 2)
                elif t == 0:
                    pe.wait_ge(d_sc, u)
                elif t == 1:
                    pe.wait_ge(d_klo, u + 1)
                else:
                    pe.wait_ge(d_qlo, HQ * u + t - 1)
                for g in range(G):
                    last = nc.tensor.transpose(query_bank(u, t)[:, P * g:P * g + P], qn[:, t, g, :], ident)
                last.then_inc(t_qT, 1)

            def scores(u):
                pe.wait_ge(d_klo, u + 1)
                pe.wait_ge(d_qlo, HQ * u + HQ)
                for b in range(HB):
                    o = PB[1][:, S * b:S * b + S]
                    mm(o, qhi[:, b, :, :], khi[:, b, :], start=True, stop=False)
                    mm(o, qhi[:, b, :, :], klo[:, b, :], start=False, stop=False)
                    last = mm(o, qlo[:, b, :, :], khi[:, b, :], start=False, stop=True)
                last.then_inc(t_s, 1)

            def transpose_probs(u):
                pe.wait_ge(p_pr, u + 1)
                pe.wait_ge(d_qlo, HQ * u + HQ)
                for t in range(HQ):
                    last = nc.tensor.transpose(PB[0][:, P * t:P * t + P], pr[:, BQ * t:BQ * t + BQ, :], ident)
                last.then_inc(t_pT, 1)

            def apply_probs(u, half):
                pe.wait_ge(d_pTlo, u + 1)
                pe.wait_ge(d_vlo, 2 * u + 2)
                for t in range(HQ):
                    if not (isinstance(u, int) and u == 0):
                        pe.wait_ge(d_y, HQ * u - HQ + t + 1)
                    split_product(PC[t][:, :], [(vhi[:, half, t, :], vlo[:, half, t, :], pThi[:, t, :, :, :],
                                                 pTlo[:, t, :, :, :])], True, True).then_inc(t_pv, 1)

            def project_out(u, half, kv, t):
                if half == 0 and t == 0:
                    pe.wait_ge(p_wo, G * kv + G)
                pe.wait_ge(d_oTlo, HQ * u + t + 1)
                split_product(PC[t][:, :], [(oThi[:, t, g, :], oTlo[:, t, g, :], wohi[:, g, :], wolo[:, g, :])
                                            for g in range(G)], True, True).then_inc(t_y, 1)

            def step(u, half, kv):
                project_q(u, half, kv, 0)
                scores(u - 1)
                for t in range(1, HQ):
                    project_q(u, half, kv, t)
                transpose_probs(u - 1)
                project_kv(u, half, kv)
                finish(u, half, kv)

            def finish(u, half, kv):
                apply_probs(u - 1, 1 - half)
                for t in range(HQ):
                    project_out(u - 1, 1 - half, kv if half else kv - 1, t)
                    if t == 0:
                        transpose_k(u)
                    for tq in queries_after(t):
                        transpose_q(u, tq)

            gate_logits()
            pe.wait_ge(d_cTlo, HQ)
            pe.wait_ge(d_cf, NQ)
            for t in range(HQ):
                project_q(0, 0, 0, t)
            project_kv(0, 0, 0)
            pe.wait_ge(d_cTlo, NQ)
            project_q(1, 1, 0, 0)
            project_q(1, 1, 0, 1)
            transpose_k(0)
            for t in range(HQ):
                transpose_q(0, t)
            project_q(1, 1, 0, 2)
            scores(0)
            project_q(1, 1, 0, 3)
            project_kv(1, 1, 0, (0,))
            transpose_probs(0)
            project_kv(1, 1, 0, (1,))
            finish(1, 1, 0)
            with pe.Fori(1, HKV) as kv:
                step(2 * kv, 0, kv)
                step(2 * kv + 1, 1, kv)

            def mix(q):
                pe.wait_ge(d_x2lo, q + 1)
                if q < 2:
                    pe.wait_ge(d_vlo, 2 * UNITS)
                else:
                    pe.wait_ge(a_fnat, q - 1)
                if q == HQ:
                    pe.wait_ge(a_part, 4)
                elif q == HQ + 1:
                    pe.wait_ge(d_part, 4)
                split_product(PA[q % 2][:, :], [(mixhi[:, q, :, :], mixlo[:, q, :, :], x2hi[:, q % 2, :],
                                                 x2lo[:, q % 2, :])], True, True).then_inc(t_f, 1)

            def mix_transpose(q):
                pe.wait_ge(a_fnat, q + 1)
                pe.wait_ge(d_y, HQ * (UNITS - 2) + q + 1)
                for c in range(KC):
                    last = nc.tensor.transpose(PC[q % HQ][:, P * c:P * c + P], fnat[:, q % 2, P * c:P * c + P], ident)
                last.then_inc(t_fT, 1)

            def gate_up(i, half, slot, groups=range(2 * KC)):
                n = tile_of(i, half)
                for k in groups:
                    j, g = k // KC, k % KC
                    if half == 0 and g == 0:
                        pe.wait_ge(d_gun, 2 * i + j + 1)
                    read = d_part if k % 2 else a_part
                    o = gate_up_bank(n, k)
                    if isinstance(n, int) and n < 2:
                        if k >= (2 if n else 6):
                            pe.wait_ge(read, 4 + k // 2 if n else 1)
                    elif isinstance(n, int) and n == 2:
                        if k in (2, 3):
                            pe.wait_ge(read, 8)
                    elif g == 0:
                        pe.wait_ge(a_part, 4 * n - 4 + 2 * j + 2)
                        pe.wait_ge(d_part, 4 * n - 4 + 2 * j + 2)
                    mm(o[:, :], gun[:, slot, j, g, :], fThi[:, g, tokens(half)], start=True, stop=False)
                    mm(o[:, :], gun[:, slot, j, g, :], fTlo[:, g, tokens(half)],
                       start=False, stop=True).then_inc(t_gu, 1)

            scores(UNITS - 1)
            mix(0)
            mix(1)
            mix_transpose(0)
            mix(2)
            mix_transpose(1)
            mix(3)
            mix_transpose(2)
            mix_transpose(3)
            transpose_probs(UNITS - 1)
            pe.wait_ge(d_fTlo, HQ)
            pe.wait_ge(a_fnat, HQ)
            gate_up(0, 0, 0)
            pe.wait_ge(a_part, 3)
            pe.wait_ge(d_part, 3)
            apply_probs(UNITS - 1, 1)
            for t in range(HQ - 1):
                project_out(UNITS - 1, 1, HKV - 1, t)
            mix(4)
            project_out(UNITS - 1, 1, HKV - 1, HQ - 1)
            mix(5)
            mix_transpose(4)
            mix(6)
            pe.wait_ge(d_pTlo, UNITS)
            gate_up(1, 0, 1, (0, 1))
            mix_transpose(5)
            mix(7)
            gate_up(1, 0, 1, (2, 3))
            mix_transpose(6)
            mix_transpose(7)
            gate_up(1, 0, 1, (4, 5, 6, 7))
            pe.wait_ge(d_fTlo, NQ)
            gate_up(0, 1, 0)
            gate_up(1, 1, 1)
            with pe.Fori(1, IC // 2) as pair:
                gate_up(2 * pair, 0, 0)
                gate_up(2 * pair, 1, 0)
                gate_up(2 * pair + 1, 0, 1)
                gate_up(2 * pair + 1, 1, 1)

            for i in range(IC):
                last = i == IC - 1
                pe.wait_ge(d_dsub, i + 1)
                if last:
                    pe.wait_ge(p_hlo, 2 * IC)
                for q in range(NQ):
                    if i == 0:
                        pe.wait_ge(d_part if q % 2 else a_part, 8 * IC - 4 + q // 2 + 1)
                    high, low = hThi[:, i, P * q:P * q + P], hTlo[:, i, P * q:P * q + P]
                    if q < EXACT:
                        if i:
                            pe.wait_ge(d_prod, EXACT * (i - 1) + q + 1)
                        mm(bank[q][:, :], high, down_ints(i % 2, i // 2 % 2), start=True, stop=False)
                        mm(bank[q][:, :], low, down_ints(i % 2, i // 2 % 2), start=False, stop=True).then_inc(t_dint, 1)
                    else:
                        if q == EXACT:
                            pe.wait_ge(d_dlo, i + 1)
                        done = split_product(bank[q][:, :], [(high, low, dnhi[:, i % 2, :], dnlo[:, i % 2, :])],
                                             i == 0, last)
                        if last:
                            done.then_inc(t_acc, 1)
                if not last:
                    done.then_inc(t_dn, 1)

        @block.scalar
        def _(act):
            A = nc.scalar.activation
            for q in range(NQ):
                act.wait_ge(d_cf, q + 1)
                A(cThi[:, q, :, :], cf[:, q % 2, :, :, :].rearrange("p c b s -> p c (b s)"),
                  ACT.Copy).then_inc(a_cThi, 1)
                if q == 2:
                    act.wait_ge(l_vec, 16)
                    act.wait_ge(t_h1, 1)
                    A(h1[:, :], PC[2][:, 0:B], ACT.Gelu, bias=vec[:, V_B0:V_B0 + 1]).then_inc(a_h1, 1)
                elif q == 4:
                    act.wait_ge(t_h2, 1)
                    A(h2[:, :], PC[2][:, 0:B], ACT.Gelu, bias=vec[:, V_B1:V_B1 + 1]).then_inc(a_h2, 1)
                elif q == 3:
                    act.wait_ge(l_wq, 16)
                    for c in range(KC):
                        A(wqhi[:, c, :], wqr[:, c, :], ACT.Copy).then_inc(a_wq, 1)
                elif q == 5:
                    act.wait_ge(l_wkv, 16)
                    for c in range(0, KC, 2):
                        A(wkvhi[:, c:c + 2, :], wkvr[:, c:c + 2, :], ACT.Copy).then_inc(a_wkv, 1)

            def split_wq(kv):
                act.wait_ge(t_q, 8 * kv)
                act.wait_ge(l_wq, 16 * kv + 16)
                for c in range(KC):
                    A(wqhi[:, c, :], wqr[:, c, :], ACT.Copy).then_inc(a_wq, 1)

            def split_wkv(kv):
                act.wait_ge(t_kv, 4 * kv)
                act.wait_ge(l_wkv, 16 * kv + 16)
                for c in range(0, KC, 2):
                    A(wkvhi[:, c:c + 2, :], wkvr[:, c:c + 2, :], ACT.Copy).then_inc(a_wkv, 1)

            def split_wo(kv):
                if not (isinstance(kv, int) and kv == 0):
                    act.wait_ge(t_y, 2 * HQ * kv)
                act.wait_ge(l_wo, 16 * kv + 16)
                for g in range(G):
                    A(wohi[:, g, :], wor[:, g, :], ACT.Copy).then_inc(a_wo, 1)

            def queries(u, t):
                first = isinstance(u, int) and u == 0
                act.wait_ge(t_q, HQ * u + t + 1)
                if not first:
                    act.wait_ge(p_qn, HQ * u - HQ + t + 1)
                A(qraw[:, t, :, :], PA[t % 2][:, :].rearrange("p (g d) -> p g d", g=G),
                  ACT.Copy).then_inc(a_qraw, 1)
                act.wait_ge(a_qraw, HQ * u + t + 1)
                if not (first and t < 2):
                    act.wait_ge(d_qss, HQ * u + t - 1)
                A(qsq[:, t % 2, :, :], qraw[:, t, :, :], ACT.Square).then_inc(a_qsq, 1)

            def keys_values(u, half, pairs=(0, 1)):
                first = isinstance(u, int) and u == 0
                for j in pairs:
                    kv2 = PA[j][:, :].rearrange("p (t w) -> p t w", t=2)
                    act.wait_ge(t_kv, 2 * u + j + 1)
                    if j == 0 and not first:
                        act.wait_ge(p_kn, u)
                    A(kraw[:, 2 * j:2 * j + 2, :], kv2[:, :, 0:HD], ACT.Copy).then_inc(a_kraw, 1)
                    A(vhi[:, half, 2 * j:2 * j + 2, :], kv2[:, :, HD:2 * HD], ACT.Copy).then_inc(a_vhi, 1)
                    act.wait_ge(a_kraw, 2 * u + j + 1)
                    if j == 0 and not first:
                        act.wait_ge(d_kss, 2 * u)
                    A(ksq[:, 2 * j:2 * j + 2, :], kraw[:, 2 * j:2 * j + 2, :], ACT.Square).then_inc(a_ksq, 1)

            def mix_input(q):
                act.wait_ge(d_y, HQ * (UNITS - 2) + q + 1)
                if q < HQ:
                    act.wait_ge(p_qn, HQ * UNITS)
                if q >= 2:
                    act.wait_ge(t_f, q - 1)
                A(x2hi[:, q % 2, :], x[:, q, :], ACT.Copy).then_inc(a_x2hi, 1)

            def keys_high(u):
                act.wait_ge(t_kT, u + 1)
                A(khi[:, :, :], PB[0][:, :].rearrange("p (b k) -> p b k", k=S), ACT.Copy,
                  scale=wn[:, 0:1]).then_inc(a_khi, 1)

            def queries_high(u, t):
                act.wait_ge(t_qT, HQ * u + t + 1)
                A(qhi[:, BQ * t:BQ * t + BQ, :, :].rearrange("p b g s -> p g b s"),
                  query_bank(u, t)[:, :].rearrange("p (g b s) -> p g b s", g=G, b=BQ),
                  ACT.Copy).then_inc(a_qhi, 1)

            def score_operands(u, last=False):
                keys_high(u)
                for t in range(HQ):
                    queries_high(u, t)
                if last:
                    mix_input(0)
                    mix_input(1)

            def exponentials(u):
                act.wait_ge(p_sub, u + 1)
                if not (isinstance(u, int) and u == 0):
                    act.wait_ge(p_pr, u)
                A(ex[:, :, :], sc[:, :, :], ACT.Exp).then_inc(a_exp, 1)

            def probs_high(u):
                act.wait_ge(t_pT, u + 1)
                for b in range(BQ):
                    A(pThi[S * b:S * b + S, :, :, b, :],
                      PB[0][S * b:S * b + S, :].rearrange("p (t g s) -> p t g s", t=HQ, g=G),
                      ACT.Copy).then_inc(a_pThi, 1)

            def outputs_high(u):
                for t in range(HQ):
                    act.wait_ge(t_pv, HQ * u + t + 1)
                    A(oThi[:, t, :, :], PC[t][:, :].rearrange("p (g n) -> p g n", g=G), ACT.Copy).then_inc(a_oThi, 1)

            def step(u, half, kv, last):
                queries(u, 0)
                if half:
                    split_wo(kv)
                exponentials(u - 1)
                queries(u, 1)
                queries(u, 2)
                queries(u, 3)
                probs_high(u - 1)
                keys_values(u, half)
                outputs_high(u - 1)
                if half and not last:
                    split_wq(kv + 1)
                    split_wkv(kv + 1)
                score_operands(u, last and half == 1)

            act.wait_ge(d_lg, 1)
            A(le[:, :, :], lg[:, :, :], ACT.Exp).then_inc(a_lexp, 1)
            act.wait_ge(d_wscale, 1)
            for t in range(HQ):
                queries(0, t)
            keys_values(0, 0)
            act.wait_ge(d_mix, 1)
            A(mixhi[:, :, :, :], mixf[:, :, :, :], ACT.Copy).then_inc(a_mixhi, 1)
            queries(1, 0)
            keys_high(0)
            for t in range(HQ):
                queries_high(0, t)
            queries(1, 1)
            queries(1, 2)
            act.wait_ge(d_mixlo, 1)
            split_wo(0)
            exponentials(0)
            queries(1, 3)
            keys_values(1, 1, (0,))
            probs_high(0)
            keys_values(1, 1, (1,))
            outputs_high(0)
            split_wq(1)
            split_wkv(1)
            score_operands(1)
            with act.Fori(1, HKV - 1) as kv:
                step(2 * kv, 0, kv, False)
                step(2 * kv + 1, 1, kv, False)
            step(UNITS - 2, 0, HKV - 1, True)
            step(UNITS - 1, 1, HKV - 1, True)

            def mix_out(q):
                act.wait_ge(t_f, q + 1)
                if q >= 2:
                    act.wait_ge(t_fT, q - 1)
                A(fnat[:, q % 2, :], PA[q % 2][:, :], ACT.Identity, bias=aggb[:, q:q + 1]).then_inc(a_fnat, 1)

            def mix_high(q):
                act.wait_ge(t_fT, q + 1)
                A(fThi[:, :, P * q:P * q + P], PC[q % HQ][:, :].rearrange("p (c t) -> p c t", c=KC),
                  ACT.Copy).then_inc(a_fThi, 1)

            def scaled(i, half, slot, j, groups=(0, 2)):
                n = tile_of(i, half)
                o_first = whole[:, tile_slot(i, half), j, :]
                if groups[0] + j == 0:
                    act.wait_ge(d_scl, i + 1)
                    if not (isinstance(n, int) and n < 2):
                        act.wait_ge(d_h, n - 1)
                for g in groups:
                    act.wait_ge(t_gu, 2 * KC * n + KC * j + g + 1)
                    if g == 2 and not (isinstance(n, int) and n == 0):
                        act.wait_ge(p_whole, 2 * n - 1 + j)
                    src = gate_up_bank(n, KC * j + g)
                    A(part[:, j, :] if g else o_first, src[:, :], ACT.Copy,
                      scale=scl[:, slot, j, g:g + 1]).then_inc(a_part, 1)

            def gate(i, half):
                n = tile_of(i, half)
                act.wait_ge(p_whole, 2 * n + 1)
                h = whole[:, tile_slot(i, half), 0, :]
                A(h, h, ACT.Silu).then_inc(a_silu, 1)

            def hidden_high(i, half):
                act.wait_ge(d_h, tile_of(i, half) + 1)
                A(hThi[:, i, tokens(half)], hf[:, tile_slot(i, half), :], ACT.Copy).then_inc(a_hhi, 1)

            def tile(i, half, slot):
                scaled(i, half, slot, 0, (0,))
                if not (isinstance(i, int) and i == 0):
                    hidden_high(*tile_before(i, half, 2))
                scaled(i, half, slot, 0, (2,))
                gate(*tile_before(i, half))
                scaled(i, half, slot, 1)

            mix_out(0)
            mix_input(2)
            mix_out(1)
            mix_input(3)
            mix_high(0)
            exponentials(UNITS - 1)
            mix_out(2)
            mix_high(1)
            mix_out(3)
            mix_high(2)
            mix_high(3)
            probs_high(UNITS - 1)
            scaled(0, 0, 0, 0)
            scaled(0, 0, 0, 1)
            gate(0, 0)
            outputs_high(UNITS - 1)
            hidden_high(0, 0)
            mix_input(4)
            mix_input(5)
            mix_out(4)
            mix_input(6)
            mix_out(5)
            mix_input(7)
            mix_high(4)
            mix_out(6)
            scaled(1, 0, 1, 0, (0,))
            mix_high(5)
            mix_out(7)
            scaled(1, 0, 1, 0, (2,))
            mix_high(6)
            mix_high(7)
            scaled(1, 0, 1, 1)
            tile(0, 1, 0)
            tile(1, 1, 1)
            for i in (2, 3):
                tile(i, 0, i % 2)
                tile(i, 1, i % 2)
            with act.Fori(2, IC // 2 - 1) as pair:
                tile(2 * pair, 0, 0)
                tile(2 * pair, 1, 0)
                tile(2 * pair + 1, 0, 1)
                tile(2 * pair + 1, 1, 1)
            tile(IC - 2, 0, 0)
            tile(IC - 2, 1, 0)

            def down_high(i, slot):
                act.wait_ge(p_dmul, i + 1)
                A(dnhi[:, slot, :], down_weights(i, slot), ACT.Copy).then_inc(a_dhi, 1)

            tile(IC - 1, 0, 1)
            scaled(IC - 1, 1, 1, 0, (0,))
            hidden_high(IC - 2, 1)
            scaled(IC - 1, 1, 1, 0, (2,))
            gate(IC - 1, 0)
            down_high(0, 0)
            scaled(IC - 1, 1, 1, 1)
            gate(IC - 1, 1)
            hidden_high(IC - 1, 0)
            down_high(1, 1)
            hidden_high(IC - 1, 1)
            with act.Fori(2, IC, 2) as i:
                down_high(i, 0)
                down_high(i + 1, 1)

        @block.vector
        def _(dve):
            V = nc.vector
            link = chain(dve, d_self)
            V.memset(ones[:, :], 1.0).then_inc(d_ones, 1)
            dve.wait_ge(l_conv, 32)
            V.tensor_tensor(cwf[:, :, :, :, :].rearrange("p j f g o -> p (j f) g o"),
                            cwr[:, :, :, None, :].rearrange("p j f a o -> p (j f) a o").broadcast_to(
                                [P, SHIFTS * PH, NGRP, CG]),
                            mask[:, None, :, None].broadcast_to([P, SHIFTS * PH, NGRP, CG]),
                            ALU.mult).then_inc(d_cwf, 1)
            dve.wait_ge(l_cond, 48)
            V.tensor_tensor(ctxr[:, :, :], condT[:, :, None].broadcast_to([P, B, S]),
                            cwT[:, None, :].broadcast_to([P, B, S]), ALU.mult).then_inc(d_ctxr, 1)
            for h in range(2):
                dve.wait_ge(t_ctx, h + 1)
                V.tensor_tensor(ctxb[:, HB * h:HB * h + HB, :], PC[h][:, :].rearrange("p (b s) -> p b s", s=S),
                                fs[:, None, :].broadcast_to([P, HB, S]), ALU.add).then_inc(d_ctxb, 1)

            def conv_out(q):
                dve.wait_ge(t_conv, q + 1)
                dve.wait_ge(d_ctxb, 2)
                if q >= 2:
                    dve.wait_ge(d_cTlo, q - 1)
                V.tensor_tensor(cf[:, q % 2, :, :, :].rearrange("p c b s -> p c (b s)"),
                                PA[q % 2][:, :].rearrange("p (c n) -> p c n", c=PH),
                                ctxb[:, None, BQ * q:BQ * q + BQ, :].rearrange("p a b s -> p a (b s)").broadcast_to(
                                    [P, PH, P]), ALU.add).then_inc(d_cf, 1)

            def conv_low(q):
                dve.wait_ge(a_cThi, q + 1)
                V.tensor_tensor(cTlo[:, q, :, :], cf[:, q % 2, :, :, :].rearrange("p c b s -> p c (b s)"),
                                cThi[:, q, :, :].bitcast(F32), ALU.subtract).then_inc(d_cTlo, 1)

            conv_out(0)
            dve.wait_ge(l_vec, 16)
            V.memset(neghalf[:, :, :], -0.5).then_inc(d_wcol, 1)
            link(V.tensor_tensor(wcol[:, 0:1], vec[:, V_QW:V_QW + 1], vec[:, V_KW:V_KW + 1], ALU.mult))
            link(V.tensor_scalar(wcol[:, 1:2], wcol[:, 0:1], -1.0, None, ALU.mult))
            V.tensor_tensor(wcol[:, 2:3], wcol[:, 0:1], wcol[:, 1:2], ALU.max).then_inc(d_wcol, 1)
            e8 = [P, NQ, EXPERTS]
            for q in range(NQ):
                if q + 1 < NQ:
                    conv_out(q + 1)
                conv_low(q)
                if q == 1:
                    dve.wait_ge(g_wmax, 1)
                    link(V.tensor_scalar(wmax[:, 1:2], wmax[:, 0:1], 1e-30, None, ALU.max))
                    link(V.reciprocal(wcol[:, 3:4], wmax[:, 1:2]))
                    link(V.tensor_scalar(scale[:, :], wmax[:, 1:2], float(HD) ** -0.5, None, ALU.mult))
                    V.tensor_tensor(wn[:, :], wcol[:, 0:1], wcol[:, 3:4], ALU.mult).then_inc(d_wscale, 1)
                if q == 4:
                    dve.wait_ge(a_h2, 1)
                    V.tensor_copy(h2r[:, :, :], h2[:, :, None].broadcast_to([P, B, S])).then_inc(d_h2r, 1)
            def gate_logits():
                dve.wait_ge(t_lg, 1)
                link(V.tensor_tensor(lg[:, :, :], PC[3][:, 0:NQ * EXPERTS].rearrange("p (q e) -> p q e", q=NQ),
                                     b2[:, None, :].broadcast_to(e8), ALU.add))
                link(V.tensor_reduce(lst[:, 0, :], lg[:, :, :], AX_X, ALU.max))
                V.tensor_tensor(lg[:, :, :], lg[:, :, :], lst[:, 0, :, None].broadcast_to(e8),
                                ALU.subtract).then_inc(d_lg, 1)

            def gate_probs():
                dve.wait_ge(a_lexp, 1)
                link(V.tensor_reduce(lst[:, 1, :], le[:, :, :], AX_X, ALU.add))
                link(V.reciprocal(lst[:, 0, :], lst[:, 1, :]))
                link(V.tensor_tensor(le[:, :, :], le[:, :, :], lst[:, 0, :, None].broadcast_to(e8), ALU.mult))
                link(V.tensor_tensor(mixb[:, :, :], le[:, :, :],
                                     vec[:, None, V_BK:V_BK + EXPERTS].broadcast_to(e8), ALU.mult))
                link(V.tensor_reduce(aggb[:, :], mixb[:, :, :], AX_X, ALU.add))

            def mixing_products():
                dve.wait_ge(l_mix, 64)
                link(V.tensor_tensor(mixp[:, :, :, :], mixw[:, None, :, :].broadcast_to([P, NQ, S, EXPERTS]),
                                     le[:, :, None, :].broadcast_to([P, NQ, S, EXPERTS]), ALU.mult))

            def mixing_sums():
                link(V.tensor_reduce(mixa[:, :, :], mixp[:, :, :, :], AX_X, ALU.add))

            def mixing_weights():
                dve.wait_ge(l_const, 16)
                V.tensor_tensor(mixf[:, :, :, :], mixa[:, :, None, :].broadcast_to([P, NQ, BQ, S]),
                                quadmask[:, None, :, None].broadcast_to([P, NQ, BQ, S]),
                                ALU.mult).then_inc(d_mix, 1)

            def queries(u, t):
                dve.wait_ge(a_qsq, HQ * u + t + 1)
                V.tensor_reduce(qss[:, t, :], qsq[:, t % 2, :, :], AX_X, ALU.add).then_inc(d_qss, 1)
                if t == HQ - 1:
                    if not (isinstance(u, int) and u == 0):
                        dve.wait_ge(p_qpow, u)
                    dve.wait_ge(d_qss, HQ * u + HQ)
                    V.tensor_scalar(qms[:, :, :], qss[:, :, :], 1.0 / HD, EPS, ALU.mult, ALU.add).then_inc(d_qms, 1)

            def keys_values(u, half, pairs=(0, 1)):
                for j in pairs:
                    dve.wait_ge(a_vhi, 2 * u + j + 1)
                    kv2 = PA[j][:, :].rearrange("p (t w) -> p t w", t=2)
                    V.tensor_tensor(vlo[:, half, 2 * j:2 * j + 2, :], kv2[:, :, HD:2 * HD],
                                    vhi[:, half, 2 * j:2 * j + 2, :].bitcast(F32), ALU.subtract).then_inc(d_vlo, 1)
                    dve.wait_ge(a_ksq, 2 * u + j + 1)
                    V.tensor_reduce(kss[:, 2 * j:2 * j + 2], ksq[:, 2 * j:2 * j + 2, :], AX_X,
                                    ALU.add).then_inc(d_kss, 1)
                if 1 not in pairs:
                    return
                if not (isinstance(u, int) and u == 0):
                    dve.wait_ge(p_kpow, u)
                dve.wait_ge(d_kss, 2 * u + 2)
                V.tensor_scalar(kms[:, :], kss[:, :], 1.0 / HD, EPS, ALU.mult, ALU.add).then_inc(d_kms, 1)

            def keys_low(u):
                dve.wait_ge(a_khi, u + 1)
                V.scalar_tensor_tensor(klo[:, :, :], PB[0][:, :].rearrange("p (b k) -> p b k", k=S), wn[:, 0:1],
                                       khi[:, :, :], ALU.mult, ALU.subtract).then_inc(d_klo, 1)

            def queries_low(u, t):
                dve.wait_ge(a_qhi, HQ * u + t + 1)
                V.tensor_tensor(qlo[:, BQ * t:BQ * t + BQ, :, :].rearrange("p b g s -> p g b s"),
                                query_bank(u, t)[:, :].rearrange("p (g b s) -> p g b s", g=G, b=BQ),
                                qhi[:, BQ * t:BQ * t + BQ, :, :].rearrange("p b g s -> p g b s"),
                                ALU.subtract).then_inc(d_qlo, 1)

            def scores_biased(u, kv):
                first = isinstance(u, int) and u == 0
                dve.wait_ge(t_s, u + 1)
                if not first:
                    dve.wait_ge(a_exp, u)
                bias = const[:, bass.ds(kv * S + C_BIAS, S)]
                V.scalar_tensor_tensor(sc[:, :, :], PB[1][:, :].rearrange("p (b k) -> p b k", k=S), scale[:, 0:1],
                                       bias[:, None, :].broadcast_to([P, HB, S]), ALU.mult,
                                       ALU.add).then_inc(d_sc, 1)
                dve.wait_ge(d_sc, u + 1)
                V.tensor_reduce(smax[:, :], sc[:, :, :], AX_X, ALU.max).then_inc(d_smax, 1)

            def probs_sum(u):
                first = isinstance(u, int) and u == 0
                dve.wait_ge(a_exp, u + 1)
                V.tensor_reduce(ssum[:, :], ex[:, :, :], AX_X, ALU.add).then_inc(d_srec, 1)
                dve.wait_ge(d_srec, 2 * u + 1)
                if not first:
                    dve.wait_ge(p_pr, u)
                V.reciprocal(srec[:, :], ssum[:, :]).then_inc(d_srec, 1)

            def probs_low(u):
                for b in range(BQ):
                    dve.wait_ge(a_pThi, BQ * u + b + 1)
                    ins = V.tensor_tensor(pTlo[S * b:S * b + S, :, :, b, :],
                                          PB[0][S * b:S * b + S, :].rearrange("p (t g s) -> p t g s", t=HQ, g=G),
                                          pThi[S * b:S * b + S, :, :, b, :].bitcast(F32), ALU.subtract)
                ins.then_inc(d_pTlo, 1)

            def outputs_low(u):
                for t in range(HQ):
                    dve.wait_ge(a_oThi, HQ * u + t + 1)
                    V.tensor_tensor(oTlo[:, t, :, :], PC[t][:, :].rearrange("p (g n) -> p g n", g=G),
                                    oThi[:, t, :, :].bitcast(F32), ALU.subtract).then_inc(d_oTlo, 1)

            def add_outputs(u, half, t):
                dve.wait_ge(t_y, HQ * u + t + 1)
                if not (isinstance(u, int) and u < 2):
                    dve.wait_ge(d_y, HQ * u - 2 * HQ + t + 1)
                q = HQ * half + t
                V.tensor_tensor(x[:, q, :], PC[t][:, :], x[:, q, :], ALU.add).then_inc(d_y, 1)

            def mix_input(q):
                dve.wait_ge(a_x2hi, q + 1)
                V.tensor_tensor(x2lo[:, q % 2, :], x[:, q, :], x2hi[:, q % 2, :].bitcast(F32),
                                ALU.subtract).then_inc(d_x2lo, 1)

            def step(u, half, kv, last=False):
                queries(u, 0)
                scores_biased(u - 1, kv if half else kv - 1)
                probs_sum(u - 1)
                for t in range(1, HQ):
                    queries(u, t)
                probs_low(u - 1)
                keys_values(u, half)
                outputs_low(u - 1)
                for t in range(HQ):
                    if last and t == HQ - 1:
                        mix_input(0)
                        mix_input(1)
                    add_outputs(u - 1, 1 - half, t)
                    if t == 0:
                        keys_low(u)
                    for tq in queries_after(t):
                        queries_low(u, tq)

            gate_logits()
            queries(0, 0)
            gate_probs()
            queries(0, 1)
            mixing_products()
            queries(0, 2)
            mixing_sums()
            queries(0, 3)
            keys_values(0, 0)
            mixing_weights()
            dve.wait_ge(a_mixhi, 1)
            V.tensor_tensor(mixlo[:, :, :, :], mixf[:, :, :, :], mixhi[:, :, :, :].bitcast(F32),
                            ALU.subtract).then_inc(d_mixlo, 1)
            queries(1, 0)
            keys_low(0)
            for t in range(HQ):
                queries_low(0, t)
            queries(1, 1)
            scores_biased(0, 0)
            queries(1, 2)
            probs_sum(0)
            queries(1, 3)
            keys_values(1, 1, (0,))
            dve.wait_ge(g_zero, 2)
            probs_low(0)
            keys_values(1, 1, (1,))
            outputs_low(0)
            dve.wait_ge(l_x, 16)
            for t in range(HQ):
                add_outputs(0, 0, t)
                if t == 0:
                    keys_low(1)
                for tq in queries_after(t):
                    queries_low(1, tq)
            step(2, 0, 1)
            step(3, 1, 1)
            with dve.Fori(2, HKV - 1) as kv:
                step(2 * kv, 0, kv)
                step(2 * kv + 1, 1, kv)
            step(UNITS - 2, 0, HKV - 1)
            step(UNITS - 1, 1, HKV - 1, True)

            def mix_low(q):
                dve.wait_ge(a_fThi, q + 1)
                V.tensor_tensor(fTlo[:, :, P * q:P * q + P], PC[q % HQ][:, :].rearrange("p (c t) -> p c t", c=KC),
                                fThi[:, :, P * q:P * q + P].bitcast(F32), ALU.subtract).then_inc(d_fTlo, 1)

            def integers(i, slot, j, first=False):
                dve.wait_ge(l_up if j else l_gate, 32 * i + 32)
                if not first:
                    dve.wait_ge(d_part, 12 if isinstance(i, int) and i == 2 else 8 * i - 8)
                if j == 0:
                    V.tensor_scalar(scl[:, slot, :, :], gus[:, i, :, :], 1.0, None, ALU.mult).then_inc(d_scl, 1)
                V.tensor_tensor(gun[:, slot, j, :, :], guw[:, j, :, :], guz[:, j, :, :],
                                ALU.subtract).then_inc(d_gun, 1)

            def scaled(i, half, slot, j, groups=(1, 3)):
                n = tile_of(i, half)
                o_first = whole[:, tile_slot(i, half), j, :]
                if j == 0:
                    dve.wait_ge(d_scl, i + 1)
                for g in groups:
                    o = part[:, j, :] if g == 3 else o_first
                    dve.wait_ge(t_gu, 2 * KC * n + KC * j + g + 1)
                    dve.wait_ge(a_part, 4 * n + 2 * j + g // 2 + 1)
                    V.scalar_tensor_tensor(o, gate_up_bank(n, KC * j + g)[:, :], scl[:, slot, j, g:g + 1], o,
                                           ALU.mult, ALU.add).then_inc(d_part, 1)

            def hidden(i, half):
                n = tile_of(i, half)
                dve.wait_ge(a_silu, n + 1)
                dve.wait_ge(p_whole, 2 * n + 2)
                if not (isinstance(n, int) and n < 2):
                    dve.wait_ge(p_hlo, n - 1)
                V.tensor_tensor(hf[:, tile_slot(i, half), :], whole[:, tile_slot(i, half), 0, :], whole[:, tile_slot(i, half), 1, :],
                                ALU.mult).then_inc(d_h, 1)

            def tile(i, half, slot):
                scaled(i, half, slot, 0)
                hidden(*tile_before(i, half))
                scaled(i, half, slot, 1)

            dve.wait_ge(l_gus, 16)
            integers(0, 0, 0, True)
            scores_biased(UNITS - 1, HKV - 1)
            integers(0, 0, 1, True)
            mix_input(2)
            mix_input(3)
            mix_low(0)
            probs_sum(UNITS - 1)
            mix_low(1)
            mix_low(2)
            mix_low(3)
            probs_low(UNITS - 1)
            scaled(0, 0, 0, 0)
            scaled(0, 0, 0, 1)
            outputs_low(UNITS - 1)
            hidden(0, 0)
            integers(1, 1, 0, True)
            integers(1, 1, 1, True)
            add_outputs(UNITS - 1, 1, 0)
            add_outputs(UNITS - 1, 1, 1)
            mix_input(4)
            add_outputs(UNITS - 1, 1, 2)
            mix_input(5)
            mix_input(6)
            add_outputs(UNITS - 1, 1, 3)
            mix_input(7)
            mix_low(4)
            scaled(1, 0, 1, 0, (1,))
            mix_low(5)
            scaled(1, 0, 1, 0, (3,))
            mix_low(6)
            mix_low(7)
            scaled(1, 0, 1, 1)
            tile(0, 1, 0)
            integers(2, 0, 0)
            tile(1, 1, 1)
            integers(2, 0, 1)
            with dve.Fori(1, IC // 2 - 1) as pair:
                tile(2 * pair, 0, 0)
                integers(2 * pair + 1, 1, 0)
                tile(2 * pair, 1, 0)
                integers(2 * pair + 1, 1, 1)
                tile(2 * pair + 1, 0, 1)
                integers(2 * pair + 2, 0, 0)
                tile(2 * pair + 1, 1, 1)
                integers(2 * pair + 2, 0, 1)
            tile(IC - 2, 0, 0)
            integers(IC - 1, 1, 0)
            tile(IC - 2, 1, 0)
            integers(IC - 1, 1, 1)

            def down_integers(i, slot, place, loaded):
                dve.wait_ge(loaded, 24 * i - 24 * slot + 48)
                if isinstance(i, int) and i < 4:
                    dve.wait_ge(t_gu, 4 * KC * IC if slot else 4 * KC * (IC - 1))
                else:
                    dve.wait_ge(t_dn, i - 3)
                V.tensor_tensor(down_ints(slot, place), guw[:, slot, :, :].rearrange("p b c -> p (b c)"),
                                guz[:, slot, :, :].rearrange("p b c -> p (b c)"), ALU.subtract).then_inc(d_dsub, 1)

            def down_low(i, slot):
                dve.wait_ge(a_dhi, i + 1)
                V.tensor_tensor(dnlo[:, slot, :], down_weights(i, slot),
                                dnhi[:, slot, :].bitcast(F32), ALU.subtract).then_inc(d_dlo, 1)

            scaled(IC - 1, 0, 1, 0)
            hidden(IC - 2, 1)
            down_integers(0, 0, 0, l_dn0)
            scaled(IC - 1, 0, 1, 1)
            scaled(IC - 1, 1, 1, 0)
            down_low(0, 0)
            hidden(IC - 1, 0)
            scaled(IC - 1, 1, 1, 1)
            down_integers(1, 1, 0, l_dn1)
            hidden(IC - 1, 1)

            def down_scaled(i, slot, place):
                if isinstance(i, int) and i == 0:
                    dve.wait_ge(d_h, 2 * IC)
                for q in range(EXACT):
                    dve.wait_ge(t_dint, EXACT * i + q + 1)
                    if not (isinstance(i, int) and i == 0):
                        if q == 0:
                            dve.wait_ge(d_sum, i)
                        else:
                            dve.wait_ge(p_sum, 2 * i - 2 + q)
                    V.tensor_tensor(down_product(q), bank[q][:, :], down_scales(slot, place),
                                    ALU.mult).then_inc(d_prod, 1)
                if not (isinstance(i, int) and i == IC - 1):
                    down_low(i + 1, 1 - slot)
                if not (isinstance(i, int) and i >= IC - 2):
                    down_integers(i + 2, slot, 1 - place, (l_dn0, l_dn1)[slot])
                dve.wait_ge(d_prod, EXACT * i + 1)
                V.tensor_tensor(x[:, 0, :], down_product(0), x[:, 0, :], ALU.add).then_inc(d_sum, 1)

            for i in range(4):
                down_scaled(i, i % 2, i // 2 % 2)
            with dve.Fori(4, IC - 2, 4) as i:
                down_scaled(i, 0, 0)
                down_scaled(i + 1, 1, 0)
                down_scaled(i + 2, 0, 1)
                down_scaled(i + 3, 1, 1)
            down_scaled(IC - 2, (IC - 2) % 2, (IC - 2) // 2 % 2)
            down_scaled(IC - 1, (IC - 1) % 2, (IC - 1) // 2 % 2)
            for q in range(EXACT, NQ):
                dve.wait_ge(t_acc, q - EXACT + 1)
                V.tensor_tensor(x[:, q, :], bank[q][:, :], x[:, q, :], ALU.add).then_inc(d_res, 1)

        @block.gpsimd
        def _(pool):
            Q = nc.gpsimd
            Q.memset(xT[:, :, 0:1], 0.0).then_inc(g_pad, 1)
            Q.memset(xT[:, :, P + 1:P + 2], 0.0).then_inc(g_pad, 1)
            pool.wait_ge(d_wcol, 2)
            Q.partition_all_reduce(wmax[:, 0:1], wcol[:, 2:3], P, bass.bass_isa.ReduceOp.max).then_inc(g_wmax, 1)

            def split_wq(kv):
                for c in range(KC):
                    pool.wait_ge(a_wq, KC * kv + c + 1)
                    Q.tensor_tensor(wqlo[:, c, :], wqr[:, c, :], wqhi[:, c, :].bitcast(F32),
                                    ALU.subtract).then_inc(p_wq, 1)

            def split_wkv(kv):
                for c in range(0, KC, 2):
                    pool.wait_ge(a_wkv, 2 * kv + c // 2 + 1)
                    Q.tensor_tensor(wkvlo[:, c:c + 2, :], wkvr[:, c:c + 2, :], wkvhi[:, c:c + 2, :].bitcast(F32),
                                    ALU.subtract).then_inc(p_wkv, 1)

            def split_wo(kv, groups):
                for g in groups:
                    pool.wait_ge(a_wo, G * kv + g + 1)
                    Q.tensor_tensor(wolo[:, g, :], wor[:, g, :], wohi[:, g, :].bitcast(F32),
                                    ALU.subtract).then_inc(p_wo, 1)

            def query_norms(u):
                pool.wait_ge(d_qms, u + 1)
                Q.tensor_tensor(qinv[:, :, :], qms[:, :, :], neghalf[:, :, :], ALU.pow).then_inc(p_qpow, 1)

            def queries(u):
                pool.wait_ge(p_qpow, u + 1)
                for t in range(HQ):
                    if not (isinstance(u, int) and u == 0):
                        pool.wait_ge(t_qT, HQ * u - HQ + t + 1)
                    Q.tensor_tensor(qn[:, t, :, :], qraw[:, t, :, :],
                                    qinv[:, t, :, None].broadcast_to([P, G, HD]), ALU.mult).then_inc(p_qn, 1)

            def keys_values(u):
                pool.wait_ge(d_kms, u + 1)
                Q.tensor_tensor(kinv[:, :], kms[:, :], neghalf[:, :, 0], ALU.pow).then_inc(p_kpow, 1)
                pool.wait_ge(p_kpow, u + 1)
                if not (isinstance(u, int) and u == 0):
                    pool.wait_ge(t_kT, u)
                Q.tensor_tensor(kn[:, :, :], kraw[:, :, :], kinv[:, :, None].broadcast_to([P, HQ, HD]),
                                ALU.mult).then_inc(p_kn, 1)

            def scores_shifted(u):
                pool.wait_ge(d_smax, u + 1)
                Q.tensor_tensor(sc[:, :, :], sc[:, :, :], smax[:, :, None].broadcast_to([P, HB, S]),
                                ALU.subtract).then_inc(p_sub, 1)

            def probs(u):
                pool.wait_ge(d_srec, 2 * u + 2)
                if not (isinstance(u, int) and u == 0):
                    pool.wait_ge(t_pT, u)
                Q.tensor_tensor(pr[:, :, :], ex[:, :, :], srec[:, :, None].broadcast_to([P, HB, S]),
                                ALU.mult).then_inc(p_pr, 1)

            def step(u, half, kv, last):
                if half:
                    split_wo(kv, (0,))
                scores_shifted(u - 1)
                if half:
                    split_wo(kv, (1,))
                probs(u - 1)
                if half:
                    split_wo(kv, (2, 3))
                query_norms(u)
                keys_values(u)
                queries(u)
                if half and not last:
                    split_wq(kv + 1)
                    split_wkv(kv + 1)

            split_wq(0)
            split_wkv(0)
            query_norms(0)
            keys_values(0)
            queries(0)
            pool.wait_ge(d_cTlo, NQ)
            pool.wait_ge(d_lg, 1)
            Q.memset(pThi[:, :, :, :, :].bitcast(F32), 0.0).then_inc(g_zero, 1)
            Q.memset(pTlo[:, :, :, :, :].bitcast(F32), 0.0).then_inc(g_zero, 1)
            pool.wait_ge(g_zero, 2)
            split_wo(0, (0,))
            scores_shifted(0)
            split_wo(0, (1,))
            probs(0)
            split_wo(0, (2, 3))
            query_norms(1)
            keys_values(1)
            queries(1)
            split_wq(1)
            split_wkv(1)
            with pool.Fori(1, HKV - 1) as kv:
                step(2 * kv, 0, kv, False)
                step(2 * kv + 1, 1, kv, False)
            step(UNITS - 2, 0, HKV - 1, True)
            step(UNITS - 1, 1, HKV - 1, True)

            def add_part(i, half, j):
                pool.wait_ge(d_part, 4 * tile_of(i, half) + 2 * j + 2)
                o = whole[:, tile_slot(i, half), j, :]
                Q.tensor_tensor(o, o, part[:, j, :], ALU.add).then_inc(p_whole, 1)

            def hidden_low(i, half):
                pool.wait_ge(a_hhi, tile_of(i, half) + 1)
                Q.tensor_tensor(hTlo[:, i, tokens(half)], hf[:, tile_slot(i, half), :], hThi[:, i, tokens(half)].bitcast(F32),
                                ALU.subtract).then_inc(p_hlo, 1)

            def tile(i, half):
                if not (isinstance(i, int) and i == 0):
                    hidden_low(*tile_before(i, half, 2))
                add_part(i, half, 0)
                add_part(i, half, 1)

            scores_shifted(UNITS - 1)
            probs(UNITS - 1)
            add_part(0, 0, 0)
            add_part(0, 0, 1)
            hidden_low(0, 0)
            add_part(1, 0, 0)
            add_part(1, 0, 1)
            tile(0, 1)
            tile(1, 1)
            tile(2, 0)
            tile(2, 1)
            with pool.Fori(3, IC - 1) as i:
                tile(i, 0)
                tile(i, 1)

            def scale_dn(i, slot, place):
                pool.wait_ge(d_dsub, i + 1)
                if not (isinstance(i, int) and i < 2):
                    pool.wait_ge(t_dn, i - 1)
                    if isinstance(i, int) and i < 4:
                        pool.wait_ge(p_hlo, 2 * IC - 1 + slot)
                Q.tensor_tensor(down_weights(i, slot),
                                down_ints(slot, place).bitcast(F32), down_scales(slot, place),
                                ALU.mult).then_inc(p_dmul, 1)

            hidden_low(IC - 2, 0)
            add_part(IC - 1, 0, 0)
            scale_dn(0, 0, 0)
            add_part(IC - 1, 0, 1)
            tile(IC - 1, 1)
            scale_dn(1, 1, 0)
            hidden_low(IC - 1, 0)
            hidden_low(IC - 1, 1)

            def add_products(i):
                for q in range(1, EXACT):
                    pool.wait_ge(d_prod, EXACT * i + q + 1)
                    if not (isinstance(i, int) and i == 0):
                        pool.wait_ge(p_sum, 2 * i - 2 + q)
                    Q.tensor_tensor(x[:, q, :], down_product(q), x[:, q, :], ALU.add).then_inc(p_sum, 1)

            def down_step(i, slot, place):
                scale_dn(i + 1, 1 - slot, (1 - place) if slot else place)
                add_products(i)

            add_products(0)
            for i in range(1, 4):
                down_step(i, i % 2, i // 2 % 2)
            with pool.Fori(4, IC - 2, 4) as i:
                down_step(i, 0, 0)
                down_step(i + 1, 1, 0)
                down_step(i + 2, 0, 1)
                down_step(i + 3, 1, 1)
            down_step(IC - 2, (IC - 2) % 2, (IC - 2) // 2 % 2)
            add_products(IC - 1)


def kernel(**inputs):
    import concourse.bacc as _bacc
    from concourse import mybir as _mybir
    from concourse.bass_utils import run_bass_kernel_spmd as _run

    a = {k: np.asarray(v) for k, v in inputs.items()}

    def tile_gu(w):
        return w.reshape(KC, P, IC, P).transpose(2, 1, 0, 3)

    def row_gu(w):
        return w.reshape(KC, IC, P).transpose(1, 0, 2)

    wk = a["L0_attn_Wk"].reshape(HKV, HD, P, PH).transpose(0, 2, 3, 1)
    wv = a["L0_attn_Wv"].reshape(HKV, HD, P, PH).transpose(0, 2, 3, 1)
    w = a["L0_cond_weight"].reshape(NGRP, CG, CG, TAPS)
    w = np.pad(w, ((0, 0), (0, 0), (0, 0), (PH - 1, SHIFTS * PH - TAPS)))
    taps = np.stack([np.stack([w[..., np.arange(SHIFTS) * PH + i - o + PH - 1] for o in range(PH)], axis=4)
                     for i in range(PH)])
    taps = taps.transpose(0, 1, 3, 4, 5, 2).reshape(P, SHIFTS, PH, CG)
    vec = np.concatenate([
        np.stack([a["L0_cond2_b0"], a["L0_cond2_b1"], a["L0_attn_q_norm_w"], a["L0_attn_k_norm_w"]],
                 axis=1),
        np.tile(a["L0_cond2_bias_k"].T, (BQ, 1))], axis=1)
    arrays = {
        "x": a["x"].reshape(NQ, P, DM).transpose(1, 0, 2),
        "xt": a["x"].reshape(B, S, P, PH).transpose(3, 1, 0, 2).reshape(P, B, P),
        "mask": group_mask(),
        "fs": a["fside_S_0"].reshape(1, S),
        "cond": a["cond_128"].T,
        "cw": a["L0_cond_c_weight"].T,
        "conv": taps,
        "wq": a["L0_attn_Wq"].reshape(HKV, G * HD, P, PH).transpose(0, 2, 3, 1),
        "wkv": np.concatenate([wk, wv], axis=3),
        "wo": a["L0_attn_Wo"].T.reshape(HKV, G, HD, DM).transpose(0, 2, 1, 3) if a["L0_attn_Wo"].shape[0] == DM else None,
        "w0": a["L0_cond2_W0"], "w1": a["L0_cond2_W1"], "w2": a["L0_cond2_W2"],
        "b2": a["L0_cond2_b2"].reshape(1, EXPERTS),
        "mix": a["L0_cond2_weight"][..., 0].transpose(2, 1, 0),
        "vec": vec,
        "gu_w": np.stack([tile_gu(a["L0_ffn_gate_w"]), tile_gu(a["L0_ffn_up_w"])], axis=2),
        "gu_z": np.stack([row_gu(a["L0_ffn_gate_z"]), row_gu(a["L0_ffn_up_z"])], axis=1).reshape(IC, 1, 2 * KC * P),
        "gu_s": np.stack([a["L0_ffn_gate_s"].reshape(KC, IC, P), a["L0_ffn_up_s"].reshape(KC, IC, P)]
                         ).transpose(3, 2, 0, 1),
        "dn_w": a["L0_ffn_down_w"].reshape(IC, P, DM),
        "dn_z": a["L0_ffn_down_z"].reshape(IC, 1, DM),
        "dn_s": a["L0_ffn_down_s"].reshape(IC, 1, DM),
        "consts": constants(),
    }
    nc = _bacc.Bacc("TRN2", target_bir_lowering=False, num_devices=1)
    feed, args = {}, []
    for name, v in arrays.items():
        v = np.ascontiguousarray(v)
        feed[f"in_{name}"] = v
        args.append(nc.dram_tensor(f"in_{name}", v.shape, _mybir.dt.from_np(v.dtype), kind="ExternalInput").ap())
    o = nc.dram_tensor("result", (P, NQ, DM), _mybir.dt.float32, kind="ExternalOutput").ap()
    build(nc, *args, o)
    r = _run(nc, [feed], core_ids=[0])
    return np.asarray(r.results[0]["result"]).transpose(1, 0, 2).reshape(B, S, DM)
```
